# Optimizing a Trainium2 kernel written in Bass

```python
import numpy as np
import jax
import jax.numpy as jnp

def _softmax(x, axis=-1):
    return jax.nn.softmax(x, axis=axis)

def _gelu(x):
    return jax.nn.gelu(x, approximate=True)

def _silu(x):
    return jax.nn.silu(x)

def _sigmoid(x):
    return jax.nn.sigmoid(x)

def _layernorm(x, axis=-1, eps=1e-05):
    m = jnp.mean(x, axis=axis, keepdims=True)
    v = jnp.var(x, axis=axis, keepdims=True)
    return (x - m) / jnp.sqrt(v + eps)

def _scatter_add(tgt, idx, src, axis=0):
    return tgt.at[idx].add(src)

def _segment_sum(src, seg, n):
    return jax.ops.segment_sum(src, seg, n)
kernel_name = 'mk_gnn_ffn_d2_gnn_r8_6c7230'

def setup_inputs(seed: int=0):
    np.random.seed(seed)
    _w = jnp.asarray

    def _rec_inputs():
        import jax
        import jax.numpy as jnp
        _gk = jax.random.key(seed)
        x = -0.0001126 + 1 * jax.random.normal(jax.random.fold_in(_gk, 1), (3750, 256), jnp.float32)
        src = jax.random.randint(jax.random.fold_in(_gk, 2), (60000,), 0, 3750, jnp.int32)
        dst = jax.random.randint(jax.random.fold_in(_gk, 3), (60000,), 0, 3750, jnp.int32)
        _o = jnp.argsort(dst, stable=True)
        src = src[_o]
        dst = dst[_o]
        edge_attr_20 = jax.random.uniform(jax.random.fold_in(_gk, 12), (60000, 20), jnp.float32, 0.0, 1)
        edge_type_8 = jax.random.randint(jax.random.fold_in(_gk, 14), (60000,), 0, 8, jnp.int32)
        return (x, src, dst, edge_attr_20, edge_type_8)
    x, src, dst, edge_attr_20, edge_type_8 = _rec_inputs()

    def _L0_gnn_setup():
        import jax, jax.numpy as jnp
        import numpy as np
        N_NODES = 3750
        N_EDGES = 60000
        IN_FEAT = 256
        OUT_FEAT = 256
        N_RELS = 8
        N_HEADS = 4
        HEAD_DIM = OUT_FEAT // N_HEADS
        LEAKY_SLOPE = 0.2
        key = jax.random.key(seed)
        ks = jax.random.split(key, 8)
        inputs = jax.random.normal(ks[0], (N_NODES, IN_FEAT), dtype=jnp.float32)
        conv_weights = jax.random.normal(ks[1], (N_RELS, N_HEADS, IN_FEAT, HEAD_DIM), dtype=jnp.float32) * (1.0 / np.sqrt(IN_FEAT))
        attn_l = jax.random.normal(ks[2], (N_RELS, N_HEADS, HEAD_DIM), dtype=jnp.float32) * 0.1
        attn_r = jax.random.normal(ks[3], (N_RELS, N_HEADS, HEAD_DIM), dtype=jnp.float32) * 0.1
        h_bias = jax.random.normal(ks[4], (OUT_FEAT,), dtype=jnp.float32) * 0.02
        edge_src = jax.random.randint(ks[5], (N_EDGES,), 0, N_NODES, dtype=jnp.int32)
        edge_dst = jax.random.randint(ks[6], (N_EDGES,), 0, N_NODES, dtype=jnp.int32)
        edge_type = jax.random.randint(ks[7], (N_EDGES,), 0, N_RELS, dtype=jnp.int32)
        return {'inputs': inputs, 'conv_weights': conv_weights, 'attn_l': attn_l, 'attn_r': attn_r, 'h_bias': h_bias, 'edge_src': edge_src, 'edge_dst': edge_dst, 'edge_type': edge_type}
    _L0_gnn_all = _L0_gnn_setup()
    _L0_gnn_in = {k: v for k, v in _L0_gnn_all.items() if k in ('conv_weights', 'attn_l', 'attn_r', 'h_bias')}
    del _L0_gnn_all

    def _L0_ffn_setup():
        import jax, jax.numpy as jnp
        import numpy as np
        B, A = (512, 8)
        IN, OUT = (256, 256)
        SH1, SH2 = (256, 128)
        EH1, EH2 = (128, 64)
        E, TOPK = (4, 2)

        def _shared_mlp(x, W1, b1, W2, b2, W3, b3):
            h = jax.nn.relu(x @ W1 + b1)
            h = jax.nn.relu(h @ W2 + b2)
            return h @ W3 + b3

        def _experts_mlp(x, eW1, eb1, eW2, eb2, eW3, eb3):
            h = jax.nn.relu(jnp.einsum('baf,efh->ebah', x, eW1) + eb1[:, None, None, :])
            h = jax.nn.relu(jnp.einsum('ebah,ehg->ebag', h, eW2) + eb2[:, None, None, :])
            o = jnp.einsum('ebag,ego->ebao', h, eW3) + eb3[:, None, None, :]
            return jnp.moveaxis(o, 0, -1)
        key = jax.random.key(seed)
        ks = jax.random.split(key, 16)
        s = 0.05
        return {'x': jax.random.normal(ks[0], (B, A, IN), jnp.float32), 'sW1': jax.random.normal(ks[1], (IN, SH1), jnp.float32) * s, 'sb1': jnp.zeros((SH1,), jnp.float32), 'sW2': jax.random.normal(ks[2], (SH1, SH2), jnp.float32) * s, 'sb2': jnp.zeros((SH2,), jnp.float32), 'sW3': jax.random.normal(ks[3], (SH2, OUT), jnp.float32) * s, 'sb3': jnp.zeros((OUT,), jnp.float32), 'eW1': jax.random.normal(ks[4], (E, IN, EH1), jnp.float32) * s, 'eb1': jnp.zeros((E, EH1), jnp.float32), 'eW2': jax.random.normal(ks[5], (E, EH1, EH2), jnp.float32) * s, 'eb2': jnp.zeros((E, EH2), jnp.float32), 'eW3': jax.random.normal(ks[6], (E, EH2, OUT), jnp.float32) * s, 'eb3': jnp.zeros((E, OUT), jnp.float32), 'gW': jax.random.normal(ks[7], (IN, E), jnp.float32) * s, 'gb': jnp.zeros((E,), jnp.float32)}
    _L0_ffn_all = _L0_ffn_setup()
    _L0_ffn_in = {k: v for k, v in _L0_ffn_all.items() if k in ('sW1', 'sb1', 'sW2', 'sb2', 'sW3', 'sb3', 'eW1', 'eb1', 'eW2', 'eb2', 'eW3', 'eb3', 'gW', 'gb')}
    del _L0_ffn_all

    def _L1_gnn_setup():
        import jax, jax.numpy as jnp
        import numpy as np
        N, E, HDIM, NG = (1250, 40000, 256, 20)
        BN_EPS = 1e-05
        key = jax.random.key(seed)
        ks = jax.random.split(key, 12)
        inp = {'x': jax.random.normal(ks[0], (N, HDIM), dtype=jnp.float32), 'rbf': jax.random.uniform(ks[1], (E, NG), dtype=jnp.float32), 'ei': jax.random.randint(ks[2], (2, E), 0, N, dtype=jnp.int64), 'Wf1': jax.random.normal(ks[3], (NG, HDIM), dtype=jnp.float32) / np.sqrt(NG), 'bf1': jnp.zeros((HDIM,), dtype=jnp.float32), 'Wf2': jax.random.normal(ks[4], (HDIM, HDIM), dtype=jnp.float32) / np.sqrt(HDIM), 'bf2': jnp.zeros((HDIM,), dtype=jnp.float32), 'Wu1': jax.random.normal(ks[5], (HDIM, HDIM), dtype=jnp.float32) / np.sqrt(HDIM), 'bu1': jnp.zeros((HDIM,), dtype=jnp.float32), 'Wu2': jax.random.normal(ks[6], (HDIM, HDIM), dtype=jnp.float32) / np.sqrt(HDIM), 'bu2': jnp.zeros((HDIM,), dtype=jnp.float32), 'gamma': jnp.ones((HDIM,), dtype=jnp.float32), 'beta': jnp.zeros((HDIM,), dtype=jnp.float32)}
        return inp
    _L1_gnn_all = _L1_gnn_setup()
    _L1_gnn_in = {k: v for k, v in _L1_gnn_all.items() if k in ('Wf1', 'bf1', 'Wf2', 'bf2', 'Wu1', 'bu1', 'Wu2', 'bu2', 'gamma', 'beta')}
    del _L1_gnn_all

    def _L1_ffn_setup():
        import jax, jax.numpy as jnp
        import numpy as np
        D_MODEL = 256
        N_EXPERTS = 16
        HIDDEN = 512
        SCALE = 0.02
        key = jax.random.key(seed)
        ks = jax.random.split(key, 5)
        x = jax.random.normal(ks[0], (4, 1024, D_MODEL), dtype=jnp.float32)
        gate_w = jax.random.normal(ks[1], (D_MODEL, N_EXPERTS), dtype=jnp.float32) * SCALE
        gate_b = jnp.zeros((N_EXPERTS,), dtype=jnp.float32)
        w1 = jax.random.normal(ks[2], (N_EXPERTS, D_MODEL, HIDDEN), dtype=jnp.float32) * SCALE
        w2 = jax.random.normal(ks[3], (N_EXPERTS, D_MODEL, HIDDEN), dtype=jnp.float32) * SCALE
        w3 = jax.random.normal(ks[4], (N_EXPERTS, HIDDEN, D_MODEL), dtype=jnp.float32) * SCALE
        return {'x': x, 'gate_w': gate_w, 'gate_b': gate_b, 'w1': w1, 'w2': w2, 'w3': w3}
    _L1_ffn_all = _L1_ffn_setup()
    _L1_ffn_in = {k: v for k, v in _L1_ffn_all.items() if k in ('gate_w', 'gate_b', 'w1', 'w2', 'w3')}
    del _L1_ffn_all
    return {'x': x, 'src': src, 'dst': dst, 'edge_attr_20': edge_attr_20, 'edge_type_8': edge_type_8, 'L0_gnn_conv_weights': _L0_gnn_in['conv_weights'], 'L0_gnn_attn_l': _L0_gnn_in['attn_l'], 'L0_gnn_attn_r': _L0_gnn_in['attn_r'], 'L0_gnn_h_bias': _L0_gnn_in['h_bias'], 'L0_ffn_sW1': _L0_ffn_in['sW1'], 'L0_ffn_sb1': _L0_ffn_in['sb1'], 'L0_ffn_sW2': _L0_ffn_in['sW2'], 'L0_ffn_sb2': _L0_ffn_in['sb2'], 'L0_ffn_sW3': _L0_ffn_in['sW3'], 'L0_ffn_sb3': _L0_ffn_in['sb3'], 'L0_ffn_eW1': _L0_ffn_in['eW1'], 'L0_ffn_eb1': _L0_ffn_in['eb1'], 'L0_ffn_eW2': _L0_ffn_in['eW2'], 'L0_ffn_eb2': _L0_ffn_in['eb2'], 'L0_ffn_eW3': _L0_ffn_in['eW3'], 'L0_ffn_eb3': _L0_ffn_in['eb3'], 'L0_ffn_gW': _L0_ffn_in['gW'], 'L0_ffn_gb': _L0_ffn_in['gb'], 'L1_gnn_Wf1': _L1_gnn_in['Wf1'], 'L1_gnn_bf1': _L1_gnn_in['bf1'], 'L1_gnn_Wf2': _L1_gnn_in['Wf2'], 'L1_gnn_bf2': _L1_gnn_in['bf2'], 'L1_gnn_Wu1': _L1_gnn_in['Wu1'], 'L1_gnn_bu1': _L1_gnn_in['bu1'], 'L1_gnn_Wu2': _L1_gnn_in['Wu2'], 'L1_gnn_bu2': _L1_gnn_in['bu2'], 'L1_gnn_gamma': _L1_gnn_in['gamma'], 'L1_gnn_beta': _L1_gnn_in['beta'], 'L1_ffn_gate_w': _L1_ffn_in['gate_w'], 'L1_ffn_gate_b': _L1_ffn_in['gate_b'], 'L1_ffn_w1': _L1_ffn_in['w1'], 'L1_ffn_w2': _L1_ffn_in['w2'], 'L1_ffn_w3': _L1_ffn_in['w3']}

def reference(x, src, dst, edge_attr_20, edge_type_8, L0_gnn_conv_weights, L0_gnn_attn_l, L0_gnn_attn_r, L0_gnn_h_bias, L0_ffn_sW1, L0_ffn_sb1, L0_ffn_sW2, L0_ffn_sb2, L0_ffn_sW3, L0_ffn_sb3, L0_ffn_eW1, L0_ffn_eb1, L0_ffn_eW2, L0_ffn_eb2, L0_ffn_eW3, L0_ffn_eb3, L0_ffn_gW, L0_ffn_gb, L1_gnn_Wf1, L1_gnn_bf1, L1_gnn_Wf2, L1_gnn_bf2, L1_gnn_Wu1, L1_gnn_bu1, L1_gnn_Wu2, L1_gnn_bu2, L1_gnn_gamma, L1_gnn_beta, L1_ffn_gate_w, L1_ffn_gate_b, L1_ffn_w1, L1_ffn_w2, L1_ffn_w3):
    import jax
    import jax.numpy as jnp

    def _L0_gnn_ref(inputs, conv_weights, attn_l, attn_r, h_bias, edge_src, edge_dst, edge_type):
        import jax, jax.numpy as jnp
        import numpy as np
        N_NODES = 3750
        N_EDGES = 60000
        IN_FEAT = 256
        OUT_FEAT = 256
        N_RELS = 8
        N_HEADS = 4
        HEAD_DIM = OUT_FEAT // N_HEADS
        LEAKY_SLOPE = 0.2
        feat_all = jnp.einsum('ni,rhid->rnhd', inputs, conv_weights)
        feat_src_e = feat_all[edge_type, edge_src]
        feat_dst_e = feat_all[edge_type, edge_dst]
        el = jnp.sum(feat_src_e * attn_l[edge_type], axis=-1)
        er = jnp.sum(feat_dst_e * attn_r[edge_type], axis=-1)
        e = jax.nn.leaky_relu(el + er, negative_slope=LEAKY_SLOPE)
        m = jax.ops.segment_max(e, edge_dst, num_segments=N_NODES)
        ex = jnp.exp(e - m[edge_dst])
        denom = jax.ops.segment_sum(ex, edge_dst, num_segments=N_NODES)
        alpha = ex / denom[edge_dst]
        h = jax.ops.segment_sum(alpha[..., None] * feat_src_e, edge_dst, num_segments=N_NODES)
        h = h.reshape(N_NODES, OUT_FEAT) + h_bias
        return h

    def _L0_ffn_ref(x, sW1, sb1, sW2, sb2, sW3, sb3, eW1, eb1, eW2, eb2, eW3, eb3, gW, gb):
        import jax, jax.numpy as jnp
        import numpy as np
        B, A = (512, 8)
        IN, OUT = (256, 256)
        SH1, SH2 = (256, 128)
        EH1, EH2 = (128, 64)
        E, TOPK = (4, 2)

        def _shared_mlp(x, W1, b1, W2, b2, W3, b3):
            h = jax.nn.relu(x @ W1 + b1)
            h = jax.nn.relu(h @ W2 + b2)
            return h @ W3 + b3

        def _experts_mlp(x, eW1, eb1, eW2, eb2, eW3, eb3):
            h = jax.nn.relu(jnp.einsum('baf,efh->ebah', x, eW1) + eb1[:, None, None, :])
            h = jax.nn.relu(jnp.einsum('ebah,ehg->ebag', h, eW2) + eb2[:, None, None, :])
            o = jnp.einsum('ebag,ego->ebao', h, eW3) + eb3[:, None, None, :]
            return jnp.moveaxis(o, 0, -1)
        all_out = _experts_mlp(x, eW1, eb1, eW2, eb2, eW3, eb3)
        shared = _shared_mlp(x, sW1, sb1, sW2, sb2, sW3, sb3)
        gates = jax.nn.softmax(x @ gW + gb, axis=-1)
        topv, topi = jax.lax.top_k(gates, TOPK)
        topw = jax.nn.softmax(topv, axis=-1)
        sel = jnp.take_along_axis(all_out, topi[:, :, None, :], axis=-1)
        gated = jnp.sum(sel * topw[:, :, None, :], axis=-1)
        return shared + gated

    def _L1_gnn_ref(x, rbf, Wf1, bf1, Wf2, bf2, Wu1, bu1, Wu2, bu2, gamma, beta, ei):
        import jax, jax.numpy as jnp
        import numpy as np
        N, E, HDIM, NG = (1250, 40000, 256, 20)
        BN_EPS = 1e-05
        row, col = (ei[0], ei[1])
        filt = jax.nn.silu(rbf @ Wf1 + bf1) @ Wf2 + bf2
        msg = x[col] * filt
        agg = jax.ops.segment_sum(msg, row, num_segments=x.shape[0])
        h = jax.nn.silu(agg @ Wu1 + bu1) @ Wu2 + bu2
        mean = jnp.mean(h, axis=0)
        var = jnp.mean(jnp.square(h - mean), axis=0)
        bn = gamma * (h - mean) * jax.lax.rsqrt(var + BN_EPS) + beta
        return x + bn

    def _L1_ffn_ref(x, gate_w, gate_b, w1, w2, w3):
        import jax, jax.numpy as jnp
        import numpy as np
        D_MODEL = 256
        N_EXPERTS = 16
        HIDDEN = 512
        SCALE = 0.02
        n_experts = w1.shape[0]
        logits = jnp.einsum('bsd,de->bse', x, gate_w) + gate_b
        probs = jax.nn.softmax(logits, axis=-1)
        top_probs, top_idx = jax.lax.top_k(probs, 2)
        top_probs = top_probs / jnp.sum(top_probs, axis=-1, keepdims=True)
        dispatch = jnp.sum(jax.nn.one_hot(top_idx, n_experts, dtype=x.dtype) * top_probs[..., None], axis=-2)
        h1 = jnp.einsum('bsd,edh->bseh', x, w1)
        h2 = jnp.einsum('bsd,edh->bseh', x, w2)
        hidden = jax.nn.silu(h1) * h2
        expert_out = jnp.einsum('bseh,eho->bseo', hidden, w3)
        return jnp.einsum('bseo,bse->bso', expert_out, dispatch)
    edge_index = jnp.stack([src, dst])
    x = x + _L0_gnn_ref(_layernorm(x, axis=-1), L0_gnn_conv_weights, L0_gnn_attn_l, L0_gnn_attn_r, L0_gnn_h_bias, src, dst, edge_type_8)
    x = x + _L0_ffn_ref(_layernorm(x, axis=-1)[None], L0_ffn_sW1, L0_ffn_sb1, L0_ffn_sW2, L0_ffn_sb2, L0_ffn_sW3, L0_ffn_sb3, L0_ffn_eW1, L0_ffn_eb1, L0_ffn_eW2, L0_ffn_eb2, L0_ffn_eW3, L0_ffn_eb3, L0_ffn_gW, L0_ffn_gb)[0]
    x = x + _L1_gnn_ref(_layernorm(x, axis=-1), edge_attr_20, L1_gnn_Wf1, L1_gnn_bf1, L1_gnn_Wf2, L1_gnn_bf2, L1_gnn_Wu1, L1_gnn_bu1, L1_gnn_Wu2, L1_gnn_bu2, L1_gnn_gamma, L1_gnn_beta, edge_index)
    x = x + _L1_ffn_ref(_layernorm(x, axis=-1)[None], L1_ffn_gate_w, L1_ffn_gate_b, L1_ffn_w1, L1_ffn_w2, L1_ffn_w3)[0]
    return x

_drawn_inputs = setup_inputs


def setup_inputs(seed=0):
    import zlib

    import numpy as np

    out = dict(_drawn_inputs(seed))
    spreads = {'L0_ffn_sb1': (0.0, 0.37),
     'L0_ffn_sb2': (0.0, 0.1),
     'L0_ffn_sb3': (0.0, 0.1),
     'L0_ffn_eb1': (0.0, 0.8),
     'L0_ffn_eb2': (0.0, 0.411),
     'L0_ffn_eb3': (0.0, 0.1),
     'L0_ffn_gb': (0.0, 0.348),
     'L1_gnn_bf1': (0.0, 0.1),
     'L1_gnn_bf2': (0.0, 0.1),
     'L1_gnn_bu1': (0.0, 0.399),
     'L1_gnn_bu2': (0.0, 0.8),
     'L1_gnn_gamma': (1.0, 0.2),
     'L1_gnn_beta': (0.0, 0.1),
     'L1_ffn_gate_b': (0.0, 0.8)}
    factors = {'L1_ffn_gate_w': 8.0, 'L1_ffn_w1': 7.843, 'L1_ffn_w2': 7.735, 'L1_ffn_w3': 7.759}
    for name, (base, spread) in spreads.items():
        noise = np.random.default_rng([zlib.crc32(name.encode()), seed]).standard_normal(out[name].shape)
        drawn = base * np.exp(spread * noise) if base else spread * noise
        out[name] = jnp.asarray(drawn.astype(out[name].dtype))
    for name, factor in factors.items():
        out[name] = (out[name] * factor).astype(out[name].dtype)
    return out
```

```python
from contextlib import ExitStack

import concourse.bass as bass
from concourse import mybir

ALU = mybir.AluOpType
ACT = mybir.ActivationFunctionType
AX = mybir.AxisListType
F32 = mybir.dt.float32
BF16 = mybir.dt.bfloat16
I32 = mybir.dt.int32

P = 128
NODES, D = 3750, 256
NT = -(-NODES // P)
TAIL = NODES - (NT - 1) * P
PADN = NT * P
EDGES = 60000
EP, EJ = 125, 480
ET = 504
assert EP * EJ == EDGES and (EDGES + NT * (P - 1)) // P <= ET and ET % 8 == 0
RELS, HEADS, HD = 8, 4, 64
FW = D + HEADS
NG = 20
W0, W1 = 4, 24
EX0, EX1, HID = 4, 16, 512
MT = 76
assert (2 * NODES + EX1 * (P - 1)) // P <= MT
LN_EPS, BN_EPS, SLOPE = 1e-5, 1e-5, 0.2
BIG = float(2.0 ** 100)


class Stage:

    def __init__(self, nc, name):
        self.nc, self.name, self.ctx, self.sems, self.open = nc, name, ExitStack(), [], None

    def __enter__(self):
        self.ctx.__enter__()
        return self

    def __exit__(self, *error):
        if self.open is not None:
            self.open.__exit__(*error)
        if self.sems and error[0] is None:
            self.nc.clear_and_free_semaphores(self.sems)
            self.nc.all_engine_barrier()
        return self.ctx.__exit__(*error)

    def sb(self, name, shape, dt=F32):
        return self.ctx.enter_context(self.nc.sbuf_tensor(f"{self.name}_{name}", shape, dt))

    def ps(self, name, shape, dt=F32):
        return self.ctx.enter_context(self.nc.psum_tensor(f"{self.name}_{name}", shape, dt))

    def sem(self, name):
        self.sems.append(self.nc.alloc_semaphore(name=f"{self.name}_{name}"))
        return self.sems[-1]

    def block(self):
        self.open = self.nc.Block()
        return self.open.__enter__()


class Chain:

    def __init__(self, eng, sem):
        self.eng, self.sem, self.n = eng, sem, 0

    def __call__(self, ins):
        self.n += 1
        ins.then_inc(self.sem, 1)
        self.eng.wait_ge(self.sem, self.n)


def bcast(ap, dims):
    return bass.AP(ap.tensor, ap.offset, [list(ap.ap[0])] + [list(d) for d in dims])


def rows(vec, n=P):
    return bass.AP(vec.tensor, vec.offset, [[0, n]] + [list(d) for d in vec.ap])


class Steps:

    def __init__(self, eng, sem, start):
        self.eng, self.sem, self.start, self.n = eng, sem, start, 0

    def __call__(self, ins):
        self.n += 1
        ins.then_inc(self.sem, 1)
        return self.n

    def wait(self, n=None):
        self.eng.wait_ge(self.sem, self.start + (self.n if n is None else n))


def flat(ap, pattern="p a b -> p (a b)"):
    return ap.rearrange(pattern)


def constants(nc, c, x_in, x_res):
    with Stage(nc, "const") as s:
        loaded, made, dv = s.sem("loaded"), s.sem("made"), s.sem("dv")
        ramp_i = s.sb("ramp_i", [P, 512], I32)
        block = s.block()

        @block.sync
        def _(sp):
            sp.wait_ge(made, 1)
            sp.dma_start(x_res[:, 0:NT - 1, :], x_in[0:(NT - 1) * P, :].rearrange("(t p) d -> p t d", p=P)).then_inc(loaded, 16)
            sp.dma_start(x_res[0:TAIL, NT - 1, :], x_in[(NT - 1) * P:NODES, :]).then_inc(loaded, 16)
            sp.wait_ge(loaded, 32)

        @block.gpsimd
        def _(pool):
            nc.gpsimd.memset(x_res[:, NT - 1, :], 0.0).then_inc(made, 1)
            nc.gpsimd.iota(ramp_i[:, :], pattern=[[1, 512]], base=0, channel_multiplier=0).then_inc(made, 1)
            nc.gpsimd.memset(c["ident"][:, :], 0.0).then_inc(made, 1)
            nc.gpsimd.memset(c["before"][:, :], 1.0).then_inc(made, 1)
            nc.gpsimd.memset(c["upto"][:, :], 1.0).then_inc(made, 1)
            nc.gpsimd.memset(c["beyond"][:, :], 1.0).then_inc(made, 1)
            pool.wait_ge(made, 6)
            nc.gpsimd.affine_select(out=c["ident"][:, :], in_=c["ident"][:, :], compare_op=ALU.not_equal, fill=1.0,
                                    base=0, pattern=[[-1, P]], channel_multiplier=1).then_inc(made, 1)
            nc.gpsimd.affine_select(out=c["before"][:, :], in_=c["before"][:, :], compare_op=ALU.is_gt, fill=0.0,
                                    base=0, pattern=[[1, P]], channel_multiplier=-1).then_inc(made, 1)
            nc.gpsimd.affine_select(out=c["beyond"][:, :], in_=c["beyond"][:, :], compare_op=ALU.is_ge, fill=0.0,
                                    base=-TAIL, pattern=[[0, 1]], channel_multiplier=1).then_inc(made, 1)
            nc.gpsimd.affine_select(out=c["upto"][:, :], in_=c["upto"][:, :], compare_op=ALU.is_ge, fill=0.0,
                                    base=0, pattern=[[1, P]], channel_multiplier=-1).then_inc(made, 1)

        @block.vector
        def _(dve):
            nc.vector.memset(c["ones"][:, :], 1.0).then_inc(dv, 1)
            nc.vector.memset(c["ln_eps"][:, :], LN_EPS).then_inc(dv, 1)
            nc.vector.memset(c["bn_eps"][:, :], BN_EPS).then_inc(dv, 1)
            nc.vector.memset(c["minus_big"][:, :], -BIG).then_inc(dv, 1)
            dve.wait_ge(made, 10)
            nc.vector.tensor_copy(c["ramp"][:, :], ramp_i[:, :]).then_inc(dv, 1)
            nc.vector.tensor_copy(c["identb"][:, :], c["ident"][:, :]).then_inc(dv, 1)


def positions(nc, name, c, n_part, n_free, bins, tiles, bin_f, pos_f, addr_i, tile_bin, mask_view=None):
    n = n_free
    with Stage(nc, name) as s:
        mask = s.sb("mask", [P, bins, n], BF16)
        run = s.sb("run", [P, bins, n])
        cnt, pre, base = s.sb("cnt", [P, bins]), s.sb("pre", [P, bins]), s.sb("base", [P, bins])
        padded_i, padded, end = s.sb("padded_i", [bins, 1], I32), s.sb("padded", [bins, 1]), s.sb("end", [bins, 1])
        reached = s.sb("reached", [bins, 512])
        tb = s.sb("tb", [1, 512])
        pos_i, lane, col = s.sb("pos_i", [P, n], I32), s.sb("lane", [P, n], I32), s.sb("col", [P, n], I32)
        pp = s.ps("pp", [P, 4, 512])
        dv, pe_s = s.sem("dv"), s.sem("pe")
        counted, rounded, ended, compared = s.sem("counted"), s.sem("rounded"), s.sem("ended"), s.sem("compared")
        block = s.block()
        q = slice(0, n_part)
        lt = c["before"]

        @block.tensor
        def _(pe):
            pe.wait_ge(counted, 1)
            nc.tensor.matmul(pp[0:bins, 0, 0:1], cnt[q, :], c["ones"][q, 0:1], start=True, stop=True).then_inc(pe_s, 1)
            pe.wait_ge(rounded, 1)
            nc.tensor.matmul(pp[0:bins, 1, 0:1], c["upto"][0:bins, 0:bins], padded[:, :], start=True, stop=True).then_inc(pe_s, 1)
            nc.tensor.matmul(pp[:, 2, 0:bins], lt[q, :], cnt[q, :], start=True, stop=False)
            nc.tensor.matmul(pp[:, 2, 0:bins], padded[:, 0:1].broadcast_to([bins, P]), lt[0:bins, 0:bins],
                             start=False, stop=True).then_inc(pe_s, 1)
            pe.wait_ge(compared, 1)
            nc.tensor.matmul(pp[0:1, 3, :], c["ones"][0:bins, 0:1], reached[:, :], start=True, stop=True).then_inc(pe_s, 1)

        @block.vector
        def _(dve):
            do = Chain(dve, dv)
            v = nc.vector
            do(v.tensor_tensor(mask[q, :, :], bcast(bin_f, [[0, bins], list(bin_f.ap[1])]),
                               bcast(c["ramp"][q, :], [[1, bins], [0, n]]), ALU.is_equal))
            v.tensor_reduce(cnt[q, :], mask[q, :, :], AX.X, ALU.add).then_inc(counted, 1)
            m2, r2 = flat(mask[q, :, :]), flat(run[q, :, :])
            do(v.tensor_tensor_scan(r2, m2, m2, 0.0, ALU.add, ALU.max))
            dve.wait_ge(counted, 1)
            do(v.tensor_tensor_scan(pre[q, :], cnt[q, :], cnt[q, :], 0.0, ALU.add, ALU.max))
            do(v.tensor_tensor(pre[q, :], cnt[q, :], pre[q, :], ALU.subtract))
            dve.wait_ge(pe_s, 1)
            do(v.tensor_scalar(padded_i[:, :], pp[0:bins, 0, 0:1], float(P - 1), None, ALU.add))
            do(v.tensor_scalar(padded_i[:, :], padded_i[:, :], 7, 7, ALU.logical_shift_right, ALU.logical_shift_left))
            v.tensor_copy(padded[:, :], padded_i[:, :]).then_inc(rounded, 1)
            dve.wait_ge(pe_s, 2)
            do(v.tensor_scalar(end[:, :], pp[0:bins, 1, 0:1], 1.0 / P, None, ALU.mult))
            v.tensor_scalar(reached[:, :], c["ramp"][0:bins, :], end[:, 0:1], None, ALU.is_ge).then_inc(compared, 1)
            dve.wait_ge(pe_s, 3)
            do(v.scalar_tensor_tensor(out=base[q, :], in0=pre[q, :], scalar=-1.0, in1=pp[q, 2, 0:bins], op0=ALU.add, op1=ALU.add))
            do(v.tensor_tensor(run[q, :, :], run[q, :, :], base[q, :].unsqueeze(2).broadcast_to([n_part, bins, n]), ALU.add))
            do(v.tensor_tensor(run[q, :, :], run[q, :, :], mask[q, :, :], ALU.mult))
            do(v.tensor_reduce(pos_f, run[q, :, :].rearrange("p b n -> p n b"), AX.X, ALU.add))
            do(v.tensor_copy(pos_i[q, :], pos_f))
            do(v.tensor_scalar(lane[q, :], pos_i[q, :], P - 1, None, ALU.bitwise_and))
            do(v.tensor_scalar(col[q, :], pos_i[q, :], 7, None, ALU.logical_shift_right))
            do(v.scalar_tensor_tensor(out=addr_i, in0=lane[q, :], scalar=float(tiles), in1=col[q, :], op0=ALU.mult, op1=ALU.add))
            dve.wait_ge(pe_s, 4)
            do(v.tensor_scalar(tb[:, :], pp[0:1, 3, :], float(bins - 1), None, ALU.min))
            do(v.tensor_copy(tile_bin[:, :], tb[:, :]))


def layer_norm(nc, name, c, x_res, xn, xnT, table=None):
    with Stage(nc, name) as s:
        st = s.sb("st", [P, NT, 6])
        mean, var, t0, rstd, shift = (s.sb(k, [P, NT]) for k in ("mean", "var", "t0", "rstd", "shift"))
        row = [s.sb(f"row{u}", [P, D]) for u in range(2)]
        pst = [s.ps(f"turned{u}", [P, 2, P]) for u in range(2)]
        dv, seen, var_ready, std_ready = s.sem("dv"), s.sem("seen"), s.sem("var_ready"), s.sem("std_ready")
        row_ready, turned, copied = s.sem("row_ready"), s.sem("turned_done"), s.sem("copied")
        kept, stored = s.sem("kept"), s.sem("stored")
        block = s.block()

        @block.vector
        def _(dve):
            v = nc.vector
            with dve.Fori(0, NT) as t:
                v.bn_stats(flat(st[:, bass.ds(t, 1), :]), flat(x_res[:, bass.ds(t, 1), :])).then_inc(seen, 1)
            dve.wait_ge(seen, NT)
            do = Chain(dve, dv)
            do(v.tensor_tensor(mean[:, :], st[:, :, 1], st[:, :, 4], ALU.add))
            do(v.tensor_tensor(t0[:, :], st[:, :, 1], st[:, :, 4], ALU.subtract))
            do(v.tensor_scalar(mean[:, :], mean[:, :], 0.5, None, ALU.mult))
            do(v.scalar_tensor_tensor(out=t0[:, :], in0=t0[:, :], scalar=0.25, in1=t0[:, :], op0=ALU.mult, op1=ALU.mult))
            do(v.tensor_tensor(var[:, :], st[:, :, 2], st[:, :, 5], ALU.add))
            v.scalar_tensor_tensor(out=var[:, :], in0=var[:, :], scalar=1.0 / D, in1=t0[:, :], op0=ALU.mult,
                                   op1=ALU.add).then_inc(var_ready, 1)
            dve.wait_ge(std_ready, 1)
            do(v.reciprocal(rstd[:, :], t0[:, :]))
            do(v.scalar_tensor_tensor(out=shift[:, :], in0=mean[:, :], scalar=-1.0, in1=rstd[:, :], op0=ALU.mult, op1=ALU.mult))

            def normalise(t, u):
                v.tensor_scalar(row[u][:, :], flat(x_res[:, bass.ds(t, 1), :]), rstd[:, bass.ds(t, 1)],
                                shift[:, bass.ds(t, 1)], ALU.mult, ALU.add).then_inc(row_ready, 1)

            for u in range(2):
                normalise(u, u)
            with dve.Fori(1, NT // 2) as i:
                for u in range(2):
                    dve.wait_ge(turned, i * 2 + u - 1)
                    dve.wait_ge(kept, i * 2 + u - 1)
                    normalise(i * 2 + u, u)

        @block.gpsimd
        def _(pool):
            with pool.Fori(0, NT // 2) as i:
                for u in range(2):
                    pool.wait_ge(row_ready, i * 2 + u + 1)
                    nc.gpsimd.tensor_copy(flat(xn[:, bass.ds(i * 2 + u, 1), :]), row[u][:, :]).then_inc(kept, 1)

        @block.scalar
        def _(act):
            act.wait_ge(var_ready, 1)
            nc.scalar.activation(t0[:, :], var[:, :], ACT.Sqrt, bias=c["ln_eps"][:, 0:1]).then_inc(std_ready, 1)
            with act.Fori(0, NT // 2) as i:
                for u in range(2):
                    act.wait_ge(turned, i * 2 + u + 1)
                    nc.scalar.activation(xnT[:, :, bass.ds((i * 2 + u) * P, P)], pst[u][:, :, :], ACT.Copy).then_inc(copied, 1)

        @block.tensor
        def _(pe):
            def turn(u):
                for h in range(2):
                    ins = nc.tensor.transpose(pst[u][:, h, :], row[u][:, h * P:(h + 1) * P], c["ident"][:, :])
                ins.then_inc(turned, 1)

            for u in range(2):
                pe.wait_ge(row_ready, u + 1)
                turn(u)
            with pe.Fori(1, NT // 2) as i:
                for u in range(2):
                    pe.wait_ge(row_ready, i * 2 + u + 1)
                    pe.wait_ge(copied, i * 2 + u - 1)
                    turn(u)

        if table is not None:
            @block.sync
            def _(sp):
                sp.wait_ge(kept, NT)
                sp.dma_start(table.rearrange("(t p) d -> p t d", p=P), xn[:, :, :]).then_inc(stored, 16)
                sp.wait_ge(stored, 16)


def edge_records(nc, c, a, rec0, rec1, pos_f, addr0, addr1, bins0, bins1, table0, table1):
    q = slice(0, EP)
    with Stage(nc, "keys") as k:
        binf0, binf1 = k.sb("binf0", [P, EJ]), k.sb("binf1", [P, EJ])
        with Stage(nc, "split") as s:
            src, dst, typ = (s.sb(n, [P, EJ], I32) for n in ("src", "dst", "typ"))
            part = s.sb("part", [P, EJ], I32)
            srcf, typf = s.sb("srcf", [P, EJ]), s.sb("typf", [P, EJ])
            attr = s.sb("attr", [P, EJ, NG])
            empty0, empty1 = s.sb("empty0", [P, ET, W0]), s.sb("empty1", [P, ET // 8, W1])
            attr_loaded, attr_kept = s.sem("attr_loaded"), s.sem("attr_kept")
            loaded, dv, cleared, filled = s.sem("loaded"), s.sem("dv"), s.sem("cleared"), s.sem("filled")
            block = s.block()

            @block.sync
            def _(sp):
                for t, name in ((src, "src"), (dst, "dst"), (typ, "edge_type_8")):
                    sp.dma_start(t[q, :], a[name].rearrange("(p j) -> p j", p=EP)).then_inc(loaded, 16)
                sp.dma_start(attr[q, :, :], a["edge_attr_20"].rearrange("(p j) g -> p j g", p=EP)).then_inc(attr_loaded, 16)
                sp.wait_ge(cleared, 6)
                sp.dma_start(table0.rearrange("(p t) w -> p t w", p=P), empty0[:, :, :]).then_inc(filled, 16)
                for i in range(8):
                    sp.dma_start(table1.rearrange("(p i t) w -> p i t w", p=P, i=8)[:, i], empty1[:, :, :]).then_inc(filled, 16)
                sp.wait_ge(filled, 9 * 16)

            @block.gpsimd
            def _(pool):
                nc.gpsimd.memset(empty0[:, :, :], 0.0).then_inc(cleared, 1)
                nc.gpsimd.memset(empty1[:, :, :], 0.0).then_inc(cleared, 1)
                pool.wait_ge(cleared, 2)
                nc.gpsimd.memset(empty0[:, :, 0:1], float(NODES)).then_inc(cleared, 1)
                nc.gpsimd.memset(empty0[:, :, 1:2], -1.0).then_inc(cleared, 1)
                nc.gpsimd.memset(empty1[:, :, NG + 1:NG + 2], -1.0).then_inc(cleared, 1)
                nc.gpsimd.memset(rec1[q, :, NG + 2:W1], 0.0).then_inc(cleared, 1)

            @block.scalar
            def _(act):
                act.wait_ge(attr_loaded, 16)
                nc.scalar.activation(rec1[q, :, 0:NG], attr[q, :, :], ACT.Copy).then_inc(attr_kept, 1)

            @block.vector
            def _(dve):
                v, do = nc.vector, Chain(dve, dv)
                dve.wait_ge(loaded, 48)
                v.tensor_copy(srcf[q, :], src[q, :])
                v.tensor_copy(rec1[q, :, NG], dst[q, :])
                v.tensor_copy(rec0[q, :, 2], typ[q, :])
                do(v.tensor_copy(typf[q, :], typ[q, :]))
                v.memset(rec0[q, :, 3], 0.0)
                do(v.scalar_tensor_tensor(out=rec0[q, :, 0], in0=typf[q, :], scalar=float(PADN), in1=srcf[q, :],
                                          op0=ALU.mult, op1=ALU.add))
                for key, local, binf in ((dst, rec0[q, :, 1], binf0), (src, rec1[q, :, NG + 1], binf1)):
                    do(v.tensor_scalar(part[q, :], key[q, :], P - 1, None, ALU.bitwise_and))
                    do(v.tensor_copy(local, part[q, :]))
                    do(v.tensor_scalar(part[q, :], key[q, :], 7, None, ALU.logical_shift_right))
                    do(v.tensor_copy(binf[q, :], part[q, :]))

        positions(nc, "by_dst", c, EP, EJ, NT, ET, binf0[q, :], pos_f[q, :], addr0[q, :], bins0)
        positions(nc, "by_src", c, EP, EJ, NT, ET, binf1[q, :], pos_f[q, :], addr1[q, :], bins1)


def project(nc, c, a, xnT, er, feat, rec0, addr0, table0, rec1):
    with Stage(nc, "proj") as s:
        w = s.sb("w", [P, 2, RELS, FW])
        wr = s.sb("wr", [P, 2, RELS * HEADS])
        al, ar = s.sb("al", [P, RELS, D]), s.sb("ar", [P, RELS, D])
        prod = s.sb("prod", [P, RELS * D])
        out = [s.sb(f"out{u}", [P, RELS, FW]) for u in range(2)]
        xs = [s.sb(f"xs{u}", [P, 2, P]) for u in range(2)]
        send = [s.sb(f"send{u}", [P, W0]) for u in range(4)]
        slot = [s.sb(f"slot{u}", [P, 1], I32) for u in range(4)]
        ps = [s.ps(f"ps{r}", [P, 512]) for r in range(7)]
        pe_er = s.ps("er", [P, 512])
        wl, al_l = s.sem("w_loaded"), s.sem("a_loaded")
        dv, xs_ready = s.sem("dv"), s.sem("xs_ready")
        mm, er_done, ev_a, ev_v = s.sem("multiplied"), s.sem("er_done"), s.sem("moved_act"), s.sem("moved_dve")
        stored = [s.sem(f"stored{u}") for u in range(2)]
        sent = [s.sem(f"sent{u}") for u in range(4)]
        staged = s.sem("staged")
        block = s.block()
        ON_ACT = 5
        MOVES_V = RELS - ON_ACT + 1

        @block.sync
        def _(sp):
            cw = a["L0_gnn_conv_weights"].rearrange("r h (c p) d -> c p r h d", p=P)
            for k in range(2):
                for r in range(RELS):
                    sp.dma_start(w[:, k, r, 0:D].rearrange("p (h d) -> p h d", h=HEADS), cw[k, :, r]).then_inc(wl, 16)
            for t, name in ((al, "L0_gnn_attn_l"), (ar, "L0_gnn_attn_r")):
                sp.dma_start(flat(t[:, :, :]), rows(a[name].rearrange("r h d -> (r h d)"))).then_inc(al_l, 16)
            fv = feat.rearrange("(r t p) f -> t p r f", r=RELS, p=P)
            with sp.Fori(0, NT // 2) as i:
                for u in range(2):
                    sp.wait_ge(ev_a, (i * 2 + u + 1) * ON_ACT)
                    sp.nop(nofuse=True)
                    sp.wait_ge(ev_v, (i * 2 + u + 1) * MOVES_V)
                    sp.nop(nofuse=True)
                    sp.dma_start(fv[bass.ds(i * 2 + u, 1)].rearrange("a p r f -> (a p) r f"), out[u][:, :, :]).then_inc(stored[u], 16)
            for u in range(2):
                sp.wait_ge(stored[u], 16 * (NT // 2))

        @block.vector
        def _(dve):
            v, do = nc.vector, Chain(dve, dv)
            dve.wait_ge(wl, 16 * 2 * RELS)
            dve.wait_ge(al_l, 32)
            for k in range(2):
                for vec, dest in ((al, w[:, k, :, D:FW]), (ar, wr[:, k, :].rearrange("p (r h) -> p r h", r=RELS))):
                    do(v.tensor_tensor(prod[:, :].rearrange("p (r f) -> p r f", r=RELS), w[:, k, :, 0:D], vec[:, :, :], ALU.mult))
                    do(v.tensor_reduce(dest, prod[:, :].rearrange("p (r h d) -> p r h d", r=RELS, h=HEADS), AX.X, ALU.add))
            with dve.Fori(0, NT // 2) as i:
                for u in range(2):
                    t = i * 2 + u
                    dve.wait_ge(stored[u], i * 16)
                    for r in range(ON_ACT, RELS):
                        dve.wait_ge(mm, t * RELS + r + 1)
                        v.tensor_copy(out[u][:, r, :], ps[r % 7][:, 0:FW]).then_inc(ev_v, 1)
                    dve.wait_ge(er_done, t + 1)
                    v.tensor_copy(flat(er[:, bass.ds(t, 1), :]), pe_er[:, 0:RELS * HEADS]).then_inc(ev_v, 1)

        @block.scalar
        def _(act):
            def take(t, u):
                nc.scalar.activation(xs[u][:, :, :], xnT[:, :, bass.ds(t * P, P)], ACT.Copy).then_inc(xs_ready, 1)

            def tile(t, u, i, last=False):
                if not last:
                    act.wait_ge(er_done, t)
                    take(t + 1, 1 - u)
                act.wait_ge(stored[u], i * 16)
                for r in range(ON_ACT):
                    act.wait_ge(mm, t * RELS + r + 1)
                    nc.scalar.activation(out[u][:, r, :], ps[r][:, 0:FW], ACT.Copy).then_inc(ev_a, 1)

            take(0, 0)
            with act.Fori(0, NT // 2 - 1) as i:
                tile(i * 2, 0, i)
                tile(i * 2 + 1, 1, i)
            tile(NT - 2, 0, NT // 2 - 1)
            tile(NT - 1, 1, NT // 2 - 1, last=True)

        @block.tensor
        def _(pe):
            def tile(t, u, first=False):
                pe.wait_ge(xs_ready, t + 1)
                for r in range(RELS):
                    if r == RELS - 1:
                        pe.wait_ge(ev_a, t * ON_ACT + 1)
                    elif not first and r == 0:
                        pe.wait_ge(ev_v, (t - 1) * MOVES_V + RELS - ON_ACT)
                    elif not first and r < ON_ACT:
                        pe.wait_ge(ev_a, (t - 1) * ON_ACT + r + 1)
                    elif not first:
                        pe.wait_ge(ev_v, (t - 1) * MOVES_V + r - ON_ACT + 1)
                    for k in range(2):
                        ins = nc.tensor.matmul(ps[r % 7][:, 0:FW], xs[u][:, k, :], w[:, k, r, :], start=(k == 0), stop=(k == 1))
                    ins.then_inc(mm, 1)
                if not first:
                    pe.wait_ge(ev_v, t * MOVES_V)
                for k in range(2):
                    ins = nc.tensor.matmul(pe_er[:, 0:RELS * HEADS], xs[u][:, k, :], wr[:, k, :], start=(k == 0), stop=(k == 1))
                ins.then_inc(er_done, 1)

            pe.wait_ge(dv, 8)
            tile(0, 0, first=True)
            tile(1, 1)
            with pe.Fori(1, NT // 2) as i:
                tile(i * 2, 0)
                tile(i * 2 + 1, 1)

        @block.gpsimd
        def _(pool):
            with pool.Fori(0, EJ // 4) as i:
                for u in range(4):
                    j = i * 4 + u
                    pool.wait_ge(sent[u], i * 16)
                    nc.gpsimd.tensor_copy(slot[u][0:EP, :], addr0[0:EP, bass.ds(j, 1)]).then_inc(staged, 1)
                    nc.gpsimd.tensor_copy(send[u][0:EP, :], flat(rec0[0:EP, bass.ds(j, 1), :])).then_inc(staged, 1)
                    pool.wait_ge(staged, j * 2 + 2)
                    pool.nop(nofuse=True)
                    nc.gpsimd.indirect_dma_start(
                        out=table0, out_offset=bass.IndirectOffsetOnAxis(ap=slot[u][0:EP, 0:1], axis=0),
                        in_=send[u][0:EP, :], in_offset=None).then_inc(sent[u], 16)
            for u in range(4):
                pool.wait_ge(sent[u], 16 * (EJ // 4))


def attend(nc, c, er, acc, rec1, addr1, table0, table1, feat, bins0):
    K = 4
    GROUPS = ET // K
    H1 = HD + 1
    F_OPS = K + 1
    A_OPS, B_OPS, C_OPS = K + 5, 4 * K - 1, HEADS * K - 1
    with Stage(nc, "att") as s:
        recs = s.sb("recs", [P, ET, W0])
        rowidx = s.sb("rowidx", [P, ET], I32)
        two = range(2)
        idx = [s.sb(f"idx{u}", [P, K], I32) for u in two]
        got = [s.sb(f"got{u}", [P, K, FW]) for u in two]
        oh = [s.sb(f"onehot{u}", [P, K, P]) for u in two]
        ohT = [s.sb(f"onehotT{u}", [P, K, P]) for u in two]
        away = [s.sb(f"away{u}", [P, K, P], BF16) for u in two]
        typ = s.sb("typ", [P, K, RELS])
        ert = s.sb("ert", [P, K, HEADS, RELS])
        ers, z = s.sb("ers", [P, K, HEADS]), s.sb("z", [P, K, HEADS])
        e = [s.sb(f"e{u}", [P, K, HEADS]) for u in two]
        ehi = [s.sb(f"ehi{u}", [P, K, HEADS], BF16) for u in two]
        elo = [s.sb(f"elo{u}", [P, K, HEADS], BF16) for u in two]
        tmax = s.sb("tmax", [P, K, HEADS])
        mrun = s.sb("mrun", [P, NT, HEADS])
        mnew, drop = s.sb("mnew", [P, K, HEADS]), s.sb("drop", [P, K, HEADS])
        keep = [s.sb(f"keep{u}", [P, K, HEADS]) for u in two]
        below, ex = s.sb("below", [P, K, HEADS]), s.sb("ex", [P, K, HEADS])
        f = [s.sb(f"f{u}", [P, K, HEADS, H1]) for u in two]
        send = [s.sb(f"send{u}", [P, W1]) for u in range(K)]
        slot = [s.sb(f"slot{u}", [P, 1], I32) for u in range(K)]
        pmax = [s.ps(f"pmax{k}", [P, HEADS, P]) for k in range(K)]
        pT = s.ps("pT", [P, K, P])
        psum = [s.ps(f"psum{k}", [P, 512]) for k in range(3)]

        def sums(k, h2):
            n = 2 * k + h2
            return psum[n // 3][:, n % 3 * 2 * H1:(n % 3 + 1) * 2 * H1]

        per = [pmax[0][:, 0, k * 32:(k + 1) * 32] for k in range(K)]
        pme = [pmax[1][:, 0, k * HEADS:(k + 1) * HEADS] for k in range(K)]

        loaded, prep = s.sem("loaded"), s.sem("prep")
        dv = s.sem("dv")
        idx_ready = s.sem("idx_ready")
        got_s = [s.sem(f"got_s{u}") for u in two]
        oh_ready, turned, ohT_ready, er_ready = s.sem("oh_ready"), s.sem("turned"), s.sem("ohT_ready"), s.sem("er_ready")
        e_ready, away_ready, max_ready, drop_ready = s.sem("e_ready"), s.sem("away_ready"), s.sem("max_ready"), s.sem("drop_ready")
        me_ready, keep_ready, below_ready, ex_ready = s.sem("me_ready"), s.sem("keep_ready"), s.sem("below_ready"), s.sem("ex_ready")
        f_ready, sum_ready, acc_done = s.sem("f_ready"), s.sem("sum_ready"), s.sem("acc_done")
        staged = s.sem("staged")
        sent = [s.sem(f"sent{u}") for u in range(K)]
        block = s.block()

        @block.sync
        def _(sp):
            sp.dma_start(recs[:, :, :], table0.rearrange("(p t) w -> p t w", p=P)).then_inc(loaded, 16)
            sp.wait_ge(loaded, 16)

        @block.gpsimd
        def _(pool):
            def gathers(g, u):
                pool.wait_ge(f_ready, (g - 1) * F_OPS)
                nc.gpsimd.tensor_copy(idx[u][:, :], rowidx[:, bass.ds(g * K, K)]).then_inc(idx_ready, 1)
                pool.wait_ge(idx_ready, g + 1)
                pool.nop(nofuse=True)
                for k in range(K):
                    nc.gpsimd.indirect_dma_start(
                        out=got[u][:, k, :], out_offset=None, in_=feat,
                        in_offset=bass.IndirectOffsetOnAxis(ap=idx[u][:, k:k + 1], axis=0)).then_inc(got_s[u], 16)

            def scatters(g):
                for k in range(K):
                    pool.wait_ge(staged, (g * K + k + 1) * 2)
                    pool.nop(nofuse=True)
                    nc.gpsimd.indirect_dma_start(
                        out=table1, out_offset=bass.IndirectOffsetOnAxis(ap=slot[k][0:EP, 0:1], axis=0),
                        in_=send[k][0:EP, :], in_offset=None).then_inc(sent[k], 16)

            pool.wait_ge(prep, 3)
            for g in range(2):
                nc.gpsimd.tensor_copy(idx[g][:, :], rowidx[:, g * K:(g + 1) * K]).then_inc(idx_ready, 1)
                pool.wait_ge(idx_ready, g + 1)
                for k in range(K):
                    nc.gpsimd.indirect_dma_start(
                        out=got[g][:, k, :], out_offset=None, in_=feat,
                        in_offset=bass.IndirectOffsetOnAxis(ap=idx[g][:, k:k + 1], axis=0)).then_inc(got_s[g], 16)
            with pool.Fori(0, EJ // K // 2) as i:
                for u in two:
                    gathers(i * 2 + 2 + u, u)
                    scatters(i * 2 + u)
            with pool.Fori(EJ // K // 2 + 1, GROUPS // 2) as i:
                for u in two:
                    gathers(i * 2 + u, u)
            for k in range(K):
                pool.wait_ge(sent[k], 16 * (EJ // K))

        def in_steps(eng, step):
            step(0, 0, True, False, False)
            step(0, 1, True, True, False)
            with eng.Fori(1, GROUPS // 2) as i:
                step(i, 0, True, True, True)
                step(i, 1, True, True, True)
            step(GROUPS // 2, 0, False, True, True)
            step(GROUPS // 2, 1, False, False, True)

        @block.vector
        def _(dve):
            v = nc.vector
            v.memset(acc[:, :, :, :], 0.0).then_inc(prep, 1)
            v.memset(mrun[:, :, :], -BIG).then_inc(prep, 1)
            dve.wait_ge(loaded, 16)
            v.tensor_copy(rowidx[:, :], recs[:, :, 0]).then_inc(prep, 1)
            dve.wait_ge(prep, 3)

            def step(i, u, a, b, cc):
                g, w_ = i * 2 + u, 1 - u
                start = (g - 2) * (A_OPS + B_OPS + C_OPS) + 2 * A_OPS + B_OPS if cc else g * A_OPS
                if not (a or b):
                    start = start - A_OPS
                count = Steps(dve, dv, start)
                if b:
                    bins = [dve.value_load(bins0[0:1, bass.ds((g - 1) * K + k, 1)], min_val=0, max_val=NT - 1) for k in range(K)]
                    if cc:
                        dve.wait_ge(drop_ready, g - 1)
                        dve.wait_ge(keep_ready, g - 1)
                    for k in range(K):
                        dve.wait_ge(max_ready, (g - 1) * K + k + 1)
                        count(v.tensor_reduce(tmax[:, k, :], pmax[k][:, :, :], AX.X, ALU.max))
                    for k in range(K):
                        m = flat(mrun[:, bass.ds(bins[k], 1), :])
                        count.wait()
                        count(v.tensor_tensor(mnew[:, k, :], m, tmax[:, k, :], ALU.max))
                        count.wait()
                        count(v.tensor_tensor(drop[:, k, :], m, mnew[:, k, :], ALU.subtract))
                        count.wait()
                        ins = v.tensor_scalar(m, mnew[:, k, :], 0.0, None, ALU.add)
                        if k < K - 1:
                            count(ins)
                    ins.then_inc(drop_ready, 1)
                if a:
                    if cc:
                        dve.wait_ge(sum_ready, (g - 1) * K)
                        dve.wait_ge(away_ready, g - 1)
                    dest = recs[:, bass.ds(g * K, K), 1]
                    kind = recs[:, bass.ds(g * K, K), 2]
                    v.tensor_tensor(oh[u][:, :, :], bcast(c["ramp"][:, 0:P], [[0, K], [1, P]]),
                                    dest.unsqueeze(2).broadcast_to([P, K, P]), ALU.is_equal).then_inc(oh_ready, 1)
                    count(v.tensor_tensor(typ[:, :, :], bcast(c["ramp"][:, 0:RELS], [[0, K], [1, RELS]]),
                                    kind.unsqueeze(2).broadcast_to([P, K, RELS]), ALU.is_equal))
                if b:
                    dve.wait_ge(me_ready, g)
                    for k in range(K):
                        v.tensor_tensor(below[:, k, :], e[w_][:, k, :], pme[k], ALU.subtract).then_inc(below_ready, 1)
                if cc:
                    bins = [dve.value_load(bins0[0:1, bass.ds((g - 2) * K + k, 1)], min_val=0, max_val=NT - 1) for k in range(K)]
                    dve.wait_ge(keep_ready, g - 1)
                    dve.wait_ge(sum_ready, (g - 1) * K)
                    dve.wait_ge(acc_done, g - 2)
                    for k in range(K):
                        for h in range(HEADS):
                            at = flat(acc[:, bass.ds(bins[k], 1), h, :])
                            ins = v.scalar_tensor_tensor(out=at, in0=at, scalar=keep[u][:, k, h:h + 1],
                                                         in1=sums(k, h // 2)[:, h % 2 * H1:(h % 2 + 1) * H1],
                                                         op0=ALU.mult, op1=ALU.add)
                            if k < K - 1 or h < HEADS - 1:
                                count(ins)
                        if k < K - 1:
                            count.wait()
                    ins.then_inc(acc_done, 1)
                if a:
                    dve.wait_ge(er_ready, g + 1)
                    count.wait()
                    for k in range(K):
                        ins = v.tensor_tensor(ert[:, k, :, :], per[k].rearrange("p (r h) -> p h r", r=RELS),
                                              typ[:, k:k + 1, :].broadcast_to([P, HEADS, RELS]), ALU.mult)
                        count(ins)
                    count.wait()
                    count(v.tensor_reduce(ers[:, :, :], ert[:, :, :, :], AX.X, ALU.add))
                    dve.wait_ge(got_s[u], (i + 1) * 16 * K)
                    count.wait()
                    count(v.tensor_tensor(z[:, :, :], ers[:, :, :], got[u][:, :, D:FW], ALU.add))
                    count.wait()
                    count(v.scalar_tensor_tensor(out=e[u][:, :, :], in0=z[:, :, :], scalar=SLOPE, in1=z[:, :, :], op0=ALU.mult, op1=ALU.max))
                    count.wait()
                    count(v.tensor_copy(ehi[u][:, :, :], e[u][:, :, :]))
                    count.wait()
                    v.tensor_tensor(elo[u][:, :, :], e[u][:, :, :], ehi[u][:, :, :], ALU.subtract).then_inc(e_ready, 1)
                if b:
                    dve.wait_ge(ex_ready, g)
                    for k in range(K):
                        v.tensor_tensor(f[w_][:, k, :, 0:HD], got[w_][:, k, 0:D].rearrange("p (h d) -> p h d", h=HEADS),
                                        ex[:, k, :].unsqueeze(2).broadcast_to([P, HEADS, HD]), ALU.mult).then_inc(f_ready, 1)
                    v.tensor_copy(f[w_][:, :, :, HD], ex[:, :, :]).then_inc(f_ready, 1)
                assert count.n == A_OPS * a + B_OPS * b + C_OPS * cc

            in_steps(dve, step)

        @block.scalar
        def _(act):
            def stage(g):
                for k in range(K):
                    act.wait_ge(sent[k], 16 * g)
                    nc.scalar.activation(slot[k][0:EP, :], addr1[0:EP, bass.ds(g * K + k, 1)], ACT.Copy).then_inc(staged, 1)
                    nc.scalar.activation(send[k][0:EP, :], flat(rec1[0:EP, bass.ds(g * K + k, 1), :]), ACT.Copy).then_inc(staged, 1)

            def step(i, u, a, b, cc, st=True):
                g, w_ = i * 2 + u, 1 - u
                if b:
                    act.wait_ge(drop_ready, g)
                    if cc:
                        act.wait_ge(acc_done, g - 2)
                    nc.scalar.activation(keep[w_][:, :, :], drop[:, :, :], ACT.Exp).then_inc(keep_ready, 1)
                if a:
                    act.wait_ge(turned, g + 1)
                    nc.scalar.activation(ohT[u][:, :, :], pT[:, :, :], ACT.Copy).then_inc(ohT_ready, 1)
                if b:
                    act.wait_ge(below_ready, g * K)
                    act.wait_ge(f_ready, (g - 1) * F_OPS)
                    nc.scalar.activation(ex[:, :, :], below[:, :, :], ACT.Exp).then_inc(ex_ready, 1)
                if a:
                    if cc:
                        act.wait_ge(max_ready, (g - 1) * K)
                    nc.scalar.activation(away[u][:, :, :], oh[u][:, :, :], ACT.Identity, bias=c["minus_big"][:, 0:1], scale=BIG).then_inc(away_ready, 1)
                    if st:
                        stage(g)

            step(0, 0, True, False, False)
            step(0, 1, True, True, False)
            with act.Fori(1, EJ // K // 2) as i:
                step(i, 0, True, True, True)
                step(i, 1, True, True, True)
            with act.Fori(EJ // K // 2, GROUPS // 2) as i:
                step(i, 0, True, True, True, st=False)
                step(i, 1, True, True, True, st=False)
            step(GROUPS // 2, 0, False, True, True)

        @block.tensor
        def _(pe):
            def step(i, u, a, b, cc):
                g, w_ = i * 2 + u, 1 - u
                if b:
                    pe.wait_ge(drop_ready, g)
                    for k in range(K):
                        ins = nc.tensor.matmul(pme[k], ohT[w_][:, k, :], mnew[:, k, :], start=True, stop=True)
                    ins.then_inc(me_ready, 1)
                if a:
                    pe.wait_ge(oh_ready, g + 1)
                    for k in range(K):
                        ins = nc.tensor.transpose(pT[:, k, :], oh[u][:, k, :], c["ident"][:, :])
                    ins.then_inc(turned, 1)
                    bins = [pe.value_load(bins0[0:1, bass.ds(g * K + k, 1)], min_val=0, max_val=NT - 1) for k in range(K)]
                    pe.wait_ge(ohT_ready, g + 1)
                    for k in range(K):
                        ins = nc.tensor.matmul(per[k], ohT[u][:, k, :], flat(er[:, bass.ds(bins[k], 1), :]), start=True, stop=True)
                    ins.then_inc(er_ready, 1)
                    pe.wait_ge(e_ready, g + 1)
                    pe.wait_ge(away_ready, g + 1)
                    for k in range(K):
                        nc.tensor.matmul(pmax[k][:, :, :], away[u][:, k, :], bcast(c["identb"][:, :], [[0, HEADS], [1, P]]),
                                         start=True, stop=False, skip_group_check=True)
                        for h in range(HEADS):
                            for part in (ehi, elo):
                                ins = nc.tensor.matmul(pmax[k][:, h, :], part[u][:, k, h:h + 1].broadcast_to([P, P]), c["identb"][:, :],
                                                       start=False, stop=(part is elo), skip_group_check=True)
                        ins.then_inc(max_ready, 1)
                if b:
                    pe.wait_ge(f_ready, g * F_OPS)
                    for k in range(K):
                        for h2 in range(2):
                            ins = nc.tensor.matmul(sums(k, h2), oh[w_][:, k, :], flat(f[w_][:, k, 2 * h2:2 * h2 + 2, :]),
                                                   start=True, stop=True)
                        ins.then_inc(sum_ready, 1)

            in_steps(pe, step)


def make_consts(s):
    return {
        "ident": s.sb("ident", [P, P]), "identb": s.sb("identb", [P, P], BF16), "ramp": s.sb("ramp", [P, 512]),
        "before": s.sb("before", [P, P]), "upto": s.sb("upto", [P, P]), "ones": s.sb("ones", [P, P]),
        "beyond": s.sb("beyond", [P, 1]), "ln_eps": s.sb("ln_eps", [P, 1]), "bn_eps": s.sb("bn_eps", [P, 1]), "minus_big": s.sb("minus_big", [P, 1]),
    }


def join_attention(nc, c, a, acc, x_res):
    with Stage(nc, "join") as s:
        rden, bias = s.sb("rden", [P, NT, HEADS]), s.sb("bias", [P, D])
        loaded, dv = s.sem("loaded"), s.sem("dv")
        block = s.block()

        @block.sync
        def _(sp):
            sp.dma_start(bias[:, :], rows(a["L0_gnn_h_bias"])).then_inc(loaded, 16)

        @block.vector
        def _(dve):
            v, do = nc.vector, Chain(dve, dv)
            do(v.tensor_scalar(rden[:, :, :], acc[:, :, :, HD], 1e-30, None, ALU.max))
            do(v.reciprocal(rden[:, :, :], rden[:, :, :]))
            heads = acc[:, :, :, 0:HD].rearrange("p t h d -> p (t h) d")
            xh = x_res[:, :, :].rearrange("p t (h d) -> p (t h) d", h=HEADS)
            do(v.tensor_tensor(heads, heads, flat(rden[:, :, :]).unsqueeze(2).broadcast_to([P, NT * HEADS, HD]), ALU.mult))
            do(v.tensor_tensor(xh, xh, heads, ALU.add))
            dve.wait_ge(loaded, 16)
            do(v.tensor_tensor(x_res[:, :, :], x_res[:, :, :], bcast(bias[:, :], [[0, NT], [1, D]]), ALU.add))


def route(nc, name, c, experts, gate_w, gate_b, xnT, mask, top):
    E = experts
    with Stage(nc, name) as s:
        gw, gb = s.sb("gw", [P, 2, E]), s.sb("gb", [P, E])
        pr, score, down = s.sb("pr", [P, NT, E]), s.sb("score", [P, NT, E]), s.sb("down", [P, E])
        red = s.sb("red", [P, NT])
        pl = s.ps("pl", [P, NT, E])
        loaded, logits, shifted, powers, dv = (s.sem(k) for k in ("loaded", "logits", "shifted", "powers", "dv"))
        block = s.block()

        def wide(ap):
            return ap.unsqueeze(2).broadcast_to([P, NT, E])

        @block.sync
        def _(sp):
            sp.dma_start(gw[:, :, :], gate_w.rearrange("(k p) e -> p k e", p=P)).then_inc(loaded, 16)
            sp.dma_start(gb[:, :], rows(gate_b)).then_inc(loaded, 16)

        @block.tensor
        def _(pe):
            pe.wait_ge(loaded, 32)
            for t in range(NT):
                for k in range(2):
                    ins = nc.tensor.matmul(pl[:, t, :], xnT[:, k, t * P:(t + 1) * P], gw[:, k, :], start=(k == 0), stop=(k == 1))
            ins.then_inc(logits, 1)

        @block.scalar
        def _(act):
            act.wait_ge(shifted, 1)
            nc.scalar.activation(pr[:, :, :], pr[:, :, :], ACT.Exp).then_inc(powers, 1)

        @block.vector
        def _(dve):
            v, do = nc.vector, Chain(dve, dv)
            do(v.tensor_scalar(down[:, :], c["ramp"][:, 0:E], -1.0, float(E), ALU.mult, ALU.add))
            dve.wait_ge(loaded, 32)
            dve.wait_ge(logits, 1)
            do(v.tensor_tensor(pr[:, :, :], pl[:, :, :], bcast(gb[:, :], [[0, NT], [1, E]]), ALU.add))
            do(v.tensor_reduce(red[:, :], pr[:, :, :], AX.X, ALU.max))
            v.tensor_tensor(pr[:, :, :], pr[:, :, :], wide(red[:, :]), ALU.subtract).then_inc(shifted, 1)
            dve.wait_ge(powers, 1)
            do(v.tensor_reduce(red[:, :], pr[:, :, :], AX.X, ALU.add))
            do(v.reciprocal(red[:, :], red[:, :]))
            do(v.tensor_tensor(pr[:, :, :], pr[:, :, :], wide(red[:, :]), ALU.mult))
            for k in range(2):
                do(v.tensor_reduce(top[k][:, :], pr[:, :, :], AX.X, ALU.max))
                do(v.tensor_tensor(score[:, :, :], pr[:, :, :], wide(top[k][:, :]), ALU.is_equal))
                do(v.tensor_tensor(score[:, :, :], score[:, :, :], bcast(down[:, :], [[0, NT], [1, E]]), ALU.mult))
                do(v.tensor_reduce(red[:, :], score[:, :, :], AX.X, ALU.max))
                do(v.tensor_tensor(mask[k][:, :, :], score[:, :, :], wide(red[:, :]), ALU.is_equal))
                if k == 0:
                    do(v.scalar_tensor_tensor(out=pr[:, :, :], in0=mask[0][:, :, :], scalar=-2.0, in1=pr[:, :, :],
                                              op0=ALU.mult, op1=ALU.add))


def mixture(nc, c, a, xnT, x_res):
    G, N = 3, 3 * P
    with Stage(nc, "mix") as S:
        mask = [S.sb(f"mask{k}", [P, NT, EX0]) for k in range(2)]
        top = [S.sb(f"top{k}", [P, NT]) for k in range(2)]
        route(nc, "route0", c, EX0, a["L0_ffn_gW"], a["L0_ffn_gb"], xnT, mask, top)
        with Stage(nc, "mixf") as s:
            gate = s.sb("gate", [P, NT, EX0])
            w1, w2, w3 = s.sb("w1", [P, 2, 2 * P]), s.sb("w2", [P, 2, P]), s.sb("w3", [P, D])
            e1w, e2w, e3w = s.sb("e1w", [P, EX0, 2, P]), s.sb("e2w", [P, EX0, 64]), s.sb("e3w", [65, EX0, D])
            b1, b2, b3 = s.sb("b1", [P, 2]), s.sb("b2", [P, 1]), s.sb("b3", [P, D])
            eb1, eb2 = s.sb("eb1", [P, EX0]), s.sb("eb2", [64, EX0])
            s1, s2 = s.sb("s1", [P, 2, N]), s.sb("s2", [P, N])
            h1, h2 = s.sb("h1", [P, EX0, N]), s.sb("h2", [65, EX0, N])
            order1, order2, outs = [0, 1, 2, 3, 4, 5], [6, 7, 0, 1, 2], [[3, 4, 5], [6, 7, 0], [1, 2, 3]]
            every = order1 + order2 + sum(outs, [])
            banks = [s.ps(f"bank{b}", [P, 512]) for b in range(8)]
            loaded, dv, gated, biased = s.sem("loaded"), s.sem("dv"), s.sem("gated"), s.sem("biased")
            drop_ready, power_ready = s.sem("drop_ready"), s.sem("power_ready")
            l1, l2, l3 = s.sem("layer1"), s.sem("layer2"), s.sem("layer3")
            r1, r2 = s.sem("relu1"), s.sem("relu2")
            added = s.sem("added")
            block = s.block()
            loads = [
                (w1[:, :, :], a["L0_ffn_sW1"].rearrange("(k p) n -> p k n", p=P)),
                (w2[:, :, :], a["L0_ffn_sW2"].rearrange("(k p) n -> p k n", p=P)),
                (w3[:, :], a["L0_ffn_sW3"]),
                (e1w[:, :, :, :].rearrange("p e k n -> p (e k) n"), a["L0_ffn_eW1"].rearrange("e (k p) n -> p (e k) n", p=P)),
                (e2w[:, :, :], a["L0_ffn_eW2"].rearrange("e p n -> p e n")),
                (e3w[0:64, :, :], a["L0_ffn_eW3"].rearrange("e p n -> p e n")),
                (e3w[64:65, :, :], a["L0_ffn_eb3"].rearrange("(o e) n -> o e n", o=1)),
                (b1[:, :], a["L0_ffn_sb1"].rearrange("(k p) -> p k", p=P)),
                (b2[:, :], a["L0_ffn_sb2"].rearrange("(p o) -> p o", o=1)),
                (eb1[:, :], a["L0_ffn_eb1"].rearrange("e p -> p e")),
                (eb2[:, :], a["L0_ffn_eb2"].rearrange("e p -> p e")),
                (b3[:, :], rows(a["L0_ffn_sb3"])),
            ]
            LOADED = 16 * len(loads)

            @block.sync
            def _(sp):
                with nc.allow_non_contiguous_dma(reason="small biases"):
                    for dest, source in loads:
                        sp.dma_start(dest, source).then_inc(loaded, 16)

            @block.gpsimd
            def _(pool):
                nc.gpsimd.memset(h2[64:65, :, :], 1.0).then_inc(biased, 1)
                pool.wait_ge(biased, 1)
                pool.wait_ge(loaded, LOADED)
                nc.gpsimd.tensor_tensor(x_res[:, :, :], x_res[:, :, :], bcast(b3[:, :], [[0, NT], [1, D]]), ALU.add).then_inc(biased, 1)

            def wait_free(eng, i, q, first):
                before = [p for p in range(q) if every[p] == every[q]]
                if not before:
                    if first:
                        return
                    i, before = i - 1, [p for p in range(len(every)) if every[p] == every[q]]
                p = before[-1]
                if p < 6:
                    eng.wait_ge(r1, i * 6 + p + 1)
                elif p < 11:
                    eng.wait_ge(r2, i * 5 + p - 5)
                else:
                    t, m = divmod(p - 11, 3)
                    eng.wait_ge(added, i * G * 5 + t * 5 + min(2 * m + 2, 5))

            @block.tensor
            def _(pe):
                pe.wait_ge(loaded, LOADED)
                pe.wait_ge(biased, 1)

                def group(i, first=False):
                    cols = [xnT[:, k, bass.ds(i * N, N)] for k in range(2)]
                    for j, w in enumerate([w1[:, :, 0:P], w1[:, :, P:2 * P]] + [e1w[:, e, :, :] for e in range(EX0)]):
                        wait_free(pe, i, j, first)
                        b = order1[j]
                        for k in range(2):
                            ins = nc.tensor.matmul(banks[b][:, 0:N], w[:, k, :], cols[k], start=(k == 0), stop=(k == 1))
                        ins.then_inc(l1, 1)
                    for j in range(5):
                        wait_free(pe, i, 6 + j, first)
                        b = order2[j]
                        pe.wait_ge(r1, i * 6 + 2 + j)
                        if j == 0:
                            for k in range(2):
                                ins = nc.tensor.matmul(banks[b][:, 0:N], w2[:, k, :], s1[:, k, :], start=(k == 0), stop=(k == 1))
                        else:
                            ins = nc.tensor.matmul(banks[b][0:64, 0:N], e2w[:, j - 1, :], h1[:, j - 1, :], start=True, stop=True)
                        ins.then_inc(l2, 1)
                    pe.wait_ge(r2, i * 5 + 5)
                    for t in range(G):
                        for m in range(3):
                            wait_free(pe, i, 11 + 3 * t + m, first)
                            b = outs[t][m]
                            for o in range(2 * m, min(2 * m + 2, 5)):
                                half = banks[b][:, (o % 2) * D:(o % 2 + 1) * D]
                                if o == 0:
                                    ins = nc.tensor.matmul(half, s2[:, t * P:(t + 1) * P], w3[:, :], start=True, stop=True)
                                else:
                                    ins = nc.tensor.matmul(half, h2[:, o - 1, t * P:(t + 1) * P], e3w[:, o - 1, :], start=True, stop=True)
                            ins.then_inc(l3, 1)

                group(0, first=True)
                with pe.Fori(1, NT // G) as i:
                    group(i)

            @block.scalar
            def _(act):
                act.wait_ge(loaded, LOADED)
                act.wait_ge(drop_ready, 1)
                nc.scalar.activation(top[1][:, :], top[1][:, :], ACT.Exp).then_inc(power_ready, 1)

                def group(i, first=False):
                    for j in range(6):
                        act.wait_ge(l1, i * 6 + j + 1)
                        if not first:
                            act.wait_ge(l2, (i - 1) * 5 + max(j, 1))
                        dest, bias = (s1[:, j, :], b1[:, j:j + 1]) if j < 2 else (h1[:, j - 2, :], eb1[:, j - 2:j - 1])
                        nc.scalar.activation(dest, banks[order1[j]][:, 0:N], ACT.Relu, bias=bias).then_inc(r1, 1)
                    for j in range(5):
                        act.wait_ge(l2, i * 5 + j + 1)
                        if not first:
                            act.wait_ge(l3, i * 9)
                        bank = banks[order2[j]]
                        if j == 0:
                            nc.scalar.activation(s2[:, :], bank[:, 0:N], ACT.Relu, bias=b2[:, 0:1]).then_inc(r2, 1)
                        else:
                            nc.scalar.activation(h2[0:64, j - 1, :], bank[0:64, 0:N], ACT.Relu, bias=eb2[:, j - 1:j]).then_inc(r2, 1)

                group(0, first=True)
                with act.Fori(1, NT // G) as i:
                    group(i)

            @block.vector
            def _(dve):
                v, do = nc.vector, Chain(dve, dv)
                v.tensor_tensor(top[1][:, :], top[1][:, :], top[0][:, :], ALU.subtract).then_inc(drop_ready, 1)
                dve.wait_ge(power_ready, 1)
                do(v.tensor_scalar(top[0][:, :], top[1][:, :], 1.0, None, ALU.add))
                do(v.reciprocal(top[0][:, :], top[0][:, :]))
                do(v.tensor_tensor(top[1][:, :], top[1][:, :], top[0][:, :], ALU.mult))
                for k in range(2):
                    do(v.tensor_tensor(mask[k][:, :, :], mask[k][:, :, :], top[k][:, :].unsqueeze(2).broadcast_to([P, NT, EX0]), ALU.mult))
                do(v.tensor_tensor(gate[:, :, :], mask[0][:, :, :], mask[1][:, :, :], ALU.add))
                dve.wait_ge(biased, 2)
                with dve.Fori(0, NT // G) as i:
                    count = Steps(dve, added, i * G * 5)
                    for t in range(G):
                        x = flat(x_res[:, bass.ds(i * G + t, 1), :])
                        for o in range(5):
                            b = outs[t][o // 2]
                            half = banks[b][:, (o % 2) * D:(o % 2 + 1) * D]
                            if o % 2 == 0:
                                dve.wait_ge(l3, i * 9 + 3 * t + o // 2 + 1)
                            count.wait()
                            if o == 0:
                                count(v.tensor_tensor(x, x, half, ALU.add))
                            else:
                                count(v.scalar_tensor_tensor(out=x, in0=half, scalar=gate[:, bass.ds(i * G + t, 1), o - 1],
                                                             in1=x, op0=ALU.mult, op1=ALU.add))


def turn_rows(nc, name, c, src, dstT):
    with Stage(nc, name) as s:
        row = [s.sb(f"row{u}", [P, D]) for u in range(2)]
        pt = [s.ps(f"pt{u}", [P, 2, P]) for u in range(2)]
        taken, turned, copied = s.sem("taken"), s.sem("turned"), s.sem("copied")
        block = s.block()

        def pairs(eng, step):
            for u in range(2):
                step(0, u, True)
            with eng.Fori(1, NT // 2) as i:
                for u in range(2):
                    step(i, u, False)

        @block.vector
        def _(dve):
            def step(i, u, first):
                if not first:
                    dve.wait_ge(turned, i * 2 + u - 1)
                nc.vector.tensor_scalar(row[u][:, :], flat(src[:, bass.ds(i * 2 + u, 1), :]), 1.0, None, ALU.mult).then_inc(taken, 1)
            pairs(dve, step)

        @block.tensor
        def _(pe):
            def step(i, u, first):
                pe.wait_ge(taken, i * 2 + u + 1)
                if not first:
                    pe.wait_ge(copied, i * 2 + u - 1)
                for h in range(2):
                    ins = nc.tensor.transpose(pt[u][:, h, :], row[u][:, h * P:(h + 1) * P], c["ident"][:, :])
                ins.then_inc(turned, 1)
            pairs(pe, step)

        @block.scalar
        def _(act):
            def step(i, u, first):
                act.wait_ge(turned, i * 2 + u + 1)
                nc.scalar.activation(dstT[:, :, bass.ds((i * 2 + u) * P, P)], pt[u][:, :, :], ACT.Copy).then_inc(copied, 1)
            pairs(act, step)


def convolve(nc, c, a, agg, table1, xtab, bins1):
    K = 4
    GROUPS = ET // K
    N = K * P
    with Stage(nc, "conv") as s:
        two = range(2)
        recs = s.sb("recs", [P, ET, W1])
        rowidx = s.sb("rowidx", [P, ET], I32)
        wf1, wf2 = s.sb("wf1", [NG, D]), s.sb("wf2", [P, 2, D])
        bf1, bf2 = s.sb("bf1", [P, 2]), s.sb("bf2", [P, D])
        idx = [s.sb(f"idx{u}", [P, K], I32) for u in two]
        got = [s.sb(f"got{u}", [P, K, D]) for u in two]
        attr = [s.sb(f"attr{u}", [P, K, NG]) for u in two]
        attrT = [s.sb(f"attrT{u}", [NG, N]) for u in two]
        act1 = [s.sb(f"act1{u}", [P, 2, N]) for u in two]
        oh = [s.sb(f"onehot{u}", [P, K, P]) for u in two]
        filt = s.sb("filt", [P, K, D])
        msg = [s.sb(f"msg{u}", [P, K, D]) for u in two]
        pT = s.ps("pT", [NG, N])
        p1 = [s.ps(f"p1{h}", [P, N]) for h in two]
        pf = [s.ps(f"pf{h}", [P, 2, D]) for h in two]
        psum = [s.ps(f"psum{h}", [P, 2, D]) for h in two]
        loaded, prep = s.sem("loaded"), s.sem("prep")
        idx_ready, attr_ready, turned, attrT_ready = (s.sem(n) for n in ("idx_ready", "attr_ready", "turned", "attrT_ready"))
        layer1, act_ready, filtered, oh_ready = (s.sem(n) for n in ("layer1", "act_ready", "filtered", "oh_ready"))
        filt_ready, msg_ready, summed, agg_done = (s.sem(n) for n in ("filt_ready", "msg_ready", "summed", "agg_done"))
        got_s = [s.sem(f"got_s{u}") for u in two]
        block = s.block()
        LOADED = 16 * 5

        def in_steps(eng, step):
            step(0, 0, {0})
            step(0, 1, {0, 1})
            step(1, 0, {0, 1, 2})
            step(1, 1, {0, 1, 2, 3})
            with eng.Fori(2, GROUPS // 2) as i:
                step(i, 0, {0, 1, 2, 3})
                step(i, 1, {0, 1, 2, 3})
            step(GROUPS // 2, 0, {1, 2, 3})
            step(GROUPS // 2, 1, {2, 3})
            step(GROUPS // 2 + 1, 0, {3})

        @block.sync
        def _(sp):
            sp.dma_start(recs[:, :, :], table1.rearrange("(p t) w -> p t w", p=P)).then_inc(loaded, 16)
            sp.dma_start(wf1[:, :], a["L1_gnn_Wf1"]).then_inc(loaded, 16)
            sp.dma_start(wf2[:, :, :], a["L1_gnn_Wf2"].rearrange("(k p) n -> p k n", p=P)).then_inc(loaded, 16)
            with nc.allow_non_contiguous_dma(reason="a small bias"):
                sp.dma_start(bf1[:, :], a["L1_gnn_bf1"].rearrange("(k p) -> p k", p=P)).then_inc(loaded, 16)
            sp.dma_start(bf2[:, :], rows(a["L1_gnn_bf2"])).then_inc(loaded, 16)

        @block.gpsimd
        def _(pool):
            nc.gpsimd.memset(agg[:, :, :], 0.0).then_inc(prep, 1)
            pool.wait_ge(prep, 2)

            def gathers(i, u, first):
                g = i * 2 + u
                if not first:
                    pool.wait_ge(msg_ready, (g - 1) * 2)
                nc.gpsimd.tensor_copy(idx[u][:, :], rowidx[:, bass.ds(g * K, K)]).then_inc(idx_ready, 1)
                pool.wait_ge(idx_ready, g + 1)
                pool.nop(nofuse=True)
                for k in range(K):
                    nc.gpsimd.indirect_dma_start(
                        out=got[u][:, k, :], out_offset=None, in_=xtab,
                        in_offset=bass.IndirectOffsetOnAxis(ap=idx[u][:, k:k + 1], axis=0)).then_inc(got_s[u], 16)

            for u in two:
                gathers(0, u, True)
            with pool.Fori(1, GROUPS // 2) as i:
                for u in two:
                    gathers(i, u, False)

        @block.scalar
        def _(act):
            act.wait_ge(loaded, LOADED)

            def step(i, u, parts):
                g, w = i * 2 + u, 1 - u
                if 0 in parts:
                    if 2 in parts:
                        act.wait_ge(turned, g - 1)
                    nc.scalar.activation(attr[u][:, :, :], recs[:, bass.ds(g * K, K), 0:NG], ACT.Copy).then_inc(attr_ready, 1)
                if 1 in parts:
                    for h in two:
                        act.wait_ge(layer1, (g - 1) * 2 + h + 1)
                        if 3 in parts:
                            act.wait_ge(filtered, (g - 2) * 2)
                        nc.scalar.activation(act1[w][:, h, :], p1[h][:, :], ACT.Silu, bias=bf1[:, h:h + 1]).then_inc(act_ready, 1)
                if 0 in parts:
                    act.wait_ge(turned, g + 1)
                    if 2 in parts:
                        act.wait_ge(layer1, (g - 1) * 2)
                    nc.scalar.activation(attrT[u][:, :], pT[:, :], ACT.Copy).then_inc(attrT_ready, 1)

            in_steps(act, step)

        @block.tensor
        def _(pe):
            pe.wait_ge(loaded, LOADED)

            def step(i, u, parts):
                g, w = i * 2 + u, 1 - u
                if 0 in parts:
                    pe.wait_ge(attr_ready, g + 1)
                    if 1 in parts:
                        pe.wait_ge(attrT_ready, g)
                    for k in range(K):
                        ins = nc.tensor.transpose(pT[:, k * P:(k + 1) * P], attr[u][:, k, :], c["ident"][:, :])
                    ins.then_inc(turned, 1)
                if 1 in parts:
                    for h in two:
                        pe.wait_ge(attrT_ready, g)
                        if 2 in parts:
                            pe.wait_ge(act_ready, (g - 2) * 2 + h + 1)
                        nc.tensor.matmul(p1[h][:, :], wf1[:, h * P:(h + 1) * P], attrT[w][:, :], start=True, stop=True).then_inc(layer1, 1)
                if 2 in parts:
                    pe.wait_ge(act_ready, (g - 1) * 2)
                    for b in two:
                        if 3 in parts:
                            pe.wait_ge(filt_ready, (g - 3) * 2 + b + 1)
                        for k in two:
                            for h in two:
                                ins = nc.tensor.matmul(pf[b][:, k, :], act1[u][:, h, (2 * b + k) * P:(2 * b + k + 1) * P], wf2[:, h, :],
                                                       start=(h == 0), stop=(h == 1))
                        ins.then_inc(filtered, 1)
                if 3 in parts:
                    for b in two:
                        pe.wait_ge(oh_ready, g - 2)
                        pe.wait_ge(msg_ready, (g - 3) * 2 + b + 1)
                        pe.wait_ge(agg_done, (g - 3) * K if not isinstance(g, int) or g > 3 else 0)
                        for k in two:
                            ins = nc.tensor.matmul(psum[b][:, k, :], oh[w][:, 2 * b + k, :], msg[w][:, 2 * b + k, :], start=True, stop=True)
                        ins.then_inc(summed, 1)

            in_steps(pe, step)

        @block.vector
        def _(dve):
            v = nc.vector
            dve.wait_ge(loaded, LOADED)
            v.tensor_copy(rowidx[:, :], recs[:, :, NG]).then_inc(prep, 1)

            def step(i, u, parts):
                g, w = i * 2 + u, 1 - u
                if 3 in parts:
                    bins = [dve.value_load(bins1[0:1, bass.ds((g - 3) * K + k, 1)], min_val=0, max_val=NT - 1) for k in range(K)]
                if 2 in parts:
                    node = recs[:, bass.ds((g - 2) * K, K), NG + 1]
                    if 3 in parts and not (isinstance(g, int) and g == 3):
                        dve.wait_ge(summed, (g - 3) * 2)
                    v.tensor_tensor(oh[u][:, :, :], bcast(c["ramp"][:, 0:P], [[0, K], [1, P]]),
                                    node.unsqueeze(2).broadcast_to([P, K, P]), ALU.is_equal).then_inc(oh_ready, 1)
                    dve.wait_ge(msg_ready, (g - 2) * 2)
                    for b in two:
                        dve.wait_ge(filtered, (g - 2) * 2 + b + 1)
                        part = filt[:, 2 * b:2 * b + 2, :]
                        v.tensor_tensor(part, pf[b][:, :, :], bcast(bf2[:, :], [[0, 2], [1, D]]), ALU.add).then_inc(filt_ready, 1)
                    dve.wait_ge(got_s[u], i * 16 * K)
                    for b in two:
                        dve.wait_ge(filt_ready, (g - 2) * 2 + b + 1)
                        part = slice(2 * b, 2 * b + 2)
                        v.tensor_tensor(msg[u][:, part, :], filt[:, part, :], got[u][:, part, :], ALU.mult).then_inc(msg_ready, 1)
                if 3 in parts:
                    for k in range(K):
                        if k % 2 == 0:
                            dve.wait_ge(summed, (g - 3) * 2 + k // 2 + 1)
                        dve.wait_ge(agg_done, (g - 3) * K + k)
                        at = flat(agg[:, bass.ds(bins[k], 1), :])
                        v.tensor_tensor(at, at, psum[k // 2][:, k % 2, :], ALU.add).then_inc(agg_done, 1)

            dve.wait_ge(prep, 2)
            in_steps(dve, step)


def update(nc, c, a, aggT, xn, x_res):
    G, N = 10, PADN // 10
    BN, BC = 10, NODES // 10
    with Stage(nc, "upd") as s:
        w1, w2 = s.sb("w1", [P, 2, D]), s.sb("w2", [P, 2, D])
        b1, b2, gamma, beta = (s.sb(n, [P, 2]) for n in ("b1", "b2", "gamma", "beta"))
        h1 = s.sb("h1", [P, 2, N])
        hT = s.sb("hT", [P, 2, PADN])
        st, mv = s.sb("st", [P, 2, BN, 6]), s.sb("mv", [P, 2, 2])
        scale, shift = s.sb("scale", [P, 2]), s.sb("shift", [P, 2])
        col = [s.sb(f"col{u}", [P, 2, P]) for u in range(2)]
        p1 = [s.ps(f"p1{h}", [P, N]) for h in range(2)]
        p2 = [s.ps(f"p2{h}", [P, N]) for h in range(2)]
        pt = [s.ps(f"pt{u}", [P, D]) for u in range(2)]
        names = ("loaded", "dv", "layer1", "act1", "layer2", "kept", "var_ready", "std_ready", "scale_ready", "xn_added",
                 "taken", "turned", "joined")
        loaded, dv, layer1, act1, layer2, kept, var_ready, std_ready, scale_ready, xn_added, taken, turned, joined = (s.sem(n) for n in names)
        block = s.block()
        loads = [
            (w1[:, :, :], a["L1_gnn_Wu1"].rearrange("(k p) n -> p k n", p=P)),
            (w2[:, :, :], a["L1_gnn_Wu2"].rearrange("(k p) n -> p k n", p=P)),
            (b1[:, :], a["L1_gnn_bu1"].rearrange("(k p) -> p k", p=P)), (b2[:, :], a["L1_gnn_bu2"].rearrange("(k p) -> p k", p=P)),
            (gamma[:, :], a["L1_gnn_gamma"].rearrange("(k p) -> p k", p=P)), (beta[:, :], a["L1_gnn_beta"].rearrange("(k p) -> p k", p=P)),
        ]

        @block.sync
        def _(sp):
            with nc.allow_non_contiguous_dma(reason="small vectors"):
                for dest, source in loads:
                    sp.dma_start(dest, source).then_inc(loaded, 16)

        @block.gpsimd
        def _(pool):
            nc.gpsimd.tensor_tensor(x_res[:, :, :], x_res[:, :, :], xn[:, :, :], ALU.add).then_inc(xn_added, 1)

        @block.tensor
        def _(pe):
            pe.wait_ge(loaded, 16 * len(loads))

            def group(i, first):
                for h in range(2):
                    if not first:
                        pe.wait_ge(act1, (i - 1) * 2 + h + 1)
                    for k in range(2):
                        ins = nc.tensor.matmul(p1[h][:, :], w1[:, k, h * P:(h + 1) * P], aggT[:, k, bass.ds(i * N, N)], start=(k == 0), stop=(k == 1))
                    ins.then_inc(layer1, 1)
                pe.wait_ge(act1, i * 2 + 2)
                for h in range(2):
                    if not first:
                        pe.wait_ge(kept, (i - 1) * 2 + h + 1)
                    for k in range(2):
                        ins = nc.tensor.matmul(p2[h][:, :], w2[:, k, h * P:(h + 1) * P], h1[:, k, :], start=(k == 0), stop=(k == 1))
                    ins.then_inc(layer2, 1)

            group(0, True)
            with pe.Fori(1, G) as i:
                group(i, False)

            def turn(i, u, first):
                pe.wait_ge(taken, (i * 2 + u + 1) * 2)
                if not first:
                    pe.wait_ge(joined, i * 2 + u - 1)
                for h in range(2):
                    ins = nc.tensor.transpose(pt[u][:, h * P:(h + 1) * P], col[u][:, h, :], c["ident"][:, :])
                ins.then_inc(turned, 1)

            for u in range(2):
                turn(0, u, True)
            with pe.Fori(1, NT // 2) as i:
                for u in range(2):
                    turn(i, u, False)

        @block.scalar
        def _(act):
            act.wait_ge(loaded, 16 * len(loads))

            def group(i, first):
                for h in range(2):
                    act.wait_ge(layer1, i * 2 + h + 1)
                    if not first:
                        act.wait_ge(layer2, (i - 1) * 2 + 2)
                    nc.scalar.activation(h1[:, h, :], p1[h][:, :], ACT.Silu, bias=b1[:, h:h + 1]).then_inc(act1, 1)

            group(0, True)
            with act.Fori(1, G) as i:
                group(i, False)
            act.wait_ge(var_ready, 1)
            nc.scalar.activation(scale[:, :], mv[:, :, 1], ACT.Sqrt, bias=c["bn_eps"][:, 0:1]).then_inc(std_ready, 1)
            act.wait_ge(scale_ready, 1)

            def take(i, u, first):
                if not first:
                    act.wait_ge(turned, i * 2 + u - 1)
                for h in range(2):
                    ins = nc.scalar.activation(col[u][:, h, :], hT[:, h, bass.ds((i * 2 + u) * P, P)], ACT.Identity,
                                               bias=shift[:, h:h + 1], scale=scale[:, h:h + 1])
                    ins.then_inc(taken, 1)

            for u in range(2):
                take(0, u, True)
            with act.Fori(1, NT // 2) as i:
                for u in range(2):
                    take(i, u, False)

        @block.vector
        def _(dve):
            v, do = nc.vector, Chain(dve, dv)
            dve.wait_ge(loaded, 16 * len(loads))
            with dve.Fori(0, G) as i:
                for h in range(2):
                    dve.wait_ge(layer2, i * 2 + h + 1)
                    v.tensor_scalar(hT[:, h, bass.ds(i * N, N)], p2[h][:, :], b2[:, h:h + 1], None, ALU.add).then_inc(kept, 1)
            dve.wait_ge(kept, 2 * G)
            for h in range(2):
                for j in range(BN):
                    do(v.bn_stats(st[:, h, j, :], hT[:, h, j * BC:(j + 1) * BC]))
                do(v.bn_aggr(mv[:, h, :], st[:, h, :, :]))
            v.memset(shift[:, :], 0.0).then_inc(var_ready, 1)
            dve.wait_ge(std_ready, 1)
            dve.wait_ge(var_ready, 1)
            do(v.reciprocal(scale[:, :], scale[:, :]))
            do(v.tensor_tensor(scale[:, :], scale[:, :], gamma[:, :], ALU.mult))
            do(v.tensor_tensor(shift[:, :], mv[:, :, 0], scale[:, :], ALU.mult))
            v.tensor_tensor(shift[:, :], beta[:, :], shift[:, :], ALU.subtract).then_inc(scale_ready, 1)
            dve.wait_ge(xn_added, 1)
            with dve.Fori(0, NT // 2) as i:
                for u in range(2):
                    dve.wait_ge(turned, i * 2 + u + 1)
                    x = flat(x_res[:, bass.ds(i * 2 + u, 1), :])
                    v.tensor_tensor(x, x, pt[u][:, :], ALU.add).then_inc(joined, 1)


def routed(nc, c, a, xnT, x_res, xtab, slots, results):
    U2 = 2
    with Stage(nc, "rt") as S:
        mask = [S.sb(f"mask{k}", [P, NT, EX1]) for k in range(2)]
        top = [S.sb(f"top{k}", [P, NT]) for k in range(2)]
        bin_f, pos_f = S.sb("bin_f", [P, 2 * NT]), S.sb("pos_f", [P, 2 * NT])
        addr_i, pos_i = S.sb("addr_i", [P, 2 * NT], I32), S.sb("pos_i", [P, 2 * NT], I32)
        expert = S.sb("expert", [1, 512], I32)
        token = S.sb("token", [P, NT], I32)
        route(nc, "route1", c, EX1, a["L1_ffn_gate_w"], a["L1_ffn_gate_b"], xnT, mask, top)

        with Stage(nc, "pick") as s:
            tmp, red = s.sb("tmp", [P, NT, EX1]), s.sb("red", [P, NT])
            empty = s.sb("empty", [P, MT], I32)
            dv, cleared, filled = s.sem("dv"), s.sem("cleared"), s.sem("filled")
            block = s.block()

            @block.gpsimd
            def _(pool):
                nc.gpsimd.memset(empty[:, :], 0).then_inc(cleared, 1)
                nc.gpsimd.iota(token[:, :], pattern=[[P, NT]], base=0, channel_multiplier=1).then_inc(cleared, 1)

            @block.sync
            def _(sp):
                sp.wait_ge(cleared, 2)
                sp.dma_start(slots.rearrange("(p t) o -> p (t o)", p=P), empty[:, :]).then_inc(filled, 16)
                sp.wait_ge(filled, 16)

            @block.vector
            def _(dve):
                v, do = nc.vector, Chain(dve, dv)
                bins = bin_f[:, :].rearrange("p (k t) -> p k t", k=2)
                for k in range(2):
                    do(v.tensor_tensor(tmp[:, :, :], mask[k][:, :, :], bcast(c["ramp"][:, 0:EX1], [[0, NT], [1, EX1]]), ALU.mult))
                    do(v.tensor_reduce(bins[:, k, :], tmp[:, :, :], AX.X, ALU.add))
                    last = bins[:, k, NT - 1:NT]
                    do(v.scalar_tensor_tensor(out=last, in0=c["beyond"][:, :], scalar=100.0, in1=last, op0=ALU.mult, op1=ALU.add))
                do(v.tensor_tensor(red[:, :], top[0][:, :], top[1][:, :], ALU.add))
                do(v.reciprocal(red[:, :], red[:, :]))
                for k in range(2):
                    do(v.tensor_tensor(top[k][:, :], top[k][:, :], red[:, :], ALU.mult))

        positions(nc, "by_expert", c, P, 2 * NT, EX1, MT, bin_f[:, :], pos_f[:, :], addr_i[:, :], expert)

        with Stage(nc, "send") as s:
            slot = [s.sb(f"slot{u}", [P, 2], I32) for u in range(2)]
            tok = [s.sb(f"tok{u}", [P, 1], I32) for u in range(2)]
            staged = s.sem("staged")
            sent = [[s.sem(f"sent{u}{k}") for k in range(2)] for u in range(2)]
            dv = s.sem("dv")
            block = s.block()

            @block.vector
            def _(dve):
                nc.vector.tensor_copy(pos_i[:, :], pos_f[:, :]).then_inc(dv, 1)

            @block.gpsimd
            def _(pool):
                def tile(t, u, i, n):
                    for k in range(2):
                        pool.wait_ge(sent[u][k], i * 16)
                    view = addr_i[:, :].rearrange("p (k t) -> p t k", k=2)
                    nc.gpsimd.tensor_copy(slot[u][:, :].unsqueeze(1), view[:, bass.ds(t, 1), :]).then_inc(staged, 1)
                    nc.gpsimd.tensor_copy(tok[u][:, :], token[:, bass.ds(t, 1)]).then_inc(staged, 1)
                    pool.wait_ge(staged, t * 2 + 2)
                    pool.nop(nofuse=True)
                    for k in range(2):
                        nc.gpsimd.indirect_dma_start(
                            out=slots, out_offset=bass.IndirectOffsetOnAxis(ap=slot[u][0:n, k:k + 1], axis=0),
                            in_=tok[u][0:n, :], in_offset=None).then_inc(sent[u][k], 16)

                with pool.Fori(0, NT // 2 - 1) as i:
                    for u in range(2):
                        tile(i * 2 + u, u, i, P)
                tile(NT - 2, 0, NT // 2 - 1, P)
                tile(NT - 1, 1, NT // 2 - 1, TAIL)
                for u in range(2):
                    for k in range(2):
                        pool.wait_ge(sent[u][k], 16 * (NT // 2))

        with Stage(nc, "moe") as s:
            tokens = s.sb("tokens", [P, MT], I32)
            two = range(2)
            idx = [s.sb(f"idx{u}", [P, 1], I32) for u in two]
            got = [s.sb(f"got{u}", [P, D]) for u in two]
            xT = [s.sb(f"xT{u}", [P, 2, P]) for u in two]
            w1 = [s.sb(f"w1{u}", [P, 2, HID]) for u in two]
            w2 = [s.sb(f"w2{u}", [P, 2, HID]) for u in two]
            w3 = [s.sb(f"w3{u}", [P, HID // P, D]) for u in two]
            gatev, hid = s.sb("gatev", [P, HID]), [s.sb(f"hid{u}", [P, HID]) for u in two]
            y = [s.sb(f"y{u}", [P, D]) for u in two]
            pT = s.ps("pT", [P, 2, P])
            p1 = [s.ps(f"p1{u}", [P, HID]) for u in two]
            p2 = [s.ps(f"p2{u}", [P, HID]) for u in two]
            p3 = [s.ps(f"p3{u}", [P, D]) for u in two]
            w_s = [[s.sem(f"w{n}_loaded{u}") for n in range(3)] for u in two]
            loaded, idx_ready = s.sem("loaded"), s.sem("idx_ready")
            got_s = [s.sem(f"got_s{u}") for u in two]
            turned, xT_ready, up, gate_ready, hid_ready, down = (
                s.sem(n) for n in ("turned", "xT_ready", "up", "gate_ready", "hid_ready", "down"))
            y_ready = [s.sem(f"y_ready{u}") for u in two]
            stored = [s.sem(f"stored{u}") for u in two]
            block = s.block()
            NH = HID // P
            T2 = MT // 2

            @block.sync
            def _(sp):
                sp.dma_start(tokens[:, :], slots.rearrange("(p t) o -> p (t o)", p=P)).then_inc(loaded, 16)
                v1 = a["L1_ffn_w1"].rearrange("e (k p) n -> e p k n", p=P)
                v2 = a["L1_ffn_w2"].rearrange("e (k p) n -> e p k n", p=P)
                v3 = a["L1_ffn_w3"].rearrange("e (k p) n -> e p k n", p=P)

                def tile(i, u, first):
                    t = i * 2 + u
                    e = sp.value_load(expert[0:1, bass.ds(t, 1)], min_val=0, max_val=EX1 - 1)
                    if not first:
                        sp.wait_ge(up, t - 1)
                        sp.nop(nofuse=True)
                    for n, (w, v) in enumerate(((w1, v1), (w2, v2))):
                        sp.dma_start(w[u][:, :, :], v[bass.ds(e, 1)].rearrange("o p k n -> (o p) k n")).then_inc(w_s[u][n], 16)
                    if not first:
                        sp.wait_ge(down, t - 1)
                        sp.nop(nofuse=True)
                    sp.dma_start(w3[u][:, :, :], v3[bass.ds(e, 1)].rearrange("o p k n -> (o p) k n")).then_inc(w_s[u][2], 16)

                for u in two:
                    tile(0, u, True)
                with sp.Fori(1, T2) as i:
                    for u in two:
                        tile(i, u, False)

            @block.gpsimd
            def _(pool):
                pool.wait_ge(loaded, 16)

                def gather(i, u, first):
                    t = i * 2 + u
                    if not first:
                        pool.wait_ge(turned, t - 1)
                    nc.gpsimd.tensor_copy(idx[u][:, :], tokens[:, bass.ds(t, 1)]).then_inc(idx_ready, 1)
                    pool.wait_ge(idx_ready, t + 1)
                    pool.nop(nofuse=True)
                    nc.gpsimd.indirect_dma_start(
                        out=got[u][:, :], out_offset=None, in_=xtab,
                        in_offset=bass.IndirectOffsetOnAxis(ap=idx[u][:, 0:1], axis=0)).then_inc(got_s[u], 16)

                for u in two:
                    gather(0, u, True)
                with pool.Fori(1, T2) as i:
                    for u in two:
                        gather(i, u, False)

            def in_steps(eng, step):
                step(0, 0, {0})
                step(0, 1, {0, 1})
                with eng.Fori(1, T2) as i:
                    step(i, 0, {0, 1, 2})
                    step(i, 1, {0, 1, 2})
                step(T2, 0, {1, 2})
                step(T2, 1, {2})

            @block.tensor
            def _(pe):
                def step(i, u, parts):
                    t, w = i * 2 + u, 1 - u
                    if 0 in parts:
                        pe.wait_ge(got_s[u], (i + 1) * 16)
                        if 1 in parts:
                            pe.wait_ge(xT_ready, t)
                        for h in two:
                            ins = nc.tensor.transpose(pT[:, h, :], got[u][:, h * P:(h + 1) * P], c["ident"][:, :])
                        ins.then_inc(turned, 1)
                    if 1 in parts:
                        pe.wait_ge(xT_ready, t)
                        done = (i + 1) * 16 if u == 1 else i * 16
                        for n, (wt, ps) in enumerate(((w1, p1), (w2, p2))):
                            pe.wait_ge(w_s[w][n], done)
                            if 2 in parts and not (isinstance(t, int) and t < 3):
                                pe.wait_ge(hid_ready, t - 2)
                            for j in range(NH):
                                for k in two:
                                    ins = nc.tensor.matmul(ps[w][:, j * P:(j + 1) * P], wt[w][:, k, j * P:(j + 1) * P], xT[w][:, k, :],
                                                           start=(k == 0), stop=(k == 1))
                        ins.then_inc(up, 1)
                    if 2 in parts:
                        pe.wait_ge(hid_ready, t - 1)
                        pe.wait_ge(w_s[u][2], i * 16)
                        pe.wait_ge(y_ready[u], i - 1)
                        for j in range(NH):
                            ins = nc.tensor.matmul(p3[u][:, :], hid[u][:, j * P:(j + 1) * P], w3[u][:, j, :], start=(j == 0), stop=(j == NH - 1))
                        ins.then_inc(down, 1)

                in_steps(pe, step)

            @block.scalar
            def _(act):
                yv = results.rearrange("(t p) d -> t p d", p=P)

                def step(i, u, parts):
                    t, w = i * 2 + u, 1 - u
                    if 0 in parts:
                        act.wait_ge(turned, t + 1)
                        if 2 in parts:
                            act.wait_ge(up, t - 1)
                        nc.scalar.activation(xT[u][:, :, :], pT[:, :, :], ACT.Copy).then_inc(xT_ready, 1)
                    if 1 in parts:
                        act.wait_ge(up, t)
                        if 2 in parts:
                            act.wait_ge(hid_ready, t - 1)
                        nc.scalar.activation(gatev[:, :], p1[w][:, :], ACT.Silu).then_inc(gate_ready, 1)
                    if 2 in parts:
                        act.wait_ge(down, t - 1)
                        act.wait_ge(stored[u], (i - 1) * 16)
                        nc.scalar.activation(y[u][:, :], p3[u][:, :], ACT.Copy).then_inc(y_ready[u], 1)
                        act.wait_ge(y_ready[u], i)
                        act.dma_start(yv[bass.ds(t - 2, 1)].rearrange("o p d -> (o p) d"), y[u][:, :]).then_inc(stored[u], 16)

                in_steps(act, step)
                for u in two:
                    act.wait_ge(stored[u], 16 * T2)

            @block.vector
            def _(dve):
                def step(i, u, parts):
                    t, w = i * 2 + u, 1 - u
                    if 1 in parts:
                        dve.wait_ge(gate_ready, t)
                        if 2 in parts and not (isinstance(t, int) and t < 3):
                            dve.wait_ge(down, t - 2)
                        nc.vector.tensor_tensor(hid[w][:, :], gatev[:, :], p2[w][:, :], ALU.mult).then_inc(hid_ready, 1)

                in_steps(dve, step)

        with Stage(nc, "comb") as s:
            two = range(2)
            idx = [s.sb(f"idx{u}", [P, 2], I32) for u in two]
            got = [[s.sb(f"got{u}{k}", [P, D]) for k in two] for u in two]
            got_s = [[s.sem(f"got_s{u}{k}") for k in two] for u in two]
            idx_ready, added = s.sem("idx_ready"), s.sem("added")
            block = s.block()

            @block.gpsimd
            def _(pool):
                def tile(t, u, i, n, first=False):
                    if not first:
                        pool.wait_ge(added, (t - 1) * 2)
                    view = pos_i[:, :].rearrange("p (k t) -> p t k", k=2)
                    nc.gpsimd.tensor_copy(idx[u][:, :].unsqueeze(1), view[:, bass.ds(t, 1), :]).then_inc(idx_ready, 1)
                    pool.wait_ge(idx_ready, t + 1)
                    pool.nop(nofuse=True)
                    for k in two:
                        nc.gpsimd.indirect_dma_start(
                            out=got[u][k][0:n, :], out_offset=None, in_=results,
                            in_offset=bass.IndirectOffsetOnAxis(ap=idx[u][0:n, k:k + 1], axis=0)).then_inc(got_s[u][k], 16)

                for u in two:
                    tile(u, u, 0, P, first=True)
                with pool.Fori(1, NT // 2 - 1) as i:
                    for u in two:
                        tile(i * 2 + u, u, i, P)
                tile(NT - 2, 0, NT // 2 - 1, P)
                tile(NT - 1, 1, NT // 2 - 1, TAIL)

            @block.vector
            def _(dve):
                def tile(t, u, i, n):
                    for k in two:
                        dve.wait_ge(got_s[u][k], (i + 1) * 16)
                        dve.wait_ge(added, t * 2 + k)
                        x = flat(x_res[0:n, bass.ds(t, 1), :])
                        nc.vector.scalar_tensor_tensor(out=x, in0=got[u][k][0:n, :], scalar=top[k][0:n, bass.ds(t, 1)], in1=x,
                                                       op0=ALU.mult, op1=ALU.add).then_inc(added, 1)

                with dve.Fori(0, NT // 2 - 1) as i:
                    for u in two:
                        tile(i * 2 + u, u, i, P)
                tile(NT - 2, 0, NT // 2 - 1, P)
                tile(NT - 1, 1, NT // 2 - 1, TAIL)


def store(nc, x_res, out):
    with Stage(nc, "store") as s:
        stored = s.sem("stored")
        block = s.block()

        @block.sync
        def _(sp):
            sp.dma_start(out[0:(NT - 1) * P, :].rearrange("(t p) d -> p t d", p=P), x_res[:, 0:NT - 1, :]).then_inc(stored, 16)
            sp.dma_start(out[(NT - 1) * P:NODES, :], x_res[0:TAIL, NT - 1, :]).then_inc(stored, 16)
            sp.wait_ge(stored, 32)


def graph_layers(nc, a, out):
    feat = nc.dram_tensor("feat", (RELS * PADN, FW), F32).ap()
    table0 = nc.dram_tensor("table0", (P * ET, W0), F32).ap()
    table1 = nc.dram_tensor("table1", (P * ET, W1), F32).ap()
    xtab = nc.dram_tensor("xtab", (PADN, D), F32).ap()
    xtab2 = nc.dram_tensor("xtab2", (PADN, D), F32).ap()
    slots = nc.dram_tensor("slots", (P * MT, 1), I32).ap()
    results = nc.dram_tensor("results", (P * MT, D), F32).ap()
    with Stage(nc, "all") as S:
        x_res = S.sb("x_res", [P, NT, D])
        c = make_consts(S)
        constants(nc, c, a["x"], x_res)
        bins0, bins1 = S.sb("bins0", [1, 512], I32), S.sb("bins1", [1, 512], I32)
        with Stage(nc, "l0") as L:
            rec1, addr1 = L.sb("rec1", [P, EJ, W1]), L.sb("addr1", [P, EJ], I32)
            er = L.sb("er", [P, NT, RELS * HEADS])
            with Stage(nc, "l0a") as M:
                rec0, addr0 = M.sb("rec0", [P, EJ, W0]), M.sb("addr0", [P, EJ], I32)
                with Stage(nc, "l0b") as N:
                    pos_f = N.sb("pos_f", [P, EJ])
                    edge_records(nc, c, a, rec0, rec1, pos_f, addr0, addr1, bins0, bins1, table0, table1)
                with Stage(nc, "l0c") as N:
                    xnT = N.sb("xnT", [P, 2, PADN])
                    with Stage(nc, "l0d") as O:
                        xn = O.sb("xn", [P, NT, D])
                        layer_norm(nc, "ln0", c, x_res, xn, xnT)
                    project(nc, c, a, xnT, er, feat, rec0, addr0, table0, rec1)
            acc = L.sb("acc", [P, NT, HEADS, HD + 1])
            attend(nc, c, er, acc, rec1, addr1, table0, table1, feat, bins0)
            join_attention(nc, c, a, acc, x_res)
        with Stage(nc, "l1") as L:
            xn, xnT = L.sb("xn", [P, NT, D]), L.sb("xnT", [P, 2, PADN])
            layer_norm(nc, "ln1", c, x_res, xn, xnT)
            mixture(nc, c, a, xnT, x_res)
        with Stage(nc, "l2") as L:
            xn = L.sb("xn", [P, NT, D])
            with Stage(nc, "l2a") as M:
                xnT = M.sb("xnT", [P, 2, PADN])
                layer_norm(nc, "ln2", c, x_res, xn, xnT, xtab)
            with Stage(nc, "l2b") as M:
                agg = M.sb("agg", [P, NT, D])
                convolve(nc, c, a, agg, table1, xtab, bins1)
                aggT = M.sb("aggT", [P, 2, PADN])
                turn_rows(nc, "turn", c, agg, aggT)
                update(nc, c, a, aggT, xn, x_res)
        with Stage(nc, "l3") as L:
            xn, xnT = L.sb("xn", [P, NT, D]), L.sb("xnT", [P, 2, PADN])
            layer_norm(nc, "ln3", c, x_res, xn, xnT, xtab2)
            routed(nc, c, a, xnT, x_res, xtab2, slots, results)
        store(nc, x_res, out)


def kernel(**inputs):
    import numpy as np
    import concourse.bacc as bacc
    from concourse.bass_utils import run_bass_kernel_spmd

    nc = bacc.Bacc("TRN2", target_bir_lowering=False, num_devices=1)
    arrays, a = {}, {}
    for name in inputs:
        array = np.ascontiguousarray(inputs[name])
        arrays[f"in_{name}"] = array
        a[name] = nc.dram_tensor(f"in_{name}", array.shape, mybir.dt.from_np(array.dtype), kind="ExternalInput").ap()
    out = nc.dram_tensor("out", (NODES, D), F32, kind="ExternalOutput").ap()
    graph_layers(nc, a, out)
    result = run_bass_kernel_spmd(nc, [arrays], core_ids=[0])
    return result.results[0]["out"]
```

```python
from contextlib import ExitStack

import concourse.bass as bass
from concourse import mybir

ALU = mybir.AluOpType
ACT = mybir.ActivationFunctionType
AX = mybir.AxisListType
F32 = mybir.dt.float32
BF16 = mybir.dt.bfloat16
I32 = mybir.dt.int32

P = 128
NODES, D = 3750, 256
NT = -(-NODES // P)
TAIL = NODES - (NT - 1) * P
PADN = NT * P
EDGES = 60000
EP, EJ = 125, 480
ET = 504
assert EP * EJ == EDGES and (EDGES + NT * (P - 1)) // P <= ET and ET % 8 == 0
K = 4
ET0 = 588
assert (EDGES + NT * (K * P - 1)) // (K * P) <= ET0 // K and ET0 % (3 * K) == 0
COLS0 = 80, 48, 352
COLS1 = 144, 16, 32, 32, 208, 48
assert sum(COLS0) == EJ == sum(COLS1) and COLS1[0] == 3 * (ET0 // K // 3 - 1)
RELS, HEADS, HD = 8, 4, 64
FW = D + HEADS
NG = 20
W0, W1 = 4, 24
EX0, EX1, HID = 4, 16, 512
MT = 76
assert (2 * NODES + EX1 * (P - 1)) // P <= MT
LN_EPS, BN_EPS, SLOPE = 1e-5, 1e-5, 0.2
BIG = float(2.0 ** 100)


class Stage:

    def __init__(self, nc, name):
        self.nc, self.name, self.ctx, self.sems, self.open = nc, name, ExitStack(), [], None

    def __enter__(self):
        self.ctx.__enter__()
        return self

    def __exit__(self, *error):
        if self.open is not None:
            self.open.__exit__(*error)
        if self.sems and error[0] is None:
            self.nc.clear_and_free_semaphores(self.sems)
            self.nc.all_engine_barrier()
        return self.ctx.__exit__(*error)

    def sb(self, name, shape, dt=F32):
        return self.ctx.enter_context(self.nc.sbuf_tensor(f"{self.name}_{name}", shape, dt))

    def ps(self, name, shape, dt=F32):
        return self.ctx.enter_context(self.nc.psum_tensor(f"{self.name}_{name}", shape, dt))

    def sem(self, name):
        self.sems.append(self.nc.alloc_semaphore(name=f"{self.name}_{name}"))
        return self.sems[-1]

    def block(self):
        self.open = self.nc.Block()
        return self.open.__enter__()


class Chain:

    def __init__(self, eng, sem):
        self.eng, self.sem, self.n = eng, sem, 0

    def __call__(self, ins):
        self.n += 1
        ins.then_inc(self.sem, 1)
        self.eng.wait_ge(self.sem, self.n)


def bcast(ap, dims):
    return bass.AP(ap.tensor, ap.offset, [list(ap.ap[0])] + [list(d) for d in dims])


def rows(vec, n=P):
    return bass.AP(vec.tensor, vec.offset, [[0, n]] + [list(d) for d in vec.ap])


class Steps:

    def __init__(self, eng, sem, start):
        self.eng, self.sem, self.start, self.n = eng, sem, start, 0

    def __call__(self, ins):
        self.n += 1
        ins.then_inc(self.sem, 1)
        return self.n

    def wait(self, n=None):
        wait_positive(self.eng, self.sem, self.start + (self.n if n is None else n))


def wait_positive(eng, sem, n):
    if not isinstance(n, int) or n > 0:
        eng.wait_ge(sem, n)


def flat(ap, pattern="p a b -> p (a b)"):
    return ap.rearrange(pattern)


def constants(nc, c, x_in, x_res):
    with Stage(nc, "const") as s:
        loaded, made, dv = s.sem("loaded"), s.sem("made"), s.sem("dv")
        ramp_i = s.sb("ramp_i", [P, 512], I32)
        block = s.block()

        @block.sync
        def _(sp):
            sp.wait_ge(made, 1)
            sp.dma_start(x_res[:, 0:NT - 1, :], x_in[0:(NT - 1) * P, :].rearrange("(t p) d -> p t d", p=P)).then_inc(loaded, 16)
            sp.dma_start(x_res[0:TAIL, NT - 1, :], x_in[(NT - 1) * P:NODES, :]).then_inc(loaded, 16)
            sp.wait_ge(loaded, 32)

        @block.gpsimd
        def _(pool):
            nc.gpsimd.memset(x_res[:, NT - 1, :], 0.0).then_inc(made, 1)
            nc.gpsimd.iota(ramp_i[:, :], pattern=[[1, 512]], base=0, channel_multiplier=0).then_inc(made, 1)
            nc.gpsimd.memset(c["ident"][:, :], 0.0).then_inc(made, 1)
            nc.gpsimd.memset(c["before"][:, :], 1.0).then_inc(made, 1)
            nc.gpsimd.memset(c["upto"][:, :], 1.0).then_inc(made, 1)
            nc.gpsimd.memset(c["beyond"][:, :], 1.0).then_inc(made, 1)
            pool.wait_ge(made, 6)
            nc.gpsimd.affine_select(out=c["ident"][:, :], in_=c["ident"][:, :], compare_op=ALU.not_equal, fill=1.0,
                                    base=0, pattern=[[-1, P]], channel_multiplier=1).then_inc(made, 1)
            nc.gpsimd.affine_select(out=c["before"][:, :], in_=c["before"][:, :], compare_op=ALU.is_gt, fill=0.0,
                                    base=0, pattern=[[1, P]], channel_multiplier=-1).then_inc(made, 1)
            nc.gpsimd.affine_select(out=c["beyond"][:, :], in_=c["beyond"][:, :], compare_op=ALU.is_ge, fill=0.0,
                                    base=-TAIL, pattern=[[0, 1]], channel_multiplier=1).then_inc(made, 1)
            nc.gpsimd.affine_select(out=c["upto"][:, :], in_=c["upto"][:, :], compare_op=ALU.is_ge, fill=0.0,
                                    base=0, pattern=[[1, P]], channel_multiplier=-1).then_inc(made, 1)

        @block.vector
        def _(dve):
            nc.vector.memset(c["ones"][:, :], 1.0).then_inc(dv, 1)
            nc.vector.memset(c["ln_eps"][:, :], LN_EPS).then_inc(dv, 1)
            nc.vector.memset(c["bn_eps"][:, :], BN_EPS).then_inc(dv, 1)
            nc.vector.memset(c["minus_big"][:, :], -BIG).then_inc(dv, 1)
            dve.wait_ge(made, 10)
            nc.vector.tensor_copy(c["ramp"][:, :], ramp_i[:, :]).then_inc(dv, 1)
            nc.vector.tensor_copy(c["identb"][:, :], c["ident"][:, :]).then_inc(dv, 1)


def positions(nc, name, c, n_part, n_free, bins, tiles, bin_f, pos_f, addr_i, tile_bin, group=1, side=None):
    SIZE = group * P
    shift = SIZE.bit_length() - 1
    n = n_free
    with Stage(nc, name) as s:
        mask = s.sb("mask", [P, bins, n], BF16)
        run = s.sb("run", [P, bins, n])
        cnt, pre, base = s.sb("cnt", [P, bins]), s.sb("pre", [P, bins]), s.sb("base", [P, bins])
        padded_i, padded, end = s.sb("padded_i", [bins, 1], I32), s.sb("padded", [bins, 1]), s.sb("end", [bins, 1])
        reached = s.sb("reached", [bins, 512])
        tb = s.sb("tb", [1, 512])
        pos_i, lane, col = s.sb("pos_i", [P, n], I32), s.sb("lane", [P, n], I32), s.sb("col", [P, n], I32)
        pp = s.ps("pp", [P, 4, 512])
        dv, pe_s = s.sem("dv"), s.sem("pe")
        counted, rounded, compared = s.sem("counted"), s.sem("rounded"), s.sem("compared")
        send = side(s) if side else None
        block = s.block()
        q = slice(0, n_part)
        lt = c["before"]

        if send is not None:
            @block.gpsimd
            def _(pool):
                send(pool)

        @block.tensor
        def _(pe):
            pe.wait_ge(counted, 1)
            nc.tensor.matmul(pp[0:bins, 0, 0:1], cnt[q, :], c["ones"][q, 0:1], start=True, stop=True).then_inc(pe_s, 1)
            pe.wait_ge(rounded, 1)
            nc.tensor.matmul(pp[0:bins, 1, 0:1], c["upto"][0:bins, 0:bins], padded[:, :], start=True, stop=True).then_inc(pe_s, 1)
            nc.tensor.matmul(pp[:, 2, 0:bins], lt[q, :], cnt[q, :], start=True, stop=False)
            nc.tensor.matmul(pp[:, 2, 0:bins], padded[:, 0:1].broadcast_to([bins, P]), lt[0:bins, 0:bins],
                             start=False, stop=True).then_inc(pe_s, 1)
            pe.wait_ge(compared, 1)
            nc.tensor.matmul(pp[0:1, 3, :], c["ones"][0:bins, 0:1], reached[:, :], start=True, stop=True).then_inc(pe_s, 1)

        @block.vector
        def _(dve):
            do = Chain(dve, dv)
            v = nc.vector
            do(v.tensor_tensor(mask[q, :, :], bcast(bin_f, [[0, bins], list(bin_f.ap[1])]),
                               bcast(c["ramp"][q, :], [[1, bins], [0, n]]), ALU.is_equal))
            v.tensor_reduce(cnt[q, :], mask[q, :, :], AX.X, ALU.add).then_inc(counted, 1)
            m2, r2 = flat(mask[q, :, :]), flat(run[q, :, :])
            do(v.tensor_tensor_scan(r2, m2, m2, 0.0, ALU.add, ALU.max))
            dve.wait_ge(counted, 1)
            do(v.tensor_tensor_scan(pre[q, :], cnt[q, :], cnt[q, :], 0.0, ALU.add, ALU.max))
            do(v.tensor_tensor(pre[q, :], cnt[q, :], pre[q, :], ALU.subtract))
            dve.wait_ge(pe_s, 1)
            do(v.tensor_scalar(padded_i[:, :], pp[0:bins, 0, 0:1], float(SIZE - 1), None, ALU.add))
            do(v.tensor_scalar(padded_i[:, :], padded_i[:, :], shift, shift, ALU.logical_shift_right, ALU.logical_shift_left))
            v.tensor_copy(padded[:, :], padded_i[:, :]).then_inc(rounded, 1)
            dve.wait_ge(pe_s, 2)
            do(v.tensor_scalar(end[:, :], pp[0:bins, 1, 0:1], 1.0 / SIZE, None, ALU.mult))
            v.tensor_scalar(reached[:, :], c["ramp"][0:bins, :], end[:, 0:1], None, ALU.is_ge).then_inc(compared, 1)
            dve.wait_ge(pe_s, 3)
            do(v.scalar_tensor_tensor(out=base[q, :], in0=pre[q, :], scalar=-1.0, in1=pp[q, 2, 0:bins], op0=ALU.add, op1=ALU.add))
            do(v.tensor_tensor(run[q, :, :], run[q, :, :], base[q, :].unsqueeze(2).broadcast_to([n_part, bins, n]), ALU.add))
            do(v.tensor_tensor(run[q, :, :], run[q, :, :], mask[q, :, :], ALU.mult))
            do(v.tensor_reduce(pos_f, run[q, :, :].rearrange("p b n -> p n b"), AX.X, ALU.add))
            do(v.tensor_copy(pos_i[q, :], pos_f))
            do(v.tensor_scalar(lane[q, :], pos_i[q, :], P - 1, None, ALU.bitwise_and))
            do(v.tensor_scalar(col[q, :], pos_i[q, :], 7, None, ALU.logical_shift_right))
            do(v.scalar_tensor_tensor(out=addr_i, in0=lane[q, :], scalar=float(tiles), in1=col[q, :], op0=ALU.mult, op1=ALU.add))
            dve.wait_ge(pe_s, 4)
            do(v.tensor_scalar(tb[:, :], pp[0:1, 3, :], float(bins - 1), None, ALU.min))
            do(v.tensor_copy(tile_bin[:, :], tb[:, :]))


class Sender:

    def __init__(self, nc, s, table, recs, addrs, width, first, columns, chunk=8):
        self.nc, self.table, self.recs, self.addrs = nc, table, recs, addrs
        self.first, self.chunk, self.pairs = first, chunk, columns // chunk // 2
        assert self.pairs * 2 * chunk == columns
        self.send = [s.sb(f"send{u}", [P, chunk, width]) for u in range(2)]
        self.slot = [s.sb(f"slot{u}", [P, chunk], I32) for u in range(2)]
        self.staged = s.sem("staged")
        self.sent = [s.sem(f"sent{u}") for u in range(2)]

    def __call__(self, pool):
        nc, chunk = self.nc, self.chunk

        def send(i, u):
            at = bass.ds((i * 2 + u) * chunk + self.first, chunk)
            wait_positive(pool, self.sent[u], i * (16 * chunk))
            nc.gpsimd.tensor_copy(self.slot[u][0:EP, :], self.addrs[0:EP, at]).then_inc(self.staged, 1)
            nc.gpsimd.tensor_copy(self.send[u][0:EP, :, :], self.recs[0:EP, at, :]).then_inc(self.staged, 1)
            pool.wait_ge(self.staged, (i * 2 + u) * 2 + 2)
            pool.nop(nofuse=True)
            for k in range(chunk):
                nc.gpsimd.indirect_dma_start(
                    out=self.table, out_offset=bass.IndirectOffsetOnAxis(ap=self.slot[u][0:EP, k:k + 1], axis=0),
                    in_=self.send[u][0:EP, k, :], in_offset=None).then_inc(self.sent[u], 16)

        for u in range(2):
            send(0, u)
        if self.pairs > 1:
            with pool.Fori(1, self.pairs) as i:
                for u in range(2):
                    send(i, u)
        for u in range(2):
            pool.wait_ge(self.sent[u], 16 * chunk * self.pairs)


def layer_norm(nc, name, c, x_res, xnT, table=None, add=False, side=None):
    SL = 5
    assert NT % SL == 0
    with Stage(nc, name) as s:
        st = s.sb("st", [P, NT, 6])
        mean, var, t0, rstd, shift = (s.sb(k, [P, NT]) for k in ("mean", "var", "t0", "rstd", "shift"))
        row = [s.sb(f"row{u}", [P, D]) for u in range(SL)]
        pst = [s.ps(f"turned{u}", [P, 2, P]) for u in range(SL)]
        dv, seen, var_ready, std_ready = s.sem("dv"), s.sem("seen"), s.sem("var_ready"), s.sem("std_ready")
        row_ready, turned, copied, added = s.sem("row_ready"), s.sem("turned_done"), s.sem("copied"), s.sem("added")
        stored = [s.sem(f"stored{u}") for u in range(SL)]
        send = side(s) if side else None
        block = s.block()

        def tiles(eng, step):
            for u in range(SL):
                step(u, 0, u)
            with eng.Fori(1, NT // SL) as i:
                for u in range(SL):
                    step(i * SL + u, i, u)

        @block.vector
        def _(dve):
            v = nc.vector
            with dve.Fori(0, NT) as t:
                v.bn_stats(flat(st[:, bass.ds(t, 1), :]), flat(x_res[:, bass.ds(t, 1), :])).then_inc(seen, 1)
            dve.wait_ge(seen, NT)
            do = Chain(dve, dv)
            do(v.tensor_tensor(mean[:, :], st[:, :, 1], st[:, :, 4], ALU.add))
            do(v.tensor_tensor(t0[:, :], st[:, :, 1], st[:, :, 4], ALU.subtract))
            do(v.tensor_scalar(mean[:, :], mean[:, :], 0.5, None, ALU.mult))
            do(v.scalar_tensor_tensor(out=t0[:, :], in0=t0[:, :], scalar=0.25, in1=t0[:, :], op0=ALU.mult, op1=ALU.mult))
            do(v.tensor_tensor(var[:, :], st[:, :, 2], st[:, :, 5], ALU.add))
            v.scalar_tensor_tensor(out=var[:, :], in0=var[:, :], scalar=1.0 / D, in1=t0[:, :], op0=ALU.mult,
                                   op1=ALU.add).then_inc(var_ready, 1)
            dve.wait_ge(std_ready, 1)
            do(v.reciprocal(rstd[:, :], t0[:, :]))
            do(v.scalar_tensor_tensor(out=shift[:, :], in0=mean[:, :], scalar=-1.0, in1=rstd[:, :], op0=ALU.mult, op1=ALU.mult))

            def normalise(t, i, u):
                wait_positive(dve, turned, t - SL + 1)
                if table is not None:
                    wait_positive(dve, stored[u], i * 16)
                if add:
                    wait_positive(dve, added, t - SL + 1)
                x = flat(x_res[:, bass.ds(t, 1), :])
                v.tensor_scalar(row[u][:, :], x, rstd[:, bass.ds(t, 1)], shift[:, bass.ds(t, 1)], ALU.mult, ALU.add).then_inc(row_ready, 1)
                if add:
                    dve.wait_ge(row_ready, t + 1)
                    v.tensor_tensor(x, x, row[u][:, :], ALU.add).then_inc(added, 1)

            tiles(dve, normalise)

        @block.scalar
        def _(act):
            act.wait_ge(var_ready, 1)
            nc.scalar.activation(t0[:, :], var[:, :], ACT.Sqrt, bias=c["ln_eps"][:, 0:1]).then_inc(std_ready, 1)

            def keep(t, i, u):
                act.wait_ge(turned, t + 1)
                nc.scalar.activation(xnT[:, :, bass.ds(t * P, P)], pst[u][:, :, :], ACT.Copy).then_inc(copied, 1)

            tiles(act, keep)

        @block.tensor
        def _(pe):
            def turn(t, i, u):
                pe.wait_ge(row_ready, t + 1)
                wait_positive(pe, copied, t - SL + 1)
                for h in range(2):
                    ins = nc.tensor.transpose(pst[u][:, h, :], row[u][:, h * P:(h + 1) * P], c["ident"][:, :])
                ins.then_inc(turned, 1)

            tiles(pe, turn)

        if send is not None:
            @block.gpsimd
            def _(pool):
                send(pool)

        if table is not None:
            @block.sync
            def _(sp):
                view = table.rearrange("(t p) d -> t p d", p=P)

                def store(t, i, u):
                    sp.wait_ge(row_ready, t + 1)
                    sp.nop(nofuse=True)
                    sp.dma_start(view[bass.ds(t, 1)].rearrange("o p d -> (o p) d"), row[u][:, :]).then_inc(stored[u], 16)

                tiles(sp, store)
                for u in range(SL):
                    sp.wait_ge(stored[u], 16 * (NT // SL))


def edge_records(nc, c, a, rec0, rec1, pos_f, addr0, addr1, bins0, bins1, table0, table1):
    q = slice(0, EP)
    with Stage(nc, "keys") as k:
        binf0, binf1 = k.sb("binf0", [P, EJ]), k.sb("binf1", [P, EJ])
        with Stage(nc, "split") as s:
            src, dst, typ = (s.sb(n, [P, EJ], I32) for n in ("src", "dst", "typ"))
            part = s.sb("part", [P, EJ], I32)
            srcf, typf = s.sb("srcf", [P, EJ]), s.sb("typf", [P, EJ])
            attr = s.sb("attr", [P, EJ, NG])
            empty0, empty1 = s.sb("empty0", [P, ET0, W0]), s.sb("empty1", [P, ET // 8, W1])
            attr_loaded, attr_kept = s.sem("attr_loaded"), s.sem("attr_kept")
            loaded, dv, cleared, filled = s.sem("loaded"), s.sem("dv"), s.sem("cleared"), s.sem("filled")
            block = s.block()

            @block.sync
            def _(sp):
                for t, name in ((src, "src"), (dst, "dst"), (typ, "edge_type_8")):
                    sp.dma_start(t[q, :], a[name].rearrange("(p j) -> p j", p=EP)).then_inc(loaded, 16)
                sp.dma_start(attr[q, :, :], a["edge_attr_20"].rearrange("(p j) g -> p j g", p=EP)).then_inc(attr_loaded, 16)
                sp.wait_ge(cleared, 6)
                sp.dma_start(table0.rearrange("(p t) w -> p t w", p=P), empty0[:, :, :]).then_inc(filled, 16)
                for i in range(8):
                    sp.dma_start(table1.rearrange("(p i t) w -> p i t w", p=P, i=8)[:, i], empty1[:, :, :]).then_inc(filled, 16)
                sp.wait_ge(filled, 9 * 16)

            @block.gpsimd
            def _(pool):
                nc.gpsimd.memset(empty0[:, :, :], 0.0).then_inc(cleared, 1)
                nc.gpsimd.memset(empty1[:, :, :], 0.0).then_inc(cleared, 1)
                pool.wait_ge(cleared, 2)
                nc.gpsimd.memset(empty0[:, :, 0:1], float(NODES)).then_inc(cleared, 1)
                nc.gpsimd.memset(empty0[:, :, 1:2], -1.0).then_inc(cleared, 1)
                nc.gpsimd.memset(empty1[:, :, NG + 1:NG + 2], -1.0).then_inc(cleared, 1)
                nc.gpsimd.memset(rec1[q, :, NG + 2:W1], 0.0).then_inc(cleared, 1)

            @block.scalar
            def _(act):
                act.wait_ge(attr_loaded, 16)
                nc.scalar.activation(rec1[q, :, 0:NG], attr[q, :, :], ACT.Copy).then_inc(attr_kept, 1)

            @block.vector
            def _(dve):
                v, do = nc.vector, Chain(dve, dv)
                dve.wait_ge(loaded, 48)
                v.tensor_copy(srcf[q, :], src[q, :])
                v.tensor_copy(rec1[q, :, NG], dst[q, :])
                v.tensor_copy(rec0[q, :, 2], typ[q, :])
                do(v.tensor_copy(typf[q, :], typ[q, :]))
                v.memset(rec0[q, :, 3], 0.0)
                do(v.scalar_tensor_tensor(out=rec0[q, :, 0], in0=typf[q, :], scalar=float(PADN), in1=srcf[q, :],
                                          op0=ALU.mult, op1=ALU.add))
                for key, local, binf in ((dst, rec0[q, :, 1], binf0), (src, rec1[q, :, NG + 1], binf1)):
                    do(v.tensor_scalar(part[q, :], key[q, :], P - 1, None, ALU.bitwise_and))
                    do(v.tensor_copy(local, part[q, :]))
                    do(v.tensor_scalar(part[q, :], key[q, :], 7, None, ALU.logical_shift_right))
                    do(v.tensor_copy(binf[q, :], part[q, :]))

        positions(nc, "by_dst", c, EP, EJ, NT, ET0, binf0[q, :], pos_f[q, :], addr0[q, :], bins0, group=K)
        positions(nc, "by_src", c, EP, EJ, NT, ET, binf1[q, :], pos_f[q, :], addr1[q, :], bins1,
                  side=lambda s: Sender(nc, s, table0, rec0, addr0, W0, 0, COLS0[0]))


def project(nc, c, a, xnT, er, feat, rec0, addr0, table0):
    with Stage(nc, "proj") as s:
        w = s.sb("w", [P, 2, RELS, FW])
        wr = s.sb("wr", [P, 2, RELS * HEADS])
        al, ar = s.sb("al", [P, RELS, D]), s.sb("ar", [P, RELS, D])
        prod = s.sb("prod", [P, RELS * D])
        out = [s.sb(f"out{u}", [P, RELS, FW]) for u in range(2)]
        xs = [s.sb(f"xs{u}", [P, 2, P]) for u in range(2)]
        ps = [s.ps(f"ps{r}", [P, 512]) for r in range(7)]
        pe_er = s.ps("er", [P, 512])
        wl, al_l = s.sem("w_loaded"), s.sem("a_loaded")
        dv, xs_ready = s.sem("dv"), s.sem("xs_ready")
        mm, er_done, ev_a, ev_v = s.sem("multiplied"), s.sem("er_done"), s.sem("moved_act"), s.sem("moved_dve")
        stored = [s.sem(f"stored{u}") for u in range(2)]
        send = Sender(nc, s, table0, rec0, addr0, W0, COLS0[0] + COLS0[1], COLS0[2])
        block = s.block()
        ON_ACT = 5
        MOVES_V = RELS - ON_ACT + 1

        @block.sync
        def _(sp):
            cw = a["L0_gnn_conv_weights"].rearrange("r h (c p) d -> c p r h d", p=P)
            for k in range(2):
                for r in range(RELS):
                    sp.dma_start(w[:, k, r, 0:D].rearrange("p (h d) -> p h d", h=HEADS), cw[k, :, r]).then_inc(wl, 16)
            for t, name in ((al, "L0_gnn_attn_l"), (ar, "L0_gnn_attn_r")):
                sp.dma_start(flat(t[:, :, :]), rows(a[name].rearrange("r h d -> (r h d)"))).then_inc(al_l, 16)
            fv = feat.rearrange("(r t p) f -> t p r f", r=RELS, p=P)
            with sp.Fori(0, NT // 2) as i:
                for u in range(2):
                    sp.wait_ge(ev_a, (i * 2 + u + 1) * ON_ACT)
                    sp.nop(nofuse=True)
                    sp.wait_ge(ev_v, (i * 2 + u + 1) * MOVES_V)
                    sp.nop(nofuse=True)
                    sp.dma_start(fv[bass.ds(i * 2 + u, 1)].rearrange("a p r f -> (a p) r f"), out[u][:, :, :]).then_inc(stored[u], 16)
            for u in range(2):
                sp.wait_ge(stored[u], 16 * (NT // 2))

        @block.vector
        def _(dve):
            v, do = nc.vector, Chain(dve, dv)
            dve.wait_ge(wl, 16 * 2 * RELS)
            dve.wait_ge(al_l, 32)
            for k in range(2):
                for vec, dest in ((al, w[:, k, :, D:FW]), (ar, wr[:, k, :].rearrange("p (r h) -> p r h", r=RELS))):
                    do(v.tensor_tensor(prod[:, :].rearrange("p (r f) -> p r f", r=RELS), w[:, k, :, 0:D], vec[:, :, :], ALU.mult))
                    do(v.tensor_reduce(dest, prod[:, :].rearrange("p (r h d) -> p r h d", r=RELS, h=HEADS), AX.X, ALU.add))
            with dve.Fori(0, NT // 2) as i:
                for u in range(2):
                    t = i * 2 + u
                    dve.wait_ge(stored[u], i * 16)
                    for r in range(ON_ACT, RELS):
                        dve.wait_ge(mm, t * RELS + r + 1)
                        v.tensor_copy(out[u][:, r, :], ps[r % 7][:, 0:FW]).then_inc(ev_v, 1)
                    dve.wait_ge(er_done, t + 1)
                    v.tensor_copy(flat(er[:, bass.ds(t, 1), :]), pe_er[:, 0:RELS * HEADS]).then_inc(ev_v, 1)

        @block.scalar
        def _(act):
            def take(t, u):
                nc.scalar.activation(xs[u][:, :, :], xnT[:, :, bass.ds(t * P, P)], ACT.Copy).then_inc(xs_ready, 1)

            def tile(t, u, i, last=False):
                if not last:
                    act.wait_ge(er_done, t)
                    take(t + 1, 1 - u)
                act.wait_ge(stored[u], i * 16)
                for r in range(ON_ACT):
                    act.wait_ge(mm, t * RELS + r + 1)
                    nc.scalar.activation(out[u][:, r, :], ps[r][:, 0:FW], ACT.Copy).then_inc(ev_a, 1)

            take(0, 0)
            with act.Fori(0, NT // 2 - 1) as i:
                tile(i * 2, 0, i)
                tile(i * 2 + 1, 1, i)
            tile(NT - 2, 0, NT // 2 - 1)
            tile(NT - 1, 1, NT // 2 - 1, last=True)

        @block.tensor
        def _(pe):
            def tile(t, u, first=False):
                pe.wait_ge(xs_ready, t + 1)
                for r in range(RELS):
                    if r == RELS - 1:
                        pe.wait_ge(ev_a, t * ON_ACT + 1)
                    elif not first and r == 0:
                        pe.wait_ge(ev_v, (t - 1) * MOVES_V + RELS - ON_ACT)
                    elif not first and r < ON_ACT:
                        pe.wait_ge(ev_a, (t - 1) * ON_ACT + r + 1)
                    elif not first:
                        pe.wait_ge(ev_v, (t - 1) * MOVES_V + r - ON_ACT + 1)
                    for k in range(2):
                        ins = nc.tensor.matmul(ps[r % 7][:, 0:FW], xs[u][:, k, :], w[:, k, r, :], start=(k == 0), stop=(k == 1))
                    ins.then_inc(mm, 1)
                if not first:
                    pe.wait_ge(ev_v, t * MOVES_V)
                for k in range(2):
                    ins = nc.tensor.matmul(pe_er[:, 0:RELS * HEADS], xs[u][:, k, :], wr[:, k, :], start=(k == 0), stop=(k == 1))
                ins.then_inc(er_done, 1)

            pe.wait_ge(dv, 8)
            tile(0, 0, first=True)
            tile(1, 1)
            with pe.Fori(1, NT // 2) as i:
                tile(i * 2, 0)
                tile(i * 2 + 1, 1)

        @block.gpsimd
        def _(pool):
            send(pool)


def attend(nc, c, er, acc, rec1, addr1, table0, table1, feat, bins0):
    GROUPS, SLOTS = ET0 // K, 3
    H1 = HD + 1
    F_OPS = 3
    N_DV = (1, 5, K + 3, HEADS - 1)
    three = range(SLOTS)
    with Stage(nc, "att") as s:
        recs = s.sb("recs", [P, ET0, W0])
        rowidx = s.sb("rowidx", [P, ET0], I32)
        idx = [s.sb(f"idx{u}", [P, K], I32) for u in three]
        got = [s.sb(f"got{u}", [P, K, FW]) for u in three]
        oh = [s.sb(f"onehot{u}", [P, K, P]) for u in three]
        ohT = [s.sb(f"onehotT{u}", [P, K, P]) for u in three]
        away = [s.sb(f"away{u}", [P, K, P], BF16) for u in three]
        typ = [s.sb(f"typ{u}", [P, K, RELS]) for u in three]
        e = [s.sb(f"e{u}", [P, K, HEADS]) for u in three]
        ehi = [s.sb(f"ehi{u}", [P, K, HEADS], BF16) for u in three]
        elo = [s.sb(f"elo{u}", [P, K, HEADS], BF16) for u in three]
        keep = [s.sb(f"keep{u}", [P, HEADS]) for u in three]
        f = [s.sb(f"f{u}", [P, K, HEADS, H1]) for u in three]
        ert = s.sb("ert", [P, K, HEADS, RELS])
        ers, z = s.sb("ers", [P, K, HEADS]), s.sb("z", [P, K, HEADS])
        tmax = s.sb("tmax", [P, K + 1, HEADS])
        mrun = s.sb("mrun", [P, NT, HEADS])
        mnew, drop = s.sb("mnew", [P, HEADS]), s.sb("drop", [P, HEADS])
        below, ex = s.sb("below", [P, K, HEADS]), s.sb("ex", [P, K, HEADS])
        send, slot = s.sb("send", [P, 3, W1]), s.sb("slot", [P, 3], I32)
        pmax = [s.ps(f"pmax{k}", [P, HEADS, P]) for k in range(K)]
        pT = s.ps("pT", [P, K, P])
        per = s.ps("per", [P, K, P])
        pme = s.ps("pme", [P, K, P])
        psum = s.ps("psum", [P, 512])

        loaded, prep, dv, idx_ready = s.sem("loaded"), s.sem("prep"), s.sem("dv"), s.sem("idx_ready")
        got_s = [s.sem(f"got_s{u}") for u in three]
        oh_ready, turned, ohT_ready, away_ready = (s.sem(n) for n in ("oh_ready", "turned", "ohT_ready", "away_ready"))
        er_ready, e_ready, max_ready, drop_ready = (s.sem(n) for n in ("er_ready", "e_ready", "max_ready", "drop_ready"))
        me_ready, keep_ready, below_ready, ex_ready = (s.sem(n) for n in ("me_ready", "keep_ready", "below_ready", "ex_ready"))
        f_ready, sum_ready, acc_done = s.sem("f_ready"), s.sem("sum_ready"), s.sem("acc_done")
        staged, sent = s.sem("staged"), s.sem("sent")
        block = s.block()

        def counted(t):
            if isinstance(t, int):
                return sum(n * min(max(t - d, 0), GROUPS) for d, n in enumerate(N_DV))
            return t * sum(N_DV) - sum(n * d for d, n in enumerate(N_DV))

        def in_steps(eng, step):
            def peeled(t):
                step(t, t // 3, t % 3, {d for d in range(4) if 0 <= t - d < GROUPS})
            for t in range(6):
                peeled(t)
            with eng.Fori(2, GROUPS // 3) as i:
                for u in three:
                    step(i * 3 + u, i, u, {0, 1, 2, 3})
            for t in range(GROUPS, GROUPS + 3):
                peeled(t)

        @block.sync
        def _(sp):
            sp.dma_start(recs[:, :, :], table0.rearrange("(p t) w -> p t w", p=P)).then_inc(loaded, 16)
            sp.wait_ge(loaded, 16)

        @block.gpsimd
        def _(pool):
            def gathers(g, u, first=False):
                if not first:
                    pool.wait_ge(f_ready, (g - 2) * F_OPS)
                nc.gpsimd.tensor_copy(idx[u][:, :], rowidx[:, bass.ds(g * K, K)]).then_inc(idx_ready, 1)
                pool.wait_ge(idx_ready, g + 1)
                pool.nop(nofuse=True)
                for k in range(K):
                    nc.gpsimd.indirect_dma_start(
                        out=got[u][:, k, :], out_offset=None, in_=feat,
                        in_offset=bass.IndirectOffsetOnAxis(ap=idx[u][:, k:k + 1], axis=0)).then_inc(got_s[u], 16)

            def stage(i):
                at = bass.ds(i * 3 - 3, 3)
                wait_positive(pool, sent, i * 48 - 48)
                nc.gpsimd.tensor_copy(slot[0:EP, :], addr1[0:EP, at]).then_inc(staged, 1)
                nc.gpsimd.tensor_copy(send[0:EP, :, :], rec1[0:EP, at, :]).then_inc(staged, 1)
                pool.wait_ge(staged, i * 2)
                pool.nop(nofuse=True)

            def scatter(u):
                nc.gpsimd.indirect_dma_start(
                    out=table1, out_offset=bass.IndirectOffsetOnAxis(ap=slot[0:EP, u:u + 1], axis=0),
                    in_=send[0:EP, u, :], in_offset=None).then_inc(sent, 16)

            def round_(i):
                stage(i)
                for u in three:
                    gathers(i * 3 + u, u)
                    scatter(u)

            pool.wait_ge(prep, 3)
            for u in three:
                gathers(u, u, first=True)
            round_(1)
            with pool.Fori(2, GROUPS // 3) as i:
                round_(i)
            pool.wait_ge(sent, 16 * COLS1[0])

        @block.vector
        def _(dve):
            v = nc.vector
            v.memset(acc[:, :, :, :], 0.0).then_inc(prep, 1)
            v.memset(mrun[:, :, :], -BIG).then_inc(prep, 1)
            dve.wait_ge(loaded, 16)
            v.tensor_copy(rowidx[:, :], recs[:, :, 0]).then_inc(prep, 1)
            dve.wait_ge(prep, 3)

            def step(t, i, u, parts):
                s1, s2 = (u - 1) % 3, (u - 2) % 3
                count = Steps(dve, dv, counted(t))
                if 2 in parts:
                    g = t - 2
                    bin2 = dve.value_load(bins0[0:1, bass.ds(g, 1)], min_val=0, max_val=NT - 1)
                if 3 in parts:
                    bin3 = dve.value_load(bins0[0:1, bass.ds(t - 3, 1)], min_val=0, max_val=NT - 1)
                if 2 in parts:
                    m = flat(mrun[:, bass.ds(bin2, 1), :])
                    count.wait()
                    count(v.tensor_scalar(tmax[:, K, :], m, 0.0, None, ALU.add))
                    for k in range(K):
                        dve.wait_ge(max_ready, g * K + k + 1)
                        count(v.tensor_reduce(tmax[:, k, :], pmax[k][:, :, :], AX.X, ALU.max))
                    wait_positive(dve, keep_ready, g)
                    wait_positive(dve, me_ready, g)
                    count.wait()
                    count(v.tensor_reduce(mnew[:, :], tmax[:, :, :].rearrange("p k h -> p h k"), AX.X, ALU.max))
                    count.wait()
                    v.tensor_tensor(drop[:, :], tmax[:, K, :], mnew[:, :], ALU.subtract).then_inc(drop_ready, 1)
                    count(v.tensor_scalar(m, mnew[:, :], 0.0, None, ALU.add))
                if 1 in parts:
                    dve.wait_ge(er_ready, t)
                    count.wait()
                    count(v.tensor_tensor(ert[:, :, :, :], per[:, :, 0:RELS * HEADS].rearrange("p k (r h) -> p k h r", r=RELS),
                                          typ[s1][:, :, :].unsqueeze(2).broadcast_to([P, K, HEADS, RELS]), ALU.mult))
                    count.wait()
                    count(v.tensor_reduce(ers[:, :, :], ert[:, :, :, :], AX.X, ALU.add))
                    dve.wait_ge(got_s[s1], ((i + 1) if u else i) * 16 * K)
                    wait_positive(dve, below_ready, t - 3)
                    count.wait()
                    count(v.tensor_tensor(z[:, :, :], ers[:, :, :], got[s1][:, :, D:FW], ALU.add))
                    count.wait()
                    count(v.scalar_tensor_tensor(out=e[s1][:, :, :], in0=z[:, :, :], scalar=SLOPE, in1=z[:, :, :], op0=ALU.mult, op1=ALU.max))
                    count.wait()
                    count(v.tensor_copy(ehi[s1][:, :, :], e[s1][:, :, :]))
                    count.wait()
                    v.tensor_tensor(elo[s1][:, :, :], e[s1][:, :, :], ehi[s1][:, :, :], ALU.subtract).then_inc(e_ready, 1)
                if 0 in parts:
                    wait_positive(dve, sum_ready, t - 2)
                    wait_positive(dve, away_ready, t - 2)
                    dest = recs[:, bass.ds(t * K, K), 1]
                    kind = recs[:, bass.ds(t * K, K), 2]
                    v.tensor_tensor(oh[u][:, :, :], bcast(c["ramp"][:, 0:P], [[0, K], [1, P]]),
                                    dest.unsqueeze(2).broadcast_to([P, K, P]), ALU.is_equal).then_inc(oh_ready, 1)
                    count(v.tensor_tensor(typ[u][:, :, :], bcast(c["ramp"][:, 0:RELS], [[0, K], [1, RELS]]),
                                          kind.unsqueeze(2).broadcast_to([P, K, RELS]), ALU.is_equal))
                if 2 in parts:
                    dve.wait_ge(me_ready, g + 1)
                    wait_positive(dve, ex_ready, g)
                    v.tensor_tensor(below[:, :, :], e[s2][:, :, :], pme[:, :, 0:HEADS], ALU.subtract).then_inc(below_ready, 1)
                if 3 in parts:
                    dve.wait_ge(keep_ready, t - 2)
                    dve.wait_ge(sum_ready, t - 2)
                    wait_positive(dve, acc_done, t - 3)
                    count.wait()
                    for h in range(HEADS):
                        at = flat(acc[:, bass.ds(bin3, 1), h, :])
                        ins = v.scalar_tensor_tensor(out=at, in0=at, scalar=keep[u][:, h:h + 1], in1=psum[:, h * H1:(h + 1) * H1],
                                                     op0=ALU.mult, op1=ALU.add)
                        if h < HEADS - 1:
                            count(ins)
                    ins.then_inc(acc_done, 1)
                if 2 in parts:
                    dve.wait_ge(ex_ready, g + 1)
                    wait_positive(dve, sum_ready, g - 2)
                    v.tensor_copy(f[s2][:, :, :, HD], ex[:, :, :]).then_inc(f_ready, 1)
                    for k in (0, 2):
                        v.tensor_tensor(f[s2][:, k:k + 2, :, 0:HD], got[s2][:, k:k + 2, 0:D].rearrange("p k (h d) -> p k h d", h=HEADS),
                                        ex[:, k:k + 2, :].unsqueeze(3).broadcast_to([P, 2, HEADS, HD]), ALU.mult).then_inc(f_ready, 1)
                assert count.n == sum(N_DV[d] for d in parts)

            in_steps(dve, step)

        @block.scalar
        def _(act):
            def step(t, i, u, parts):
                s2 = (u - 2) % 3
                if 2 in parts:
                    g = t - 2
                    act.wait_ge(drop_ready, g + 1)
                    wait_positive(act, acc_done, g - 2)
                    nc.scalar.activation(keep[s2][:, :], drop[:, :], ACT.Exp).then_inc(keep_ready, 1)
                if 0 in parts:
                    act.wait_ge(oh_ready, t + 1)
                    wait_positive(act, max_ready, (t - 2) * K)
                    nc.scalar.activation(away[u][:, :, :], oh[u][:, :, :], ACT.Identity, bias=c["minus_big"][:, 0:1], scale=BIG).then_inc(away_ready, 1)
                if 2 in parts:
                    act.wait_ge(below_ready, g + 1)
                    wait_positive(act, f_ready, g * F_OPS)
                    nc.scalar.activation(ex[:, :, :], below[:, :, :], ACT.Exp).then_inc(ex_ready, 1)
                if 0 in parts:
                    act.wait_ge(turned, t + 1)
                    wait_positive(act, me_ready, t - 2)
                    nc.scalar.activation(ohT[u][:, :, :], pT[:, :, :], ACT.Copy).then_inc(ohT_ready, 1)

            in_steps(act, step)

        @block.tensor
        def _(pe):
            def step(t, i, u, parts):
                s1, s2 = (u - 1) % 3, (u - 2) % 3
                if 1 in parts:
                    bin1 = pe.value_load(bins0[0:1, bass.ds(t - 1, 1)], min_val=0, max_val=NT - 1)
                if 1 in parts:
                    pe.wait_ge(ohT_ready, t)
                    wait_positive(pe, e_ready, t - 1)
                    for k in range(K):
                        ins = nc.tensor.matmul(per[:, k, 0:RELS * HEADS], ohT[s1][:, k, :], flat(er[:, bass.ds(bin1, 1), :]), start=True, stop=True)
                    ins.then_inc(er_ready, 1)
                if 2 in parts:
                    pe.wait_ge(drop_ready, t - 1)
                    wait_positive(pe, below_ready, t - 2)
                    for k in range(K):
                        ins = nc.tensor.matmul(pme[:, k, 0:HEADS], ohT[s2][:, k, :], mnew[:, :], start=True, stop=True)
                    ins.then_inc(me_ready, 1)
                if 1 in parts:
                    pe.wait_ge(e_ready, t)
                    pe.wait_ge(away_ready, t)
                    for k in range(K):
                        nc.tensor.matmul(pmax[k][:, :, :], away[s1][:, k, :], bcast(c["identb"][:, :], [[0, HEADS], [1, P]]),
                                         start=True, stop=False, skip_group_check=True)
                        for h in range(HEADS):
                            for part in (ehi, elo):
                                ins = nc.tensor.matmul(pmax[k][:, h, :], part[s1][:, k, h:h + 1].broadcast_to([P, P]), c["identb"][:, :],
                                                       start=False, stop=(part is elo), skip_group_check=True)
                        ins.then_inc(max_ready, 1)
                if 0 in parts:
                    pe.wait_ge(oh_ready, t + 1)
                    wait_positive(pe, ohT_ready, t)
                    for k in range(K):
                        ins = nc.tensor.transpose(pT[:, k, :], oh[u][:, k, :], c["ident"][:, :])
                    ins.then_inc(turned, 1)
                if 2 in parts:
                    g = t - 2
                    wait_positive(pe, acc_done, g)
                    for k in range(K):
                        if k % 2 == 0:
                            pe.wait_ge(f_ready, g * F_OPS + 2 + k // 2)
                        ins = nc.tensor.matmul(psum[:, 0:HEADS * H1], oh[s2][:, k, :], flat(f[s2][:, k, :, :]), start=(k == 0), stop=(k == K - 1))
                    ins.then_inc(sum_ready, 1)

            in_steps(pe, step)


def make_consts(s):
    return {
        "ident": s.sb("ident", [P, P]), "identb": s.sb("identb", [P, P], BF16), "ramp": s.sb("ramp", [P, 512]),
        "before": s.sb("before", [P, P]), "upto": s.sb("upto", [P, P]), "ones": s.sb("ones", [P, P]),
        "beyond": s.sb("beyond", [P, 1]), "ln_eps": s.sb("ln_eps", [P, 1]), "bn_eps": s.sb("bn_eps", [P, 1]), "minus_big": s.sb("minus_big", [P, 1]),
    }


def join_attention(nc, c, a, acc, x_res, side):
    with Stage(nc, "join") as s:
        rden, bias = s.sb("rden", [P, NT, HEADS]), s.sb("bias", [P, D])
        loaded, dv = s.sem("loaded"), s.sem("dv")
        send = side(s)
        block = s.block()

        @block.gpsimd
        def _(pool):
            send(pool)

        @block.sync
        def _(sp):
            sp.dma_start(bias[:, :], rows(a["L0_gnn_h_bias"])).then_inc(loaded, 16)

        @block.vector
        def _(dve):
            v, do = nc.vector, Chain(dve, dv)
            do(v.tensor_scalar(rden[:, :, :], acc[:, :, :, HD], 1e-30, None, ALU.max))
            do(v.reciprocal(rden[:, :, :], rden[:, :, :]))
            heads = acc[:, :, :, 0:HD].rearrange("p t h d -> p (t h) d")
            xh = x_res[:, :, :].rearrange("p t (h d) -> p (t h) d", h=HEADS)
            do(v.tensor_tensor(heads, heads, flat(rden[:, :, :]).unsqueeze(2).broadcast_to([P, NT * HEADS, HD]), ALU.mult))
            do(v.tensor_tensor(xh, xh, heads, ALU.add))
            dve.wait_ge(loaded, 16)
            do(v.tensor_tensor(x_res[:, :, :], x_res[:, :, :], bcast(bias[:, :], [[0, NT], [1, D]]), ALU.add))


def route(nc, name, c, experts, gate_w, gate_b, xnT, mask, top, side=None):
    E = experts
    with Stage(nc, name) as s:
        gw, gb = s.sb("gw", [P, 2, E]), s.sb("gb", [P, E])
        pr, score, down = s.sb("pr", [P, NT, E]), s.sb("score", [P, NT, E]), s.sb("down", [P, E])
        red = s.sb("red", [P, NT])
        pl = s.ps("pl", [P, NT, E])
        loaded, logits, shifted, powers, dv = (s.sem(k) for k in ("loaded", "logits", "shifted", "powers", "dv"))
        send = side(s) if side else None
        block = s.block()

        if send is not None:
            @block.gpsimd
            def _(pool):
                send(pool)

        def wide(ap):
            return ap.unsqueeze(2).broadcast_to([P, NT, E])

        @block.sync
        def _(sp):
            sp.dma_start(gw[:, :, :], gate_w.rearrange("(k p) e -> p k e", p=P)).then_inc(loaded, 16)
            sp.dma_start(gb[:, :], rows(gate_b)).then_inc(loaded, 16)

        @block.tensor
        def _(pe):
            pe.wait_ge(loaded, 32)
            for t in range(NT):
                for k in range(2):
                    ins = nc.tensor.matmul(pl[:, t, :], xnT[:, k, t * P:(t + 1) * P], gw[:, k, :], start=(k == 0), stop=(k == 1))
            ins.then_inc(logits, 1)

        @block.scalar
        def _(act):
            act.wait_ge(shifted, 1)
            nc.scalar.activation(pr[:, :, :], pr[:, :, :], ACT.Exp).then_inc(powers, 1)

        @block.vector
        def _(dve):
            v, do = nc.vector, Chain(dve, dv)
            do(v.tensor_scalar(down[:, :], c["ramp"][:, 0:E], -1.0, float(E), ALU.mult, ALU.add))
            dve.wait_ge(loaded, 32)
            dve.wait_ge(logits, 1)
            do(v.tensor_tensor(pr[:, :, :], pl[:, :, :], bcast(gb[:, :], [[0, NT], [1, E]]), ALU.add))
            do(v.tensor_reduce(red[:, :], pr[:, :, :], AX.X, ALU.max))
            v.tensor_tensor(pr[:, :, :], pr[:, :, :], wide(red[:, :]), ALU.subtract).then_inc(shifted, 1)
            dve.wait_ge(powers, 1)
            do(v.tensor_reduce(red[:, :], pr[:, :, :], AX.X, ALU.add))
            do(v.reciprocal(red[:, :], red[:, :]))
            do(v.tensor_tensor(pr[:, :, :], pr[:, :, :], wide(red[:, :]), ALU.mult))
            for k in range(2):
                do(v.tensor_reduce(top[k][:, :], pr[:, :, :], AX.X, ALU.max))
                do(v.tensor_tensor(score[:, :, :], pr[:, :, :], wide(top[k][:, :]), ALU.is_equal))
                do(v.tensor_tensor(score[:, :, :], score[:, :, :], bcast(down[:, :], [[0, NT], [1, E]]), ALU.mult))
                do(v.tensor_reduce(red[:, :], score[:, :, :], AX.X, ALU.max))
                do(v.tensor_tensor(mask[k][:, :, :], score[:, :, :], wide(red[:, :]), ALU.is_equal))
                if k == 0:
                    do(v.scalar_tensor_tensor(out=pr[:, :, :], in0=mask[0][:, :, :], scalar=-2.0, in1=pr[:, :, :],
                                              op0=ALU.mult, op1=ALU.add))


def mixture(nc, c, a, xnT, x_res, side):
    G, N = 3, 3 * P
    with Stage(nc, "mix") as S:
        mask = [S.sb(f"mask{k}", [P, NT, EX0]) for k in range(2)]
        top = [S.sb(f"top{k}", [P, NT]) for k in range(2)]
        route(nc, "route0", c, EX0, a["L0_ffn_gW"], a["L0_ffn_gb"], xnT, mask, top, side(2))
        with Stage(nc, "mixf") as s:
            gate = s.sb("gate", [P, NT, EX0])
            w1, w2, w3 = s.sb("w1", [P, 2, 2 * P]), s.sb("w2", [P, 2, P]), s.sb("w3", [P, D])
            e1w, e2w, e3w = s.sb("e1w", [P, EX0, 2, P]), s.sb("e2w", [P, EX0, 64]), s.sb("e3w", [65, EX0, D])
            b1, b2, b3 = s.sb("b1", [P, 2]), s.sb("b2", [P, 1]), s.sb("b3", [P, D])
            eb1, eb2 = s.sb("eb1", [P, EX0]), s.sb("eb2", [64, EX0])
            s1, s2 = s.sb("s1", [P, 2, N]), s.sb("s2", [P, N])
            h1, h2 = s.sb("h1", [P, EX0, N]), s.sb("h2", [65, EX0, N])
            order1, order2, outs = [0, 1, 2, 3, 4, 5], [6, 7, 0, 1, 2], [[3, 4, 5], [6, 7, 0], [1, 2, 3]]
            every = order1 + order2 + sum(outs, [])
            banks = [s.ps(f"bank{b}", [P, 512]) for b in range(8)]
            loaded, dv, gated, biased = s.sem("loaded"), s.sem("dv"), s.sem("gated"), s.sem("biased")
            drop_ready, power_ready = s.sem("drop_ready"), s.sem("power_ready")
            l1, l2, l3 = s.sem("layer1"), s.sem("layer2"), s.sem("layer3")
            r1, r2 = s.sem("relu1"), s.sem("relu2")
            added = s.sem("added")
            send = side(3)(s)
            block = s.block()
            loads = [
                (w1[:, :, :], a["L0_ffn_sW1"].rearrange("(k p) n -> p k n", p=P)),
                (w2[:, :, :], a["L0_ffn_sW2"].rearrange("(k p) n -> p k n", p=P)),
                (w3[:, :], a["L0_ffn_sW3"]),
                (e1w[:, :, :, :].rearrange("p e k n -> p (e k) n"), a["L0_ffn_eW1"].rearrange("e (k p) n -> p (e k) n", p=P)),
                (e2w[:, :, :], a["L0_ffn_eW2"].rearrange("e p n -> p e n")),
                (e3w[0:64, :, :], a["L0_ffn_eW3"].rearrange("e p n -> p e n")),
                (e3w[64:65, :, :], a["L0_ffn_eb3"].rearrange("(o e) n -> o e n", o=1)),
                (b1[:, :], a["L0_ffn_sb1"].rearrange("(k p) -> p k", p=P)),
                (b2[:, :], a["L0_ffn_sb2"].rearrange("(p o) -> p o", o=1)),
                (eb1[:, :], a["L0_ffn_eb1"].rearrange("e p -> p e")),
                (eb2[:, :], a["L0_ffn_eb2"].rearrange("e p -> p e")),
                (b3[:, :], rows(a["L0_ffn_sb3"])),
            ]
            LOADED = 16 * len(loads)

            @block.sync
            def _(sp):
                with nc.allow_non_contiguous_dma(reason="small biases"):
                    for dest, source in loads:
                        sp.dma_start(dest, source).then_inc(loaded, 16)

            @block.gpsimd
            def _(pool):
                nc.gpsimd.memset(h2[64:65, :, :], 1.0).then_inc(biased, 1)
                pool.wait_ge(biased, 1)
                pool.wait_ge(loaded, LOADED)
                nc.gpsimd.tensor_tensor(x_res[:, :, :], x_res[:, :, :], bcast(b3[:, :], [[0, NT], [1, D]]), ALU.add).then_inc(biased, 1)
                send(pool)

            def wait_free(eng, i, q, first):
                before = [p for p in range(q) if every[p] == every[q]]
                if not before:
                    if first:
                        return
                    i, before = i - 1, [p for p in range(len(every)) if every[p] == every[q]]
                p = before[-1]
                if p < 6:
                    eng.wait_ge(r1, i * 6 + p + 1)
                elif p < 11:
                    eng.wait_ge(r2, i * 5 + p - 5)
                else:
                    t, m = divmod(p - 11, 3)
                    eng.wait_ge(added, i * G * 5 + t * 5 + min(2 * m + 2, 5))

            @block.tensor
            def _(pe):
                pe.wait_ge(loaded, LOADED)
                pe.wait_ge(biased, 1)

                def group(i, first=False):
                    cols = [xnT[:, k, bass.ds(i * N, N)] for k in range(2)]
                    for j, w in enumerate([w1[:, :, 0:P], w1[:, :, P:2 * P]] + [e1w[:, e, :, :] for e in range(EX0)]):
                        wait_free(pe, i, j, first)
                        b = order1[j]
                        for k in range(2):
                            ins = nc.tensor.matmul(banks[b][:, 0:N], w[:, k, :], cols[k], start=(k == 0), stop=(k == 1))
                        ins.then_inc(l1, 1)
                    for j in range(5):
                        wait_free(pe, i, 6 + j, first)
                        b = order2[j]
                        pe.wait_ge(r1, i * 6 + 2 + j)
                        if j == 0:
                            for k in range(2):
                                ins = nc.tensor.matmul(banks[b][:, 0:N], w2[:, k, :], s1[:, k, :], start=(k == 0), stop=(k == 1))
                        else:
                            ins = nc.tensor.matmul(banks[b][0:64, 0:N], e2w[:, j - 1, :], h1[:, j - 1, :], start=True, stop=True)
                        ins.then_inc(l2, 1)
                    pe.wait_ge(r2, i * 5 + 5)
                    for t in range(G):
                        for m in range(3):
                            wait_free(pe, i, 11 + 3 * t + m, first)
                            b = outs[t][m]
                            for o in range(2 * m, min(2 * m + 2, 5)):
                                half = banks[b][:, (o % 2) * D:(o % 2 + 1) * D]
                                if o == 0:
                                    ins = nc.tensor.matmul(half, s2[:, t * P:(t + 1) * P], w3[:, :], start=True, stop=True)
                                else:
                                    ins = nc.tensor.matmul(half, h2[:, o - 1, t * P:(t + 1) * P], e3w[:, o - 1, :], start=True, stop=True)
                            ins.then_inc(l3, 1)

                group(0, first=True)
                with pe.Fori(1, NT // G) as i:
                    group(i)

            @block.scalar
            def _(act):
                act.wait_ge(loaded, LOADED)
                act.wait_ge(drop_ready, 1)
                nc.scalar.activation(top[1][:, :], top[1][:, :], ACT.Exp).then_inc(power_ready, 1)

                def group(i, first=False):
                    for j in range(6):
                        act.wait_ge(l1, i * 6 + j + 1)
                        if not first:
                            act.wait_ge(l2, (i - 1) * 5 + max(j, 1))
                        dest, bias = (s1[:, j, :], b1[:, j:j + 1]) if j < 2 else (h1[:, j - 2, :], eb1[:, j - 2:j - 1])
                        nc.scalar.activation(dest, banks[order1[j]][:, 0:N], ACT.Relu, bias=bias).then_inc(r1, 1)
                    for j in range(5):
                        act.wait_ge(l2, i * 5 + j + 1)
                        if not first:
                            act.wait_ge(l3, i * 9)
                        bank = banks[order2[j]]
                        if j == 0:
                            nc.scalar.activation(s2[:, :], bank[:, 0:N], ACT.Relu, bias=b2[:, 0:1]).then_inc(r2, 1)
                        else:
                            nc.scalar.activation(h2[0:64, j - 1, :], bank[0:64, 0:N], ACT.Relu, bias=eb2[:, j - 1:j]).then_inc(r2, 1)

                group(0, first=True)
                with act.Fori(1, NT // G) as i:
                    group(i)

            @block.vector
            def _(dve):
                v, do = nc.vector, Chain(dve, dv)
                v.tensor_tensor(top[1][:, :], top[1][:, :], top[0][:, :], ALU.subtract).then_inc(drop_ready, 1)
                dve.wait_ge(power_ready, 1)
                do(v.tensor_scalar(top[0][:, :], top[1][:, :], 1.0, None, ALU.add))
                do(v.reciprocal(top[0][:, :], top[0][:, :]))
                do(v.tensor_tensor(top[1][:, :], top[1][:, :], top[0][:, :], ALU.mult))
                for k in range(2):
                    do(v.tensor_tensor(mask[k][:, :, :], mask[k][:, :, :], top[k][:, :].unsqueeze(2).broadcast_to([P, NT, EX0]), ALU.mult))
                do(v.tensor_tensor(gate[:, :, :], mask[0][:, :, :], mask[1][:, :, :], ALU.add))
                dve.wait_ge(biased, 2)
                with dve.Fori(0, NT // G) as i:
                    count = Steps(dve, added, i * G * 5)
                    for t in range(G):
                        x = flat(x_res[:, bass.ds(i * G + t, 1), :])
                        for o in range(5):
                            b = outs[t][o // 2]
                            half = banks[b][:, (o % 2) * D:(o % 2 + 1) * D]
                            if o % 2 == 0:
                                dve.wait_ge(l3, i * 9 + 3 * t + o // 2 + 1)
                            count.wait()
                            if o == 0:
                                count(v.tensor_tensor(x, x, half, ALU.add))
                            else:
                                count(v.scalar_tensor_tensor(out=x, in0=half, scalar=gate[:, bass.ds(i * G + t, 1), o - 1],
                                                             in1=x, op0=ALU.mult, op1=ALU.add))


def turn_rows(nc, name, c, src, dstT):
    with Stage(nc, name) as s:
        row = [s.sb(f"row{u}", [P, D]) for u in range(2)]
        pt = [s.ps(f"pt{u}", [P, 2, P]) for u in range(2)]
        taken, turned, copied = s.sem("taken"), s.sem("turned"), s.sem("copied")
        block = s.block()

        def pairs(eng, step):
            for u in range(2):
                step(0, u, True)
            with eng.Fori(1, NT // 2) as i:
                for u in range(2):
                    step(i, u, False)

        @block.vector
        def _(dve):
            def step(i, u, first):
                if not first:
                    dve.wait_ge(turned, i * 2 + u - 1)
                nc.vector.tensor_scalar(row[u][:, :], flat(src[:, bass.ds(i * 2 + u, 1), :]), 1.0, None, ALU.mult).then_inc(taken, 1)
            pairs(dve, step)

        @block.tensor
        def _(pe):
            def step(i, u, first):
                pe.wait_ge(taken, i * 2 + u + 1)
                if not first:
                    pe.wait_ge(copied, i * 2 + u - 1)
                for h in range(2):
                    ins = nc.tensor.transpose(pt[u][:, h, :], row[u][:, h * P:(h + 1) * P], c["ident"][:, :])
                ins.then_inc(turned, 1)
            pairs(pe, step)

        @block.scalar
        def _(act):
            def step(i, u, first):
                act.wait_ge(turned, i * 2 + u + 1)
                nc.scalar.activation(dstT[:, :, bass.ds((i * 2 + u) * P, P)], pt[u][:, :, :], ACT.Copy).then_inc(copied, 1)
            pairs(act, step)


def convolve(nc, c, a, agg, table1, xtab, bins1):
    K = 4
    GROUPS = ET // K
    N = K * P
    with Stage(nc, "conv") as s:
        two = range(2)
        recs = s.sb("recs", [P, ET, W1])
        rowidx = s.sb("rowidx", [P, ET], I32)
        wf1, wf2 = s.sb("wf1", [NG, D]), s.sb("wf2", [P, 2, D])
        bf1, bf2 = s.sb("bf1", [P, 2]), s.sb("bf2", [P, D])
        idx = [s.sb(f"idx{u}", [P, K], I32) for u in two]
        got = [s.sb(f"got{u}", [P, K, D]) for u in two]
        attr = [s.sb(f"attr{u}", [P, K, NG]) for u in two]
        attrT = [s.sb(f"attrT{u}", [NG, N]) for u in two]
        act1 = [s.sb(f"act1{u}", [P, 2, N]) for u in two]
        oh = [s.sb(f"onehot{u}", [P, K, P]) for u in two]
        filt = s.sb("filt", [P, K, D])
        msg = [s.sb(f"msg{u}", [P, K, D]) for u in two]
        pT = s.ps("pT", [NG, N])
        p1 = [s.ps(f"p1{h}", [P, N]) for h in two]
        pf = [s.ps(f"pf{h}", [P, 2, D]) for h in two]
        psum = [s.ps(f"psum{h}", [P, 2, D]) for h in two]
        loaded, prep = s.sem("loaded"), s.sem("prep")
        idx_ready, attr_ready, turned, attrT_ready = (s.sem(n) for n in ("idx_ready", "attr_ready", "turned", "attrT_ready"))
        layer1, act_ready, filtered, oh_ready = (s.sem(n) for n in ("layer1", "act_ready", "filtered", "oh_ready"))
        filt_ready, msg_ready, summed, agg_done = (s.sem(n) for n in ("filt_ready", "msg_ready", "summed", "agg_done"))
        got_s = [s.sem(f"got_s{u}") for u in two]
        block = s.block()
        LOADED = 16 * 5

        def in_steps(eng, step):
            step(0, 0, {0})
            step(0, 1, {0, 1})
            step(1, 0, {0, 1, 2})
            step(1, 1, {0, 1, 2, 3})
            with eng.Fori(2, GROUPS // 2) as i:
                step(i, 0, {0, 1, 2, 3})
                step(i, 1, {0, 1, 2, 3})
            step(GROUPS // 2, 0, {1, 2, 3})
            step(GROUPS // 2, 1, {2, 3})
            step(GROUPS // 2 + 1, 0, {3})

        @block.sync
        def _(sp):
            sp.dma_start(recs[:, :, :], table1.rearrange("(p t) w -> p t w", p=P)).then_inc(loaded, 16)
            sp.dma_start(wf1[:, :], a["L1_gnn_Wf1"]).then_inc(loaded, 16)
            sp.dma_start(wf2[:, :, :], a["L1_gnn_Wf2"].rearrange("(k p) n -> p k n", p=P)).then_inc(loaded, 16)
            with nc.allow_non_contiguous_dma(reason="a small bias"):
                sp.dma_start(bf1[:, :], a["L1_gnn_bf1"].rearrange("(k p) -> p k", p=P)).then_inc(loaded, 16)
            sp.dma_start(bf2[:, :], rows(a["L1_gnn_bf2"])).then_inc(loaded, 16)

        @block.gpsimd
        def _(pool):
            nc.gpsimd.memset(agg[:, :, :], 0.0).then_inc(prep, 1)
            pool.wait_ge(prep, 2)

            def gathers(i, u, first):
                g = i * 2 + u
                if not first:
                    pool.wait_ge(msg_ready, (g - 1) * 2)
                nc.gpsimd.tensor_copy(idx[u][:, :], rowidx[:, bass.ds(g * K, K)]).then_inc(idx_ready, 1)
                pool.wait_ge(idx_ready, g + 1)
                pool.nop(nofuse=True)
                for k in range(K):
                    nc.gpsimd.indirect_dma_start(
                        out=got[u][:, k, :], out_offset=None, in_=xtab,
                        in_offset=bass.IndirectOffsetOnAxis(ap=idx[u][:, k:k + 1], axis=0)).then_inc(got_s[u], 16)

            for u in two:
                gathers(0, u, True)
            with pool.Fori(1, GROUPS // 2) as i:
                for u in two:
                    gathers(i, u, False)

        @block.scalar
        def _(act):
            act.wait_ge(loaded, LOADED)

            def step(i, u, parts):
                g, w = i * 2 + u, 1 - u
                if 0 in parts:
                    if 2 in parts:
                        act.wait_ge(turned, g - 1)
                    nc.scalar.activation(attr[u][:, :, :], recs[:, bass.ds(g * K, K), 0:NG], ACT.Copy).then_inc(attr_ready, 1)
                if 1 in parts:
                    for h in two:
                        act.wait_ge(layer1, (g - 1) * 2 + h + 1)
                        if 3 in parts:
                            act.wait_ge(filtered, (g - 2) * 2)
                        nc.scalar.activation(act1[w][:, h, :], p1[h][:, :], ACT.Silu, bias=bf1[:, h:h + 1]).then_inc(act_ready, 1)
                if 0 in parts:
                    act.wait_ge(turned, g + 1)
                    if 2 in parts:
                        act.wait_ge(layer1, (g - 1) * 2)
                    nc.scalar.activation(attrT[u][:, :], pT[:, :], ACT.Copy).then_inc(attrT_ready, 1)

            in_steps(act, step)

        @block.tensor
        def _(pe):
            pe.wait_ge(loaded, LOADED)

            def step(i, u, parts):
                g, w = i * 2 + u, 1 - u
                if 0 in parts:
                    pe.wait_ge(attr_ready, g + 1)
                    if 1 in parts:
                        pe.wait_ge(attrT_ready, g)
                    for k in range(K):
                        ins = nc.tensor.transpose(pT[:, k * P:(k + 1) * P], attr[u][:, k, :], c["ident"][:, :])
                    ins.then_inc(turned, 1)
                if 1 in parts:
                    for h in two:
                        pe.wait_ge(attrT_ready, g)
                        if 2 in parts:
                            pe.wait_ge(act_ready, (g - 2) * 2 + h + 1)
                        nc.tensor.matmul(p1[h][:, :], wf1[:, h * P:(h + 1) * P], attrT[w][:, :], start=True, stop=True).then_inc(layer1, 1)
                if 2 in parts:
                    pe.wait_ge(act_ready, (g - 1) * 2)
                    for b in two:
                        if 3 in parts:
                            pe.wait_ge(filt_ready, (g - 3) * 2 + b + 1)
                        for k in two:
                            for h in two:
                                ins = nc.tensor.matmul(pf[b][:, k, :], act1[u][:, h, (2 * b + k) * P:(2 * b + k + 1) * P], wf2[:, h, :],
                                                       start=(h == 0), stop=(h == 1))
                        ins.then_inc(filtered, 1)
                if 3 in parts:
                    for b in two:
                        pe.wait_ge(oh_ready, g - 2)
                        pe.wait_ge(msg_ready, (g - 3) * 2 + b + 1)
                        pe.wait_ge(agg_done, (g - 3) * K if not isinstance(g, int) or g > 3 else 0)
                        for k in two:
                            ins = nc.tensor.matmul(psum[b][:, k, :], oh[w][:, 2 * b + k, :], msg[w][:, 2 * b + k, :], start=True, stop=True)
                        ins.then_inc(summed, 1)

            in_steps(pe, step)

        @block.vector
        def _(dve):
            v = nc.vector
            dve.wait_ge(loaded, LOADED)
            v.tensor_copy(rowidx[:, :], recs[:, :, NG]).then_inc(prep, 1)

            def step(i, u, parts):
                g, w = i * 2 + u, 1 - u
                if 3 in parts:
                    bins = [dve.value_load(bins1[0:1, bass.ds((g - 3) * K + k, 1)], min_val=0, max_val=NT - 1) for k in range(K)]
                if 2 in parts:
                    node = recs[:, bass.ds((g - 2) * K, K), NG + 1]
                    if 3 in parts and not (isinstance(g, int) and g == 3):
                        dve.wait_ge(summed, (g - 3) * 2)
                    v.tensor_tensor(oh[u][:, :, :], bcast(c["ramp"][:, 0:P], [[0, K], [1, P]]),
                                    node.unsqueeze(2).broadcast_to([P, K, P]), ALU.is_equal).then_inc(oh_ready, 1)
                    dve.wait_ge(msg_ready, (g - 2) * 2)
                    for b in two:
                        dve.wait_ge(filtered, (g - 2) * 2 + b + 1)
                        part = filt[:, 2 * b:2 * b + 2, :]
                        v.tensor_tensor(part, pf[b][:, :, :], bcast(bf2[:, :], [[0, 2], [1, D]]), ALU.add).then_inc(filt_ready, 1)
                    dve.wait_ge(got_s[u], i * 16 * K)
                    for b in two:
                        dve.wait_ge(filt_ready, (g - 2) * 2 + b + 1)
                        part = slice(2 * b, 2 * b + 2)
                        v.tensor_tensor(msg[u][:, part, :], filt[:, part, :], got[u][:, part, :], ALU.mult).then_inc(msg_ready, 1)
                if 3 in parts:
                    for k in range(K):
                        if k % 2 == 0:
                            dve.wait_ge(summed, (g - 3) * 2 + k // 2 + 1)
                        dve.wait_ge(agg_done, (g - 3) * K + k)
                        at = flat(agg[:, bass.ds(bins[k], 1), :])
                        v.tensor_tensor(at, at, psum[k // 2][:, k % 2, :], ALU.add).then_inc(agg_done, 1)

            dve.wait_ge(prep, 2)
            in_steps(dve, step)


def update(nc, c, a, aggT, x_res):
    G, N = 10, PADN // 10
    BN, BC = 10, NODES // 10
    with Stage(nc, "upd") as s:
        w1, w2 = s.sb("w1", [P, 2, D]), s.sb("w2", [P, 2, D])
        b1, b2, gamma, beta = (s.sb(n, [P, 2]) for n in ("b1", "b2", "gamma", "beta"))
        h1 = s.sb("h1", [P, 2, N])
        hT = s.sb("hT", [P, 2, PADN])
        st, mv = s.sb("st", [P, 2, BN, 6]), s.sb("mv", [P, 2, 2])
        scale, shift = s.sb("scale", [P, 2]), s.sb("shift", [P, 2])
        col = [s.sb(f"col{u}", [P, 2, P]) for u in range(2)]
        p1 = [s.ps(f"p1{h}", [P, N]) for h in range(2)]
        p2 = [s.ps(f"p2{h}", [P, N]) for h in range(2)]
        pt = [s.ps(f"pt{u}", [P, D]) for u in range(2)]
        names = ("loaded", "dv", "layer1", "act1", "layer2", "kept", "var_ready", "std_ready", "scale_ready",
                 "taken", "turned", "joined")
        loaded, dv, layer1, act1, layer2, kept, var_ready, std_ready, scale_ready, taken, turned, joined = (s.sem(n) for n in names)
        block = s.block()
        loads = [
            (w1[:, :, :], a["L1_gnn_Wu1"].rearrange("(k p) n -> p k n", p=P)),
            (w2[:, :, :], a["L1_gnn_Wu2"].rearrange("(k p) n -> p k n", p=P)),
            (b1[:, :], a["L1_gnn_bu1"].rearrange("(k p) -> p k", p=P)), (b2[:, :], a["L1_gnn_bu2"].rearrange("(k p) -> p k", p=P)),
            (gamma[:, :], a["L1_gnn_gamma"].rearrange("(k p) -> p k", p=P)), (beta[:, :], a["L1_gnn_beta"].rearrange("(k p) -> p k", p=P)),
        ]

        @block.sync
        def _(sp):
            with nc.allow_non_contiguous_dma(reason="small vectors"):
                for dest, source in loads:
                    sp.dma_start(dest, source).then_inc(loaded, 16)

        @block.tensor
        def _(pe):
            pe.wait_ge(loaded, 16 * len(loads))

            def group(i, first):
                for h in range(2):
                    if not first:
                        pe.wait_ge(act1, (i - 1) * 2 + h + 1)
                    for k in range(2):
                        ins = nc.tensor.matmul(p1[h][:, :], w1[:, k, h * P:(h + 1) * P], aggT[:, k, bass.ds(i * N, N)], start=(k == 0), stop=(k == 1))
                    ins.then_inc(layer1, 1)
                pe.wait_ge(act1, i * 2 + 2)
                for h in range(2):
                    if not first:
                        pe.wait_ge(kept, (i - 1) * 2 + h + 1)
                    for k in range(2):
                        ins = nc.tensor.matmul(p2[h][:, :], w2[:, k, h * P:(h + 1) * P], h1[:, k, :], start=(k == 0), stop=(k == 1))
                    ins.then_inc(layer2, 1)

            group(0, True)
            with pe.Fori(1, G) as i:
                group(i, False)

            def turn(i, u, first):
                pe.wait_ge(taken, (i * 2 + u + 1) * 2)
                if not first:
                    pe.wait_ge(joined, i * 2 + u - 1)
                for h in range(2):
                    ins = nc.tensor.transpose(pt[u][:, h * P:(h + 1) * P], col[u][:, h, :], c["ident"][:, :])
                ins.then_inc(turned, 1)

            for u in range(2):
                turn(0, u, True)
            with pe.Fori(1, NT // 2) as i:
                for u in range(2):
                    turn(i, u, False)

        @block.scalar
        def _(act):
            act.wait_ge(loaded, 16 * len(loads))

            def group(i, first):
                for h in range(2):
                    act.wait_ge(layer1, i * 2 + h + 1)
                    if not first:
                        act.wait_ge(layer2, (i - 1) * 2 + 2)
                    nc.scalar.activation(h1[:, h, :], p1[h][:, :], ACT.Silu, bias=b1[:, h:h + 1]).then_inc(act1, 1)

            group(0, True)
            with act.Fori(1, G) as i:
                group(i, False)
            act.wait_ge(var_ready, 1)
            nc.scalar.activation(scale[:, :], mv[:, :, 1], ACT.Sqrt, bias=c["bn_eps"][:, 0:1]).then_inc(std_ready, 1)
            act.wait_ge(scale_ready, 1)

            def take(i, u, first):
                if not first:
                    act.wait_ge(turned, i * 2 + u - 1)
                for h in range(2):
                    ins = nc.scalar.activation(col[u][:, h, :], hT[:, h, bass.ds((i * 2 + u) * P, P)], ACT.Identity,
                                               bias=shift[:, h:h + 1], scale=scale[:, h:h + 1])
                    ins.then_inc(taken, 1)

            for u in range(2):
                take(0, u, True)
            with act.Fori(1, NT // 2) as i:
                for u in range(2):
                    take(i, u, False)

        @block.vector
        def _(dve):
            v, do = nc.vector, Chain(dve, dv)
            dve.wait_ge(loaded, 16 * len(loads))
            with dve.Fori(0, G) as i:
                for h in range(2):
                    dve.wait_ge(layer2, i * 2 + h + 1)
                    v.tensor_scalar(hT[:, h, bass.ds(i * N, N)], p2[h][:, :], b2[:, h:h + 1], None, ALU.add).then_inc(kept, 1)
            dve.wait_ge(kept, 2 * G)
            for h in range(2):
                for j in range(BN):
                    do(v.bn_stats(st[:, h, j, :], hT[:, h, j * BC:(j + 1) * BC]))
                do(v.bn_aggr(mv[:, h, :], st[:, h, :, :]))
            v.memset(shift[:, :], 0.0).then_inc(var_ready, 1)
            dve.wait_ge(std_ready, 1)
            dve.wait_ge(var_ready, 1)
            do(v.reciprocal(scale[:, :], scale[:, :]))
            do(v.tensor_tensor(scale[:, :], scale[:, :], gamma[:, :], ALU.mult))
            do(v.tensor_tensor(shift[:, :], mv[:, :, 0], scale[:, :], ALU.mult))
            v.tensor_tensor(shift[:, :], beta[:, :], shift[:, :], ALU.subtract).then_inc(scale_ready, 1)
            with dve.Fori(0, NT // 2) as i:
                for u in range(2):
                    dve.wait_ge(turned, i * 2 + u + 1)
                    x = flat(x_res[:, bass.ds(i * 2 + u, 1), :])
                    v.tensor_tensor(x, x, pt[u][:, :], ALU.add).then_inc(joined, 1)


def routed(nc, c, a, xnT, x_res, xtab, slots, results):
    U2 = 2
    with Stage(nc, "rt") as S:
        mask = [S.sb(f"mask{k}", [P, NT, EX1]) for k in range(2)]
        top = [S.sb(f"top{k}", [P, NT]) for k in range(2)]
        bin_f, pos_f = S.sb("bin_f", [P, 2 * NT]), S.sb("pos_f", [P, 2 * NT])
        addr_i, pos_i = S.sb("addr_i", [P, 2 * NT], I32), S.sb("pos_i", [P, 2 * NT], I32)
        expert = S.sb("expert", [1, 512], I32)
        token = S.sb("token", [P, NT], I32)
        route(nc, "route1", c, EX1, a["L1_ffn_gate_w"], a["L1_ffn_gate_b"], xnT, mask, top)

        with Stage(nc, "pick") as s:
            tmp, red = s.sb("tmp", [P, NT, EX1]), s.sb("red", [P, NT])
            empty = s.sb("empty", [P, MT], I32)
            dv, cleared, filled = s.sem("dv"), s.sem("cleared"), s.sem("filled")
            block = s.block()

            @block.gpsimd
            def _(pool):
                nc.gpsimd.memset(empty[:, :], 0).then_inc(cleared, 1)
                nc.gpsimd.iota(token[:, :], pattern=[[P, NT]], base=0, channel_multiplier=1).then_inc(cleared, 1)

            @block.sync
            def _(sp):
                sp.wait_ge(cleared, 2)
                sp.dma_start(slots.rearrange("(p t) o -> p (t o)", p=P), empty[:, :]).then_inc(filled, 16)
                sp.wait_ge(filled, 16)

            @block.vector
            def _(dve):
                v, do = nc.vector, Chain(dve, dv)
                bins = bin_f[:, :].rearrange("p (k t) -> p k t", k=2)
                for k in range(2):
                    do(v.tensor_tensor(tmp[:, :, :], mask[k][:, :, :], bcast(c["ramp"][:, 0:EX1], [[0, NT], [1, EX1]]), ALU.mult))
                    do(v.tensor_reduce(bins[:, k, :], tmp[:, :, :], AX.X, ALU.add))
                    last = bins[:, k, NT - 1:NT]
                    do(v.scalar_tensor_tensor(out=last, in0=c["beyond"][:, :], scalar=100.0, in1=last, op0=ALU.mult, op1=ALU.add))
                do(v.tensor_tensor(red[:, :], top[0][:, :], top[1][:, :], ALU.add))
                do(v.reciprocal(red[:, :], red[:, :]))
                for k in range(2):
                    do(v.tensor_tensor(top[k][:, :], top[k][:, :], red[:, :], ALU.mult))

        positions(nc, "by_expert", c, P, 2 * NT, EX1, MT, bin_f[:, :], pos_f[:, :], addr_i[:, :], expert)

        with Stage(nc, "send") as s:
            slot = [s.sb(f"slot{u}", [P, 2], I32) for u in range(2)]
            tok = [s.sb(f"tok{u}", [P, 1], I32) for u in range(2)]
            staged = s.sem("staged")
            sent = [[s.sem(f"sent{u}{k}") for k in range(2)] for u in range(2)]
            dv = s.sem("dv")
            block = s.block()

            @block.vector
            def _(dve):
                nc.vector.tensor_copy(pos_i[:, :], pos_f[:, :]).then_inc(dv, 1)

            @block.gpsimd
            def _(pool):
                def tile(t, u, i, n):
                    for k in range(2):
                        pool.wait_ge(sent[u][k], i * 16)
                    view = addr_i[:, :].rearrange("p (k t) -> p t k", k=2)
                    nc.gpsimd.tensor_copy(slot[u][:, :].unsqueeze(1), view[:, bass.ds(t, 1), :]).then_inc(staged, 1)
                    nc.gpsimd.tensor_copy(tok[u][:, :], token[:, bass.ds(t, 1)]).then_inc(staged, 1)
                    pool.wait_ge(staged, t * 2 + 2)
                    pool.nop(nofuse=True)
                    for k in range(2):
                        nc.gpsimd.indirect_dma_start(
                            out=slots, out_offset=bass.IndirectOffsetOnAxis(ap=slot[u][0:n, k:k + 1], axis=0),
                            in_=tok[u][0:n, :], in_offset=None).then_inc(sent[u][k], 16)

                with pool.Fori(0, NT // 2 - 1) as i:
                    for u in range(2):
                        tile(i * 2 + u, u, i, P)
                tile(NT - 2, 0, NT // 2 - 1, P)
                tile(NT - 1, 1, NT // 2 - 1, TAIL)
                for u in range(2):
                    for k in range(2):
                        pool.wait_ge(sent[u][k], 16 * (NT // 2))

        with Stage(nc, "moe") as s:
            tokens = s.sb("tokens", [P, MT], I32)
            two = range(2)
            idx = [s.sb(f"idx{u}", [P, 1], I32) for u in two]
            got = [s.sb(f"got{u}", [P, D]) for u in two]
            xT = [s.sb(f"xT{u}", [P, 2, P]) for u in two]
            w1 = [s.sb(f"w1{u}", [P, 2, HID]) for u in two]
            w2 = [s.sb(f"w2{u}", [P, 2, HID]) for u in two]
            w3 = [s.sb(f"w3{u}", [P, HID // P, D]) for u in two]
            gatev, hid = s.sb("gatev", [P, HID]), [s.sb(f"hid{u}", [P, HID]) for u in two]
            y = [s.sb(f"y{u}", [P, D]) for u in two]
            pT = s.ps("pT", [P, 2, P])
            p1 = [s.ps(f"p1{u}", [P, HID]) for u in two]
            p2 = [s.ps(f"p2{u}", [P, HID]) for u in two]
            p3 = [s.ps(f"p3{u}", [P, D]) for u in two]
            w_s = [[s.sem(f"w{n}_loaded{u}") for n in range(3)] for u in two]
            loaded, idx_ready = s.sem("loaded"), s.sem("idx_ready")
            got_s = [s.sem(f"got_s{u}") for u in two]
            turned, xT_ready, up, gate_ready, hid_ready, down = (
                s.sem(n) for n in ("turned", "xT_ready", "up", "gate_ready", "hid_ready", "down"))
            y_ready = [s.sem(f"y_ready{u}") for u in two]
            stored = [s.sem(f"stored{u}") for u in two]
            block = s.block()
            NH = HID // P
            T2 = MT // 2

            @block.sync
            def _(sp):
                sp.dma_start(tokens[:, :], slots.rearrange("(p t) o -> p (t o)", p=P)).then_inc(loaded, 16)
                v1 = a["L1_ffn_w1"].rearrange("e (k p) n -> e p k n", p=P)
                v2 = a["L1_ffn_w2"].rearrange("e (k p) n -> e p k n", p=P)
                v3 = a["L1_ffn_w3"].rearrange("e (k p) n -> e p k n", p=P)

                def tile(i, u, first):
                    t = i * 2 + u
                    e = sp.value_load(expert[0:1, bass.ds(t, 1)], min_val=0, max_val=EX1 - 1)
                    if not first:
                        sp.wait_ge(up, t - 1)
                        sp.nop(nofuse=True)
                    for n, (w, v) in enumerate(((w1, v1), (w2, v2))):
                        sp.dma_start(w[u][:, :, :], v[bass.ds(e, 1)].rearrange("o p k n -> (o p) k n")).then_inc(w_s[u][n], 16)
                    if not first:
                        sp.wait_ge(down, t - 1)
                        sp.nop(nofuse=True)
                    sp.dma_start(w3[u][:, :, :], v3[bass.ds(e, 1)].rearrange("o p k n -> (o p) k n")).then_inc(w_s[u][2], 16)

                for u in two:
                    tile(0, u, True)
                with sp.Fori(1, T2) as i:
                    for u in two:
                        tile(i, u, False)

            @block.gpsimd
            def _(pool):
                pool.wait_ge(loaded, 16)

                def gather(i, u, first):
                    t = i * 2 + u
                    if not first:
                        pool.wait_ge(turned, t - 1)
                    nc.gpsimd.tensor_copy(idx[u][:, :], tokens[:, bass.ds(t, 1)]).then_inc(idx_ready, 1)
                    pool.wait_ge(idx_ready, t + 1)
                    pool.nop(nofuse=True)
                    nc.gpsimd.indirect_dma_start(
                        out=got[u][:, :], out_offset=None, in_=xtab,
                        in_offset=bass.IndirectOffsetOnAxis(ap=idx[u][:, 0:1], axis=0)).then_inc(got_s[u], 16)

                for u in two:
                    gather(0, u, True)
                with pool.Fori(1, T2) as i:
                    for u in two:
                        gather(i, u, False)

            def in_steps(eng, step):
                step(0, 0, {0})
                step(0, 1, {0, 1})
                with eng.Fori(1, T2) as i:
                    step(i, 0, {0, 1, 2})
                    step(i, 1, {0, 1, 2})
                step(T2, 0, {1, 2})
                step(T2, 1, {2})

            @block.tensor
            def _(pe):
                def step(i, u, parts):
                    t, w = i * 2 + u, 1 - u
                    if 0 in parts:
                        pe.wait_ge(got_s[u], (i + 1) * 16)
                        if 1 in parts:
                            pe.wait_ge(xT_ready, t)
                        for h in two:
                            ins = nc.tensor.transpose(pT[:, h, :], got[u][:, h * P:(h + 1) * P], c["ident"][:, :])
                        ins.then_inc(turned, 1)
                    if 1 in parts:
                        pe.wait_ge(xT_ready, t)
                        done = (i + 1) * 16 if u == 1 else i * 16
                        for n, (wt, ps) in enumerate(((w1, p1), (w2, p2))):
                            pe.wait_ge(w_s[w][n], done)
                            if 2 in parts and not (isinstance(t, int) and t < 3):
                                pe.wait_ge(hid_ready, t - 2)
                            for j in range(NH):
                                for k in two:
                                    ins = nc.tensor.matmul(ps[w][:, j * P:(j + 1) * P], wt[w][:, k, j * P:(j + 1) * P], xT[w][:, k, :],
                                                           start=(k == 0), stop=(k == 1))
                        ins.then_inc(up, 1)
                    if 2 in parts:
                        pe.wait_ge(hid_ready, t - 1)
                        pe.wait_ge(w_s[u][2], i * 16)
                        pe.wait_ge(y_ready[u], i - 1)
                        for j in range(NH):
                            ins = nc.tensor.matmul(p3[u][:, :], hid[u][:, j * P:(j + 1) * P], w3[u][:, j, :], start=(j == 0), stop=(j == NH - 1))
                        ins.then_inc(down, 1)

                in_steps(pe, step)

            @block.scalar
            def _(act):
                yv = results.rearrange("(t p) d -> t p d", p=P)

                def step(i, u, parts):
                    t, w = i * 2 + u, 1 - u
                    if 0 in parts:
                        act.wait_ge(turned, t + 1)
                        if 2 in parts:
                            act.wait_ge(up, t - 1)
                        nc.scalar.activation(xT[u][:, :, :], pT[:, :, :], ACT.Copy).then_inc(xT_ready, 1)
                    if 1 in parts:
                        act.wait_ge(up, t)
                        if 2 in parts:
                            act.wait_ge(hid_ready, t - 1)
                        nc.scalar.activation(gatev[:, :], p1[w][:, :], ACT.Silu).then_inc(gate_ready, 1)
                    if 2 in parts:
                        act.wait_ge(down, t - 1)
                        act.wait_ge(stored[u], (i - 1) * 16)
                        nc.scalar.activation(y[u][:, :], p3[u][:, :], ACT.Copy).then_inc(y_ready[u], 1)
                        act.wait_ge(y_ready[u], i)
                        act.dma_start(yv[bass.ds(t - 2, 1)].rearrange("o p d -> (o p) d"), y[u][:, :]).then_inc(stored[u], 16)

                in_steps(act, step)
                for u in two:
                    act.wait_ge(stored[u], 16 * T2)

            @block.vector
            def _(dve):
                def step(i, u, parts):
                    t, w = i * 2 + u, 1 - u
                    if 1 in parts:
                        dve.wait_ge(gate_ready, t)
                        if 2 in parts and not (isinstance(t, int) and t < 3):
                            dve.wait_ge(down, t - 2)
                        nc.vector.tensor_tensor(hid[w][:, :], gatev[:, :], p2[w][:, :], ALU.mult).then_inc(hid_ready, 1)

                in_steps(dve, step)

        with Stage(nc, "comb") as s:
            two = range(2)
            idx = [s.sb(f"idx{u}", [P, 2], I32) for u in two]
            got = [[s.sb(f"got{u}{k}", [P, D]) for k in two] for u in two]
            got_s = [[s.sem(f"got_s{u}{k}") for k in two] for u in two]
            idx_ready, added = s.sem("idx_ready"), s.sem("added")
            block = s.block()

            @block.gpsimd
            def _(pool):
                def tile(t, u, i, n, first=False):
                    if not first:
                        pool.wait_ge(added, (t - 1) * 2)
                    view = pos_i[:, :].rearrange("p (k t) -> p t k", k=2)
                    nc.gpsimd.tensor_copy(idx[u][:, :].unsqueeze(1), view[:, bass.ds(t, 1), :]).then_inc(idx_ready, 1)
                    pool.wait_ge(idx_ready, t + 1)
                    pool.nop(nofuse=True)
                    for k in two:
                        nc.gpsimd.indirect_dma_start(
                            out=got[u][k][0:n, :], out_offset=None, in_=results,
                            in_offset=bass.IndirectOffsetOnAxis(ap=idx[u][0:n, k:k + 1], axis=0)).then_inc(got_s[u][k], 16)

                for u in two:
                    tile(u, u, 0, P, first=True)
                with pool.Fori(1, NT // 2 - 1) as i:
                    for u in two:
                        tile(i * 2 + u, u, i, P)
                tile(NT - 2, 0, NT // 2 - 1, P)
                tile(NT - 1, 1, NT // 2 - 1, TAIL)

            @block.vector
            def _(dve):
                def tile(t, u, i, n):
                    for k in two:
                        dve.wait_ge(got_s[u][k], (i + 1) * 16)
                        dve.wait_ge(added, t * 2 + k)
                        x = flat(x_res[0:n, bass.ds(t, 1), :])
                        nc.vector.scalar_tensor_tensor(out=x, in0=got[u][k][0:n, :], scalar=top[k][0:n, bass.ds(t, 1)], in1=x,
                                                       op0=ALU.mult, op1=ALU.add).then_inc(added, 1)

                with dve.Fori(0, NT // 2 - 1) as i:
                    for u in two:
                        tile(i * 2 + u, u, i, P)
                tile(NT - 2, 0, NT // 2 - 1, P)
                tile(NT - 1, 1, NT // 2 - 1, TAIL)


def store(nc, x_res, out):
    with Stage(nc, "store") as s:
        stored = s.sem("stored")
        block = s.block()

        @block.sync
        def _(sp):
            sp.dma_start(out[0:(NT - 1) * P, :].rearrange("(t p) d -> p t d", p=P), x_res[:, 0:NT - 1, :]).then_inc(stored, 16)
            sp.dma_start(out[(NT - 1) * P:NODES, :], x_res[0:TAIL, NT - 1, :]).then_inc(stored, 16)
            sp.wait_ge(stored, 32)


def graph_layers(nc, a, out):
    feat = nc.dram_tensor("feat", (RELS * PADN, FW), F32).ap()
    table0 = nc.dram_tensor("table0", (P * ET0, W0), F32).ap()
    table1 = nc.dram_tensor("table1", (P * ET, W1), F32).ap()
    xtab = nc.dram_tensor("xtab", (PADN, D), F32).ap()
    xtab2 = nc.dram_tensor("xtab2", (PADN, D), F32).ap()
    slots = nc.dram_tensor("slots", (P * MT, 1), I32).ap()
    results = nc.dram_tensor("results", (P * MT, D), F32).ap()
    with Stage(nc, "all") as S:
        x_res = S.sb("x_res", [P, NT, D])
        c = make_consts(S)
        constants(nc, c, a["x"], x_res)
        bins0, bins1 = S.sb("bins0", [1, 512], I32), S.sb("bins1", [1, 512], I32)
        with Stage(nc, "recs1") as R:
            rec1, addr1 = R.sb("rec1", [P, EJ, W1]), R.sb("addr1", [P, EJ], I32)

            def side1(k):
                return lambda s: Sender(nc, s, table1, rec1, addr1, W1, sum(COLS1[:k]), COLS1[k])

            with Stage(nc, "l0") as L:
                er = L.sb("er", [P, NT, RELS * HEADS])
                with Stage(nc, "l0a") as M:
                    rec0, addr0 = M.sb("rec0", [P, EJ, W0]), M.sb("addr0", [P, EJ], I32)
                    with Stage(nc, "l0b") as N:
                        pos_f = N.sb("pos_f", [P, EJ])
                        edge_records(nc, c, a, rec0, rec1, pos_f, addr0, addr1, bins0, bins1, table0, table1)
                    with Stage(nc, "l0c") as N:
                        xnT = N.sb("xnT", [P, 2, PADN])
                        layer_norm(nc, "ln0", c, x_res, xnT, side=lambda s: Sender(nc, s, table0, rec0, addr0, W0, COLS0[0], COLS0[1]))
                        project(nc, c, a, xnT, er, feat, rec0, addr0, table0)
                acc = L.sb("acc", [P, NT, HEADS, HD + 1])
                attend(nc, c, er, acc, rec1, addr1, table0, table1, feat, bins0)
                join_attention(nc, c, a, acc, x_res, side1(1))
            with Stage(nc, "l1") as L:
                xnT = L.sb("xnT", [P, 2, PADN])
                layer_norm(nc, "ln1", c, x_res, xnT, side=side1(2))
                mixture(nc, c, a, xnT, x_res, lambda k: side1(k + 1))
            with Stage(nc, "l2a") as L:
                xnT = L.sb("xnT", [P, 2, PADN])
                layer_norm(nc, "ln2", c, x_res, xnT, xtab, add=True, side=side1(5))
        with Stage(nc, "l2b") as L:
            agg = L.sb("agg", [P, NT, D])
            convolve(nc, c, a, agg, table1, xtab, bins1)
            aggT = L.sb("aggT", [P, 2, PADN])
            turn_rows(nc, "turn", c, agg, aggT)
            update(nc, c, a, aggT, x_res)
        with Stage(nc, "l3") as L:
            xnT = L.sb("xnT", [P, 2, PADN])
            layer_norm(nc, "ln3", c, x_res, xnT, xtab2)
            routed(nc, c, a, xnT, x_res, xtab2, slots, results)
        store(nc, x_res, out)


def kernel(**inputs):
    import numpy as np
    import concourse.bacc as bacc
    from concourse.bass_utils import run_bass_kernel_spmd

    nc = bacc.Bacc("TRN2", target_bir_lowering=False, num_devices=1)
    arrays, a = {}, {}
    for name in inputs:
        array = np.ascontiguousarray(inputs[name])
        arrays[f"in_{name}"] = array
        a[name] = nc.dram_tensor(f"in_{name}", array.shape, mybir.dt.from_np(array.dtype), kind="ExternalInput").ap()
    out = nc.dram_tensor("out", (NODES, D), F32, kind="ExternalOutput").ap()
    graph_layers(nc, a, out)
    result = run_bass_kernel_spmd(nc, [arrays], core_ids=[0])
    return result.results[0]["out"]
```

```python
from contextlib import ExitStack

import concourse.bass as bass
from concourse import mybir

ALU = mybir.AluOpType
ACT = mybir.ActivationFunctionType
AX = mybir.AxisListType
F32 = mybir.dt.float32
BF16 = mybir.dt.bfloat16
I32 = mybir.dt.int32

P = 128
NODES, D = 3750, 256
NT = -(-NODES // P)
TAIL = NODES - (NT - 1) * P
PADN = NT * P
EDGES = 60000
EP, EJ = 125, 480
K = 4
ET = 588
assert EP * EJ == EDGES and (EDGES + NT * (K * P - 1)) // (K * P) <= ET // K and ET % (3 * K) == 0
COLS0 = 80, 48, 352
ROUND = 4
COLS1 = ROUND * (ET // K // 3 - 1), 16, 32, 32, 160, 48
assert sum(COLS0) == EJ == sum(COLS1)
RELS, HEADS, HD = 8, 4, 64
FW = D + HEADS
NG = 20
W0, W1 = 4, 24
EX0, EX1, HID = 4, 16, 512
MT = 76
assert (2 * NODES + EX1 * (P - 1)) // P <= MT
LN_EPS, BN_EPS, SLOPE = 1e-5, 1e-5, 0.2
BIG = float(2.0 ** 100)


class Stage:

    def __init__(self, nc, name):
        self.nc, self.name, self.ctx, self.sems, self.open = nc, name, ExitStack(), [], None

    def __enter__(self):
        self.ctx.__enter__()
        return self

    def __exit__(self, *error):
        if self.open is not None:
            self.open.__exit__(*error)
        if self.sems and error[0] is None:
            self.nc.clear_and_free_semaphores(self.sems)
            self.nc.all_engine_barrier()
        return self.ctx.__exit__(*error)

    def sb(self, name, shape, dt=F32):
        return self.ctx.enter_context(self.nc.sbuf_tensor(f"{self.name}_{name}", shape, dt))

    def ps(self, name, shape, dt=F32):
        return self.ctx.enter_context(self.nc.psum_tensor(f"{self.name}_{name}", shape, dt))

    def sem(self, name):
        self.sems.append(self.nc.alloc_semaphore(name=f"{self.name}_{name}"))
        return self.sems[-1]

    def block(self):
        self.open = self.nc.Block()
        return self.open.__enter__()


class Chain:

    def __init__(self, eng, sem):
        self.eng, self.sem, self.n = eng, sem, 0

    def __call__(self, ins):
        self.n += 1
        ins.then_inc(self.sem, 1)
        self.eng.wait_ge(self.sem, self.n)


def bcast(ap, dims):
    return bass.AP(ap.tensor, ap.offset, [list(ap.ap[0])] + [list(d) for d in dims])


def rows(vec, n=P):
    return bass.AP(vec.tensor, vec.offset, [[0, n]] + [list(d) for d in vec.ap])


class Steps:

    def __init__(self, eng, sem, start):
        self.eng, self.sem, self.start, self.n = eng, sem, start, 0

    def __call__(self, ins):
        self.n += 1
        ins.then_inc(self.sem, 1)
        return self.n

    def wait(self, n=None):
        wait_positive(self.eng, self.sem, self.start + (self.n if n is None else n))


def wait_positive(eng, sem, n):
    if not isinstance(n, int) or n > 0:
        eng.wait_ge(sem, n)


def keep_apart(eng):
    eng.nop(nofuse=True)


def flat(ap, pattern="p a b -> p (a b)"):
    return ap.rearrange(pattern)


def constants(nc, c, x_res):
    with Stage(nc, "const") as s:
        made, dv = s.sem("made"), s.sem("dv")
        ramp_i = s.sb("ramp_i", [P, 512], I32)
        block = s.block()

        @block.gpsimd
        def _(pool):
            nc.gpsimd.memset(x_res[:, NT - 1, :], 0.0).then_inc(made, 1)
            nc.gpsimd.iota(ramp_i[:, :], pattern=[[1, 512]], base=0, channel_multiplier=0).then_inc(made, 1)
            nc.gpsimd.memset(c["ident"][:, :], 0.0).then_inc(made, 1)
            nc.gpsimd.memset(c["before"][:, :], 1.0).then_inc(made, 1)
            nc.gpsimd.memset(c["upto"][:, :], 1.0).then_inc(made, 1)
            nc.gpsimd.memset(c["beyond"][:, :], 1.0).then_inc(made, 1)
            pool.wait_ge(made, 6)
            nc.gpsimd.affine_select(out=c["ident"][:, :], in_=c["ident"][:, :], compare_op=ALU.not_equal, fill=1.0,
                                    base=0, pattern=[[-1, P]], channel_multiplier=1).then_inc(made, 1)
            nc.gpsimd.affine_select(out=c["before"][:, :], in_=c["before"][:, :], compare_op=ALU.is_gt, fill=0.0,
                                    base=0, pattern=[[1, P]], channel_multiplier=-1).then_inc(made, 1)
            nc.gpsimd.affine_select(out=c["beyond"][:, :], in_=c["beyond"][:, :], compare_op=ALU.is_ge, fill=0.0,
                                    base=-TAIL, pattern=[[0, 1]], channel_multiplier=1).then_inc(made, 1)
            nc.gpsimd.affine_select(out=c["upto"][:, :], in_=c["upto"][:, :], compare_op=ALU.is_ge, fill=0.0,
                                    base=0, pattern=[[1, P]], channel_multiplier=-1).then_inc(made, 1)

        @block.vector
        def _(dve):
            nc.vector.memset(c["ones"][:, :], 1.0).then_inc(dv, 1)
            nc.vector.memset(c["ln_eps"][:, :], LN_EPS).then_inc(dv, 1)
            nc.vector.memset(c["bn_eps"][:, :], BN_EPS).then_inc(dv, 1)
            nc.vector.memset(c["minus_big"][:, :], -BIG).then_inc(dv, 1)
            dve.wait_ge(made, 10)
            nc.vector.tensor_copy(c["ramp"][:, :], ramp_i[:, :]).then_inc(dv, 1)
            nc.vector.tensor_copy(c["identb"][:, :], c["ident"][:, :]).then_inc(dv, 1)


def positions(nc, name, c, n_part, n_free, bins, tiles, bin_f, pos_f, addr_i, tile_bin, group=1, side=None):
    SIZE = group * P
    shift = SIZE.bit_length() - 1
    n = n_free
    with Stage(nc, name) as s:
        mask = s.sb("mask", [P, bins, n], BF16)
        run = s.sb("run", [P, bins, n])
        cnt, pre, base = s.sb("cnt", [P, bins]), s.sb("pre", [P, bins]), s.sb("base", [P, bins])
        padded_i, padded, end = s.sb("padded_i", [bins, 1], I32), s.sb("padded", [bins, 1]), s.sb("end", [bins, 1])
        reached = s.sb("reached", [bins, 512])
        tb = s.sb("tb", [1, 512])
        pos_i, lane = s.sb("pos_i", [P, n], I32), s.sb("lane", [P, n], I32)
        pp = s.ps("pp", [P, 4, 512])
        dv, pe_s = s.sem("dv"), s.sem("pe")
        counted, rounded, compared = s.sem("counted"), s.sem("rounded"), s.sem("compared")
        send = side(s) if side else None
        block = s.block()
        q = slice(0, n_part)
        before = c["before"]

        if send is not None:
            @block.gpsimd
            def _(pool):
                send(pool)

            if isinstance(send, Filler):
                @block.sync
                def _(sp):
                    send.sync(sp)

        @block.tensor
        def _(pe):
            pe.wait_ge(counted, 1)
            nc.tensor.matmul(pp[0:bins, 0, 0:1], cnt[q, :], c["ones"][q, 0:1], start=True, stop=True).then_inc(pe_s, 1)
            pe.wait_ge(rounded, 1)
            nc.tensor.matmul(pp[0:bins, 1, 0:1], c["upto"][0:bins, 0:bins], padded[:, :], start=True, stop=True).then_inc(pe_s, 1)
            nc.tensor.matmul(pp[:, 2, 0:bins], before[q, :], cnt[q, :], start=True, stop=False)
            nc.tensor.matmul(pp[:, 2, 0:bins], padded[:, 0:1].broadcast_to([bins, P]), before[0:bins, 0:bins],
                             start=False, stop=True).then_inc(pe_s, 1)
            pe.wait_ge(compared, 1)
            nc.tensor.matmul(pp[0:1, 3, :], c["ones"][0:bins, 0:1], reached[:, :], start=True, stop=True).then_inc(pe_s, 1)

        @block.vector
        def _(dve):
            do = Chain(dve, dv)
            v = nc.vector
            do(v.tensor_tensor(mask[q, :, :], bcast(bin_f, [[0, bins], list(bin_f.ap[1])]),
                               bcast(c["ramp"][q, :], [[1, bins], [0, n]]), ALU.is_equal))
            m2, r2 = flat(mask[q, :, :]), flat(run[q, :, :])
            do(v.tensor_tensor_scan(r2, m2, m2, 0.0, ALU.add, ALU.max))
            do(v.memset(pre[q, :], 0.0))
            do(v.tensor_scalar(pre[q, 1:bins], run[q, 0:bins - 1, n - 1], -1.0, None, ALU.mult))
            v.tensor_tensor(cnt[q, :], run[q, :, n - 1], pre[q, :], ALU.add).then_inc(counted, 1)
            dve.wait_ge(pe_s, 1)
            do(v.tensor_scalar(padded_i[:, :], pp[0:bins, 0, 0:1], float(SIZE - 1), None, ALU.add))
            do(v.tensor_scalar(padded_i[:, :], padded_i[:, :], shift, shift, ALU.logical_shift_right, ALU.logical_shift_left))
            v.tensor_copy(padded[:, :], padded_i[:, :]).then_inc(rounded, 1)
            dve.wait_ge(pe_s, 2)
            do(v.tensor_scalar(end[:, :], pp[0:bins, 1, 0:1], 1.0 / SIZE, None, ALU.mult))
            v.tensor_scalar(reached[:, :], c["ramp"][0:bins, :], end[:, 0:1], None, ALU.is_ge).then_inc(compared, 1)
            dve.wait_ge(pe_s, 3)
            do(v.scalar_tensor_tensor(out=base[q, :], in0=pre[q, :], scalar=-1.0, in1=pp[q, 2, 0:bins], op0=ALU.add, op1=ALU.add))
            do(v.tensor_tensor(run[q, :, :], run[q, :, :], base[q, :].unsqueeze(2).broadcast_to([n_part, bins, n]), ALU.add))
            do(v.tensor_tensor(run[q, :, :], run[q, :, :], mask[q, :, :], ALU.mult))
            do(v.tensor_reduce(pos_f, run[q, :, :].rearrange("p b n -> p n b"), AX.X, ALU.add))
            do(v.tensor_copy(pos_i[q, :], pos_f))
            do(v.tensor_scalar(lane[q, :], pos_i[q, :], P - 1, None, ALU.bitwise_and))
            do(v.tensor_scalar(pos_i[q, :], pos_i[q, :], 7, None, ALU.logical_shift_right))
            do(v.scalar_tensor_tensor(out=addr_i, in0=lane[q, :], scalar=float(tiles), in1=pos_i[q, :], op0=ALU.mult, op1=ALU.add))
            dve.wait_ge(pe_s, 4)
            do(v.tensor_scalar(tb[:, :], pp[0:1, 3, :], float(bins - 1), None, ALU.min))
            do(v.tensor_copy(tile_bin[:, :], tb[:, :]))


class Sender:

    def __init__(self, nc, s, table, recs, addrs, width, first, columns, chunk=8):
        self.nc, self.table, self.recs, self.addrs = nc, table, recs, addrs
        self.first, self.chunk, self.pairs = first, chunk, columns // chunk // 2
        assert self.pairs * 2 * chunk == columns
        self.send = [s.sb(f"send{u}", [P, chunk, width]) for u in range(2)]
        self.slot = [s.sb(f"slot{u}", [P, chunk], I32) for u in range(2)]
        self.staged = s.sem("staged")
        self.sent = [s.sem(f"sent{u}") for u in range(2)]

    def __call__(self, pool):
        nc, chunk = self.nc, self.chunk

        def send(i, u):
            at = bass.ds((i * 2 + u) * chunk + self.first, chunk)
            wait_positive(pool, self.sent[u], i * (16 * chunk))
            nc.gpsimd.tensor_copy(self.slot[u][0:EP, :], self.addrs[0:EP, at]).then_inc(self.staged, 1)
            nc.gpsimd.tensor_copy(self.send[u][0:EP, :, :], self.recs[0:EP, at, :]).then_inc(self.staged, 1)
            pool.wait_ge(self.staged, (i * 2 + u) * 2 + 2)
            keep_apart(pool)
            for k in range(chunk):
                nc.gpsimd.indirect_dma_start(
                    out=self.table, out_offset=bass.IndirectOffsetOnAxis(ap=self.slot[u][0:EP, k:k + 1], axis=0),
                    in_=self.send[u][0:EP, k, :], in_offset=None).then_inc(self.sent[u], 16)

        for u in range(2):
            send(0, u)
        if self.pairs > 1:
            with pool.Fori(1, self.pairs) as i:
                for u in range(2):
                    send(i, u)
        for u in range(2):
            pool.wait_ge(self.sent[u], 16 * chunk * self.pairs)


def layer_norm(nc, name, c, x_res, xnT, table=None, add=False, side=None):
    SL = 5
    assert NT % SL == 0
    with Stage(nc, name) as s:
        st = s.sb("st", [P, NT, 6])
        mean, var, t0, rstd, shift = (s.sb(k, [P, NT]) for k in ("mean", "var", "t0", "rstd", "shift"))
        row = [s.sb(f"row{u}", [P, D]) for u in range(SL)]
        pst = [s.ps(f"turned{u}", [P, 2, P]) for u in range(SL)]
        dv, seen, var_ready, std_ready = s.sem("dv"), s.sem("seen"), s.sem("var_ready"), s.sem("std_ready")
        row_ready, turned, copied, added = s.sem("row_ready"), s.sem("turned_done"), s.sem("copied"), s.sem("added")
        stored = [s.sem(f"stored{u}") for u in range(SL)]
        send = side(s) if side else None
        block = s.block()

        def tiles(eng, step):
            for u in range(SL):
                step(u, 0, u)
            with eng.Fori(1, NT // SL) as i:
                for u in range(SL):
                    step(i * SL + u, i, u)

        @block.vector
        def _(dve):
            v = nc.vector
            with dve.Fori(0, NT) as t:
                v.bn_stats(flat(st[:, bass.ds(t, 1), :]), flat(x_res[:, bass.ds(t, 1), :])).then_inc(seen, 1)
            dve.wait_ge(seen, NT)
            do = Chain(dve, dv)
            do(v.tensor_tensor(mean[:, :], st[:, :, 1], st[:, :, 4], ALU.add))
            do(v.tensor_tensor(t0[:, :], st[:, :, 1], st[:, :, 4], ALU.subtract))
            do(v.tensor_scalar(mean[:, :], mean[:, :], 0.5, None, ALU.mult))
            do(v.scalar_tensor_tensor(out=t0[:, :], in0=t0[:, :], scalar=0.25, in1=t0[:, :], op0=ALU.mult, op1=ALU.mult))
            do(v.tensor_tensor(var[:, :], st[:, :, 2], st[:, :, 5], ALU.add))
            v.scalar_tensor_tensor(out=var[:, :], in0=var[:, :], scalar=1.0 / D, in1=t0[:, :], op0=ALU.mult,
                                   op1=ALU.add).then_inc(var_ready, 1)
            dve.wait_ge(std_ready, 1)
            do(v.reciprocal(rstd[:, :], t0[:, :]))
            do(v.scalar_tensor_tensor(out=shift[:, :], in0=mean[:, :], scalar=-1.0, in1=rstd[:, :], op0=ALU.mult, op1=ALU.mult))

            def normalise(t, i, u):
                wait_positive(dve, turned, t - SL + 1)
                if table is not None:
                    wait_positive(dve, stored[u], i * 16)
                if add:
                    wait_positive(dve, added, t - SL + 1)
                x = flat(x_res[:, bass.ds(t, 1), :])
                v.tensor_scalar(row[u][:, :], x, rstd[:, bass.ds(t, 1)], shift[:, bass.ds(t, 1)], ALU.mult, ALU.add).then_inc(row_ready, 1)
                if add:
                    dve.wait_ge(row_ready, t + 1)
                    v.tensor_tensor(x, x, row[u][:, :], ALU.add).then_inc(added, 1)

            tiles(dve, normalise)

        @block.scalar
        def _(act):
            act.wait_ge(var_ready, 1)
            nc.scalar.activation(t0[:, :], var[:, :], ACT.Sqrt, bias=c["ln_eps"][:, 0:1]).then_inc(std_ready, 1)

            def keep(t, i, u):
                act.wait_ge(turned, t + 1)
                nc.scalar.activation(xnT[:, :, bass.ds(t * P, P)], pst[u][:, :, :], ACT.Copy).then_inc(copied, 1)

            tiles(act, keep)

        @block.tensor
        def _(pe):
            def turn(t, i, u):
                pe.wait_ge(row_ready, t + 1)
                wait_positive(pe, copied, t - SL + 1)
                for h in range(2):
                    ins = nc.tensor.transpose(pst[u][:, h, :], row[u][:, h * P:(h + 1) * P], c["ident"][:, :])
                ins.then_inc(turned, 1)

            tiles(pe, turn)

        if send is not None:
            @block.gpsimd
            def _(pool):
                send(pool)

        if table is not None:
            @block.sync
            def _(sp):
                view = table.rearrange("(t p) d -> t p d", p=P)

                def store(t, i, u):
                    sp.wait_ge(row_ready, t + 1)
                    keep_apart(sp)
                    sp.dma_start(view[bass.ds(t, 1)].rearrange("o p d -> (o p) d"), row[u][:, :]).then_inc(stored[u], 16)

                tiles(sp, store)
                for u in range(SL):
                    sp.wait_ge(stored[u], 16 * (NT // SL))


class Filler:

    def __init__(self, nc, s, x_in, x_res, table0, table1):
        self.nc, self.x_in, self.x_res, self.table0, self.table1 = nc, x_in, x_res, table0, table1
        self.PARTS = 28
        self.empty0, self.empty1 = s.sb("empty0", [P, ET, W0]), s.sb("empty1", [P, ET // self.PARTS, W1])
        self.cleared, self.filled = s.sem("cleared"), s.sem("filled")

    def __call__(self, pool):
        nc, cleared = self.nc, self.cleared
        nc.gpsimd.memset(self.empty0[:, :, :], 0.0).then_inc(cleared, 1)
        nc.gpsimd.memset(self.empty1[:, :, :], 0.0).then_inc(cleared, 1)
        pool.wait_ge(cleared, 2)
        nc.gpsimd.memset(self.empty0[:, :, 0:1], float(NODES)).then_inc(cleared, 1)
        nc.gpsimd.memset(self.empty0[:, :, 1:2], -1.0).then_inc(cleared, 1)
        nc.gpsimd.memset(self.empty1[:, :, NG + 1:NG + 2], -1.0).then_inc(cleared, 1)

    def sync(self, sp):
        x_in, x_res, filled, parts = self.x_in, self.x_res, self.filled, self.PARTS
        sp.dma_start(x_res[:, 0:NT - 1, :], x_in[0:(NT - 1) * P, :].rearrange("(t p) d -> p t d", p=P)).then_inc(filled, 16)
        sp.dma_start(x_res[0:TAIL, NT - 1, :], x_in[(NT - 1) * P:NODES, :]).then_inc(filled, 16)
        sp.wait_ge(self.cleared, 5)
        sp.dma_start(self.table0.rearrange("(p t) w -> p t w", p=P), self.empty0[:, :, :]).then_inc(filled, 16)
        for i in range(parts):
            sp.dma_start(self.table1.rearrange("(p i t) w -> p i t w", p=P, i=parts)[:, i], self.empty1[:, :, :]).then_inc(filled, 16)
        sp.wait_ge(filled, (3 + parts) * 16)


def edge_records(nc, c, a, x_res, rec0, rec1, pos_f, addr0, addr1, bins0, bins1, table0, table1):
    q = slice(0, EP)
    with Stage(nc, "keys") as k:
        binf0, binf1 = k.sb("binf0", [P, EJ]), k.sb("binf1", [P, EJ])
        with Stage(nc, "split") as s:
            src, dst, typ = (s.sb(n, [P, EJ], I32) for n in ("src", "dst", "typ"))
            part = s.sb("part", [P, EJ], I32)
            srcf, typf = s.sb("srcf", [P, EJ]), s.sb("typf", [P, EJ])
            attr = s.sb("attr", [P, EJ, NG])
            attr_loaded, attr_kept = s.sem("attr_loaded"), s.sem("attr_kept")
            loaded, dv, cleared = s.sem("loaded"), s.sem("dv"), s.sem("cleared")
            block = s.block()

            @block.sync
            def _(sp):
                for t, name in ((src, "src"), (dst, "dst"), (typ, "edge_type_8")):
                    sp.dma_start(t[q, :], a[name].rearrange("(p j) -> p j", p=EP)).then_inc(loaded, 16)
                sp.dma_start(attr[q, :, :], a["edge_attr_20"].rearrange("(p j) g -> p j g", p=EP)).then_inc(attr_loaded, 16)

            @block.gpsimd
            def _(pool):
                nc.gpsimd.memset(rec1[q, :, NG + 2:W1], 0.0).then_inc(cleared, 1)

            @block.scalar
            def _(act):
                act.wait_ge(attr_loaded, 16)
                nc.scalar.activation(rec1[q, :, 0:NG], attr[q, :, :], ACT.Copy).then_inc(attr_kept, 1)

            @block.vector
            def _(dve):
                v, do = nc.vector, Chain(dve, dv)
                dve.wait_ge(loaded, 48)
                v.tensor_copy(srcf[q, :], src[q, :])
                v.tensor_copy(rec1[q, :, NG], dst[q, :])
                v.tensor_copy(rec0[q, :, 2], typ[q, :])
                do(v.tensor_copy(typf[q, :], typ[q, :]))
                v.memset(rec0[q, :, 3], 0.0)
                do(v.scalar_tensor_tensor(out=rec0[q, :, 0], in0=typf[q, :], scalar=float(PADN), in1=srcf[q, :],
                                          op0=ALU.mult, op1=ALU.add))
                for key, local, binf in ((dst, rec0[q, :, 1], binf0), (src, rec1[q, :, NG + 1], binf1)):
                    do(v.tensor_scalar(part[q, :], key[q, :], P - 1, None, ALU.bitwise_and))
                    do(v.tensor_copy(local, part[q, :]))
                    do(v.tensor_scalar(part[q, :], key[q, :], 7, None, ALU.logical_shift_right))
                    do(v.tensor_copy(binf[q, :], part[q, :]))

        positions(nc, "by_dst", c, EP, EJ, NT, ET, binf0[q, :], pos_f[q, :], addr0[q, :], bins0, group=K,
                  side=lambda s: Filler(nc, s, a["x"], x_res, table0, table1))
        positions(nc, "by_src", c, EP, EJ, NT, ET, binf1[q, :], pos_f[q, :], addr1[q, :], bins1, group=K,
                  side=lambda s: Sender(nc, s, table0, rec0, addr0, W0, 0, COLS0[0]))


def project(nc, a, xnT, er, feat, rec0, addr0, table0):
    with Stage(nc, "proj") as s:
        w = s.sb("w", [P, 2, RELS, FW])
        wr = s.sb("wr", [P, 2, RELS * HEADS])
        al, ar = s.sb("al", [P, RELS, D]), s.sb("ar", [P, RELS, D])
        prod = s.sb("prod", [P, RELS * D])
        out = [s.sb(f"out{u}", [P, RELS, FW]) for u in range(2)]
        xs = [s.sb(f"xs{u}", [P, 2, P]) for u in range(2)]
        ps = [s.ps(f"ps{r}", [P, 512]) for r in range(7)]
        pe_er = s.ps("er", [P, 512])
        w_loaded, a_loaded = s.sem("w_loaded"), s.sem("a_loaded")
        dv, xs_ready = s.sem("dv"), s.sem("xs_ready")
        mm, er_done, ev_a, ev_v = s.sem("multiplied"), s.sem("er_done"), s.sem("moved_act"), s.sem("moved_dve")
        stored = [s.sem(f"stored{u}") for u in range(2)]
        send = Sender(nc, s, table0, rec0, addr0, W0, COLS0[0] + COLS0[1], COLS0[2])
        block = s.block()
        ON_ACT = 5
        MOVES_V = RELS - ON_ACT + 1

        @block.sync
        def _(sp):
            cw = a["L0_gnn_conv_weights"].rearrange("r h (c p) d -> c p r h d", p=P)
            for k in range(2):
                for r in range(RELS):
                    sp.dma_start(w[:, k, r, 0:D].rearrange("p (h d) -> p h d", h=HEADS), cw[k, :, r]).then_inc(w_loaded, 16)
            for t, name in ((al, "L0_gnn_attn_l"), (ar, "L0_gnn_attn_r")):
                sp.dma_start(flat(t[:, :, :]), rows(a[name].rearrange("r h d -> (r h d)"))).then_inc(a_loaded, 16)
            fv = feat.rearrange("(r t p) f -> t p r f", r=RELS, p=P)
            with sp.Fori(0, NT // 2) as i:
                for u in range(2):
                    sp.wait_ge(ev_a, (i * 2 + u + 1) * ON_ACT)
                    keep_apart(sp)
                    sp.wait_ge(ev_v, (i * 2 + u + 1) * MOVES_V)
                    keep_apart(sp)
                    sp.dma_start(fv[bass.ds(i * 2 + u, 1)].rearrange("a p r f -> (a p) r f"), out[u][:, :, :]).then_inc(stored[u], 16)
            for u in range(2):
                sp.wait_ge(stored[u], 16 * (NT // 2))

        @block.vector
        def _(dve):
            v, do = nc.vector, Chain(dve, dv)
            dve.wait_ge(w_loaded, 16 * 2 * RELS)
            dve.wait_ge(a_loaded, 32)
            for k in range(2):
                for vec, dest in ((al, w[:, k, :, D:FW]), (ar, wr[:, k, :].rearrange("p (r h) -> p r h", r=RELS))):
                    do(v.tensor_tensor(prod[:, :].rearrange("p (r f) -> p r f", r=RELS), w[:, k, :, 0:D], vec[:, :, :], ALU.mult))
                    do(v.tensor_reduce(dest, prod[:, :].rearrange("p (r h d) -> p r h d", r=RELS, h=HEADS), AX.X, ALU.add))

            def tiles(i):
                for u in range(2):
                    t = i * 2 + u
                    wait_positive(dve, stored[u], i * 16)
                    for r in range(ON_ACT, RELS):
                        dve.wait_ge(mm, t * RELS + r + 1)
                        v.tensor_copy(out[u][:, r, :], ps[r % 7][:, 0:FW]).then_inc(ev_v, 1)
                    dve.wait_ge(er_done, t + 1)
                    v.tensor_copy(flat(er[:, bass.ds(t, 1), :]), pe_er[:, 0:RELS * HEADS]).then_inc(ev_v, 1)

            tiles(0)
            with dve.Fori(1, NT // 2) as i:
                tiles(i)

        @block.scalar
        def _(act):
            def take(t, u):
                nc.scalar.activation(xs[u][:, :, :], xnT[:, :, bass.ds(t * P, P)], ACT.Copy).then_inc(xs_ready, 1)

            def tile(t, u, i, last=False):
                if not last:
                    wait_positive(act, er_done, t)
                    take(t + 1, 1 - u)
                wait_positive(act, stored[u], i * 16)
                for r in range(ON_ACT):
                    act.wait_ge(mm, t * RELS + r + 1)
                    nc.scalar.activation(out[u][:, r, :], ps[r][:, 0:FW], ACT.Copy).then_inc(ev_a, 1)

            take(0, 0)
            tile(0, 0, 0)
            tile(1, 1, 0)
            with act.Fori(1, NT // 2 - 1) as i:
                tile(i * 2, 0, i)
                tile(i * 2 + 1, 1, i)
            tile(NT - 2, 0, NT // 2 - 1)
            tile(NT - 1, 1, NT // 2 - 1, last=True)

        @block.tensor
        def _(pe):
            def tile(t, u, first=False):
                pe.wait_ge(xs_ready, t + 1)
                for r in range(RELS):
                    if r == RELS - 1:
                        pe.wait_ge(ev_a, t * ON_ACT + 1)
                    elif not first and r == 0:
                        pe.wait_ge(ev_v, (t - 1) * MOVES_V + RELS - ON_ACT)
                    elif not first and r < ON_ACT:
                        pe.wait_ge(ev_a, (t - 1) * ON_ACT + r + 1)
                    elif not first:
                        pe.wait_ge(ev_v, (t - 1) * MOVES_V + r - ON_ACT + 1)
                    for k in range(2):
                        ins = nc.tensor.matmul(ps[r % 7][:, 0:FW], xs[u][:, k, :], w[:, k, r, :], start=(k == 0), stop=(k == 1))
                    ins.then_inc(mm, 1)
                if not first:
                    pe.wait_ge(ev_v, t * MOVES_V)
                for k in range(2):
                    ins = nc.tensor.matmul(pe_er[:, 0:RELS * HEADS], xs[u][:, k, :], wr[:, k, :], start=(k == 0), stop=(k == 1))
                ins.then_inc(er_done, 1)

            pe.wait_ge(dv, 8)
            tile(0, 0, first=True)
            tile(1, 1)
            with pe.Fori(1, NT // 2) as i:
                tile(i * 2, 0)
                tile(i * 2 + 1, 1)

        @block.gpsimd
        def _(pool):
            send(pool)


def attend(nc, c, er, acc, rec1, addr1, table0, table1, feat, bins0):
    GROUPS, SLOTS = ET // K, 3
    H1 = HD + 1
    ON_DVE = 2
    LAST = (K - ON_DVE) * HEADS
    N_DV = (1, 5, K + 4, HEADS - 1)
    three = range(SLOTS)
    with Stage(nc, "att") as s:
        recs = s.sb("recs", [P, ET, W0])
        rowidx = s.sb("rowidx", [P, ET], I32)
        idx = [s.sb(f"idx{u}", [P, K], I32) for u in three]
        got = [s.sb(f"got{u}", [P, K, FW]) for u in three]
        oh = [s.sb(f"onehot{u}", [P, K, P]) for u in three]
        ohT = [s.sb(f"onehotT{u}", [P, K, P], BF16) for u in three]
        away = [s.sb(f"away{u}", [P, K, P], BF16) for u in three]
        typ = [s.sb(f"typ{u}", [P, K, RELS]) for u in three]
        e = [s.sb(f"e{u}", [P, K, HEADS]) for u in three]
        ehi = [s.sb(f"ehi{u}", [P, K, HEADS], BF16) for u in three]
        elo = [s.sb(f"elo{u}", [P, K, HEADS], BF16) for u in three]
        keep = [s.sb(f"keep{u}", [P, HEADS]) for u in three]
        f = [s.sb(f"f{u}", [P, K, HEADS, H1]) for u in three]
        ert = s.sb("ert", [P, K, HEADS, RELS])
        ers, z = s.sb("ers", [P, K, HEADS]), s.sb("z", [P, K, HEADS])
        tmax = s.sb("tmax", [P, K + 1, HEADS])
        mrun = s.sb("mrun", [P, NT, HEADS])
        mnew, drop = s.sb("mnew", [P, HEADS]), s.sb("drop", [P, HEADS])
        mparts = s.sb("mparts", [P, 2, HEADS], BF16)
        erparts = s.sb("erparts", [P, 3, NT, RELS * HEADS], BF16)
        rest = s.sb("rest", [P, NT, RELS * HEADS])
        below, ex = s.sb("below", [P, K, HEADS]), s.sb("ex", [P, K, HEADS])
        send, slot = s.sb("send", [P, ROUND, W1]), s.sb("slot", [P, ROUND], I32)
        pmax = [s.ps(f"pmax{k}", [P, HEADS, P]) for k in range(K)]
        pT = s.ps("pT", [P, K, P], BF16)
        per = s.ps("per", [P, K, P])
        pme = s.ps("pme", [P, K, P])
        psum = s.ps("psum", [P, 512])

        loaded, prep, dv, idx_ready = s.sem("loaded"), s.sem("prep"), s.sem("dv"), s.sem("idx_ready")
        got_s = [s.sem(f"got_s{u}") for u in three]
        oh_ready, turned, ohT_ready, away_ready = (s.sem(n) for n in ("oh_ready", "turned", "ohT_ready", "away_ready"))
        er_ready, e_ready, max_ready, drop_ready = (s.sem(n) for n in ("er_ready", "e_ready", "max_ready", "drop_ready"))
        me_ready, keep_ready, below_ready, ex_ready = (s.sem(n) for n in ("me_ready", "keep_ready", "below_ready", "ex_ready"))
        f_ready, col_ready, last_ready, sum_ready, acc_done, m_ready = s.sem("f_ready"), s.sem("col_ready"), s.sem("last_ready"), s.sem("sum_ready"), s.sem("acc_done"), s.sem("m_ready")
        staged, sent = s.sem("staged"), s.sem("sent")
        block = s.block()

        def counted(t):
            if isinstance(t, int):
                return sum(n * min(max(t - d, 0), GROUPS) for d, n in enumerate(N_DV))
            return t * sum(N_DV) - sum(n * d for d, n in enumerate(N_DV))

        def in_steps(eng, step):
            def peeled(t):
                step(t, t // 3, t % 3, {d for d in range(4) if 0 <= t - d < GROUPS})
            for t in range(6):
                peeled(t)
            with eng.Fori(2, GROUPS // 3) as i:
                for u in three:
                    step(i * 3 + u, i, u, {0, 1, 2, 3})
            for t in range(GROUPS, GROUPS + 3):
                peeled(t)

        @block.sync
        def _(sp):
            sp.dma_start(recs[:, :, :], table0.rearrange("(p t) w -> p t w", p=P)).then_inc(loaded, 16)
            sp.wait_ge(loaded, 16)

        @block.gpsimd
        def _(pool):
            def gathers(g, u, first=False):
                if not first:
                    pool.wait_ge(f_ready, g - 2)
                    pool.wait_ge(last_ready, (g - 2) * LAST)
                nc.gpsimd.tensor_copy(idx[u][:, :], rowidx[:, bass.ds(g * K, K)]).then_inc(idx_ready, 1)
                pool.wait_ge(idx_ready, g + 1)
                keep_apart(pool)
                for k in range(K):
                    nc.gpsimd.indirect_dma_start(
                        out=got[u][:, k, :], out_offset=None, in_=feat,
                        in_offset=bass.IndirectOffsetOnAxis(ap=idx[u][:, k:k + 1], axis=0)).then_inc(got_s[u], 16)

            def stage(i):
                at = bass.ds((i - 1) * ROUND, ROUND)
                wait_positive(pool, sent, (i - 1) * (16 * ROUND))
                nc.gpsimd.tensor_copy(slot[0:EP, :], addr1[0:EP, at]).then_inc(staged, 1)
                nc.gpsimd.tensor_copy(send[0:EP, :, :], rec1[0:EP, at, :]).then_inc(staged, 1)
                pool.wait_ge(staged, i * 2)
                keep_apart(pool)

            def scatter(k):
                nc.gpsimd.indirect_dma_start(
                    out=table1, out_offset=bass.IndirectOffsetOnAxis(ap=slot[0:EP, k:k + 1], axis=0),
                    in_=send[0:EP, k, :], in_offset=None).then_inc(sent, 16)

            def gather_and_scatter(i):
                stage(i)
                for u in three:
                    gathers(i * 3 + u, u)
                    for k in range(u * ROUND // 3, (u + 1) * ROUND // 3):
                        scatter(k)

            pool.wait_ge(prep, 3)
            for u in three:
                gathers(u, u, first=True)
            gather_and_scatter(1)
            with pool.Fori(2, GROUPS // 3) as i:
                gather_and_scatter(i)
            pool.wait_ge(sent, 16 * COLS1[0])

        @block.vector
        def _(dve):
            v = nc.vector
            v.memset(acc[:, :, :, :], 0.0).then_inc(prep, 1)
            v.memset(mrun[:, :, :], -BIG).then_inc(prep, 1)
            dve.wait_ge(loaded, 16)
            v.tensor_copy(rowidx[:, :], recs[:, :, 0]).then_inc(prep, 1)
            do = Chain(dve, prep)
            do.n = 3
            dve.wait_ge(prep, 3)
            do(v.tensor_copy(erparts[:, 0], er[:, :, :]))
            do(v.tensor_tensor(rest[:, :, :], er[:, :, :], erparts[:, 0], ALU.subtract))
            do(v.tensor_copy(erparts[:, 1], rest[:, :, :]))
            do(v.tensor_tensor(erparts[:, 2], rest[:, :, :], erparts[:, 1], ALU.subtract))

            def step(t, i, u, parts):
                s1, s2 = (u - 1) % 3, (u - 2) % 3
                count = Steps(dve, dv, counted(t))

                def bin_of(g):
                    return dve.value_load(bins0[0:1, bass.ds(g, 1)], min_val=0, max_val=NT - 1)

                def kinds():
                    kind = recs[:, bass.ds(t * K, K), 2]
                    count(v.tensor_tensor(typ[u][:, :, :], bcast(c["ramp"][:, 0:RELS], [[0, K], [1, RELS]]),
                                          kind.unsqueeze(2).broadcast_to([P, K, RELS]), ALU.is_equal))

                def shrink(h):
                    at = flat(acc[:, bass.ds(bin3, 1), h, :])
                    ins = v.scalar_tensor_tensor(out=at, in0=at, scalar=keep[u][:, h:h + 1], in1=psum[:, h * H1:(h + 1) * H1],
                                                 op0=ALU.mult, op1=ALU.add)
                    if h < HEADS - 1:
                        count(ins)
                    else:
                        ins.then_inc(acc_done, 1)

                if 2 in parts:
                    g = t - 2
                    count.wait()
                    for k in range(K):
                        if k == K - 1:
                            bin2 = bin_of(g)
                        dve.wait_ge(max_ready, g * K + k + 1)
                        count(v.tensor_reduce(tmax[:, k, :], pmax[k][:, :, :], AX.X, ALU.max))
                    if 3 in parts:
                        bin3 = bin_of(t - 3)
                    m = flat(mrun[:, bass.ds(bin2, 1), :])
                    count(v.tensor_scalar(tmax[:, K, :], m, 0.0, None, ALU.add))
                    wait_positive(dve, keep_ready, g)
                    wait_positive(dve, me_ready, g)
                    wait_positive(dve, m_ready, g)
                    count.wait()
                    count(v.tensor_reduce(mnew[:, :], tmax[:, :, :].rearrange("p k h -> p h k"), AX.X, ALU.max))
                    n = count.n
                    if 0 in parts:
                        kinds()
                    count.wait(n)
                    v.tensor_tensor(drop[:, :], tmax[:, K, :], mnew[:, :], ALU.subtract).then_inc(drop_ready, 1)
                    n = count(v.tensor_copy(mparts[:, 0, :], mnew[:, :]))
                    count(v.tensor_scalar(m, mnew[:, :], 0.0, None, ALU.add))
                    count.wait(n)
                    v.tensor_tensor(mparts[:, 1, :], mnew[:, :], mparts[:, 0, :], ALU.subtract).then_inc(m_ready, 1)
                elif 0 in parts:
                    kinds()
                if 1 in parts:
                    dve.wait_ge(er_ready, t)
                    count.wait()
                    n = count(v.tensor_tensor(ert[:, :, :, :], per[:, :, 0:RELS * HEADS].rearrange("p k (r h) -> p k h r", r=RELS),
                                          typ[s1][:, :, :].unsqueeze(2).broadcast_to([P, K, HEADS, RELS]), ALU.mult))
                    count.wait(n)
                    n = count(v.tensor_reduce(ers[:, :, :], ert[:, :, :, :], AX.X, ALU.add))
                    dve.wait_ge(got_s[s1], ((i + 1) if u else i) * 16 * K)
                    wait_positive(dve, below_ready, t - 3)
                    count.wait(n)
                    n = count(v.tensor_tensor(z[:, :, :], ers[:, :, :], got[s1][:, :, D:FW], ALU.add))
                    count.wait(n)
                    n = count(v.scalar_tensor_tensor(out=e[s1][:, :, :], in0=z[:, :, :], scalar=SLOPE, in1=z[:, :, :], op0=ALU.mult, op1=ALU.max))
                    count.wait(n)
                    n = count(v.tensor_copy(ehi[s1][:, :, :], e[s1][:, :, :]))
                    count.wait(n)
                    v.tensor_tensor(elo[s1][:, :, :], e[s1][:, :, :], ehi[s1][:, :, :], ALU.subtract).then_inc(e_ready, 1)
                if 2 in parts:
                    dve.wait_ge(me_ready, g + 1)
                    wait_positive(dve, col_ready, g)
                    v.tensor_tensor(below[:, :, :], e[s2][:, :, :], pme[:, :, 0:HEADS], ALU.subtract).then_inc(below_ready, 1)
                if 0 in parts:
                    wait_positive(dve, sum_ready, t - 2)
                    wait_positive(dve, away_ready, t - 2)
                    dest = recs[:, bass.ds(t * K, K), 1]
                    v.tensor_tensor(oh[u][:, :, :], bcast(c["ramp"][:, 0:P], [[0, K], [1, P]]),
                                    dest.unsqueeze(2).broadcast_to([P, K, P]), ALU.is_equal).then_inc(oh_ready, 1)
                if 3 in parts:
                    if 2 not in parts:
                        bin3 = bin_of(t - 3)
                    dve.wait_ge(keep_ready, t - 2)
                    dve.wait_ge(sum_ready, t - 2)
                    wait_positive(dve, acc_done, t - 3)
                    for h in range(HEADS):
                        shrink(h)
                if 2 in parts:
                    dve.wait_ge(ex_ready, g + 1)
                    wait_positive(dve, sum_ready, g - 2)
                    n = ON_DVE
                    v.tensor_tensor(f[s2][:, 0:n, :, 0:HD], got[s2][:, 0:n, 0:D].rearrange("p k (h d) -> p k h d", h=HEADS),
                                    ex[:, 0:n, :].unsqueeze(3).broadcast_to([P, n, HEADS, HD]), ALU.mult).then_inc(f_ready, 1)
                assert count.n == sum(N_DV[d] for d in parts)

            in_steps(dve, step)

        @block.scalar
        def _(act):
            def step(t, i, u, parts):
                s2 = (u - 2) % 3
                if 2 in parts:
                    g = t - 2
                    act.wait_ge(drop_ready, g + 1)
                    wait_positive(act, acc_done, g - 2)
                    nc.scalar.activation(keep[s2][:, :], drop[:, :], ACT.Exp).then_inc(keep_ready, 1)
                if 2 in parts:
                    act.wait_ge(below_ready, g + 1)
                    wait_positive(act, f_ready, g)
                    wait_positive(act, last_ready, g * LAST)
                    nc.scalar.activation(ex[:, :, :], below[:, :, :], ACT.Exp).then_inc(ex_ready, 1)
                    wait_positive(act, sum_ready, g - 2)
                    nc.scalar.activation(f[s2][:, :, :, HD], below[:, :, :], ACT.Exp).then_inc(col_ready, 1)
                if 0 in parts:
                    act.wait_ge(oh_ready, t + 1)
                    wait_positive(act, max_ready, (t - 2) * K)
                    nc.scalar.activation(away[u][:, :, :], oh[u][:, :, :], ACT.Identity, bias=c["minus_big"][:, 0:1], scale=BIG).then_inc(away_ready, 1)
                if 2 in parts:
                    act.wait_ge(got_s[s2], ((i + 1) if u == 2 else i) * 16 * K)
                    act.wait_ge(ex_ready, g + 1)
                    for k in range(ON_DVE, K):
                        for h in range(HEADS):
                            nc.scalar.activation(f[s2][:, k, h, 0:HD], got[s2][:, k, h * HD:(h + 1) * HD], ACT.Copy,
                                                 scale=ex[:, k, h:h + 1]).then_inc(last_ready, 1)
                if 0 in parts:
                    act.wait_ge(turned, t + 1)
                    wait_positive(act, me_ready, t - 2)
                    nc.scalar.activation(ohT[u][:, :, :], pT[:, :, :], ACT.Identity, bias=c["ones"][:, 0:1], scale=1.0 / BIG).then_inc(ohT_ready, 1)

            in_steps(act, step)

        @block.tensor
        def _(pe):
            def step(t, i, u, parts):
                s1, s2 = (u - 1) % 3, (u - 2) % 3
                if 2 in parts:
                    pe.wait_ge(m_ready, t - 1)
                    wait_positive(pe, below_ready, t - 2)
                    for k in range(K):
                        for n in range(2):
                            ins = nc.tensor.matmul(pme[:, k, 0:HEADS], ohT[s2][:, k, :], mparts[:, n, :], start=(n == 0), stop=(n == 1))
                    ins.then_inc(me_ready, 1)
                if 1 in parts:
                    pe.wait_ge(e_ready, t)
                    pe.wait_ge(away_ready, t)
                    for k in range(K):
                        nc.tensor.matmul(pmax[k][:, :, :], away[s1][:, k, :], bcast(c["identb"][:, :], [[0, HEADS], [1, P]]),
                                         start=True, stop=False, skip_group_check=True)
                        for h in range(HEADS):
                            for part in (ehi, elo):
                                ins = nc.tensor.matmul(pmax[k][:, h, :], part[s1][:, k, h:h + 1].broadcast_to([P, P]), c["identb"][:, :],
                                                       start=False, stop=(part is elo), skip_group_check=True)
                        ins.then_inc(max_ready, 1)
                if 0 in parts:
                    pe.wait_ge(away_ready, t + 1)
                    wait_positive(pe, ohT_ready, t)
                    for k in range(K):
                        ins = nc.tensor.transpose(pT[:, k, :], away[u][:, k, :], c["identb"][:, :])
                    ins.then_inc(turned, 1)
                    bin0 = pe.value_load(bins0[0:1, bass.ds(t, 1)], min_val=0, max_val=NT - 1)
                if 0 in parts:
                    pe.wait_ge(ohT_ready, t + 1)
                    wait_positive(pe, e_ready, t)
                    for k in range(K):
                        for n in range(3):
                            ins = nc.tensor.matmul(per[:, k, 0:RELS * HEADS], ohT[u][:, k, :], flat(erparts[:, n, bass.ds(bin0, 1), :]),
                                                   start=(n == 0), stop=(n == 2))
                    ins.then_inc(er_ready, 1)
                if 2 in parts:
                    g = t - 2
                    wait_positive(pe, acc_done, g)
                    pe.wait_ge(col_ready, g + 1)
                    for k in range(K):
                        if k == 0:
                            pe.wait_ge(f_ready, g + 1)
                        if k >= ON_DVE:
                            pe.wait_ge(last_ready, g * LAST + (k - ON_DVE + 1) * HEADS)
                        ins = nc.tensor.matmul(psum[:, 0:HEADS * H1], oh[s2][:, k, :], flat(f[s2][:, k, :, :]), start=(k == 0), stop=(k == K - 1))
                    ins.then_inc(sum_ready, 1)

            in_steps(pe, step)


def make_consts(s):
    return {
        "ident": s.sb("ident", [P, P]), "identb": s.sb("identb", [P, P], BF16), "ramp": s.sb("ramp", [P, 512]),
        "before": s.sb("before", [P, P]), "upto": s.sb("upto", [P, P]), "ones": s.sb("ones", [P, P]),
        "beyond": s.sb("beyond", [P, 1]), "ln_eps": s.sb("ln_eps", [P, 1]), "bn_eps": s.sb("bn_eps", [P, 1]), "minus_big": s.sb("minus_big", [P, 1]),
    }


def join_attention(nc, a, acc, x_res, side):
    with Stage(nc, "join") as s:
        rden, bias = s.sb("rden", [P, NT, HEADS]), s.sb("bias", [P, D])
        loaded, dv = s.sem("loaded"), s.sem("dv")
        send = side(s)
        block = s.block()

        @block.gpsimd
        def _(pool):
            send(pool)

        @block.sync
        def _(sp):
            sp.dma_start(bias[:, :], rows(a["L0_gnn_h_bias"])).then_inc(loaded, 16)

        @block.vector
        def _(dve):
            v, do = nc.vector, Chain(dve, dv)
            do(v.tensor_scalar(rden[:, :, :], acc[:, :, :, HD], 1e-30, None, ALU.max))
            do(v.reciprocal(rden[:, :, :], rden[:, :, :]))
            heads = acc[:, :, :, 0:HD].rearrange("p t h d -> p (t h) d")
            xh = x_res[:, :, :].rearrange("p t (h d) -> p (t h) d", h=HEADS)
            do(v.tensor_tensor(heads, heads, flat(rden[:, :, :]).unsqueeze(2).broadcast_to([P, NT * HEADS, HD]), ALU.mult))
            do(v.tensor_tensor(xh, xh, heads, ALU.add))
            dve.wait_ge(loaded, 16)
            do(v.tensor_tensor(x_res[:, :, :], x_res[:, :, :], bcast(bias[:, :], [[0, NT], [1, D]]), ALU.add))


def route(nc, name, c, experts, gate_w, gate_b, xnT, mask, top, side=None):
    E = experts
    with Stage(nc, name) as s:
        gw, gb = s.sb("gw", [P, 2, E]), s.sb("gb", [P, E])
        pr, score, down = s.sb("pr", [P, NT, E]), s.sb("score", [P, NT, E]), s.sb("down", [P, E])
        red = s.sb("red", [P, NT])
        pl = s.ps("pl", [P, NT, E])
        loaded, logits, shifted, powers, dv = (s.sem(k) for k in ("loaded", "logits", "shifted", "powers", "dv"))
        send = side(s) if side else None
        block = s.block()

        if send is not None:
            @block.gpsimd
            def _(pool):
                send(pool)

        def wide(ap):
            return ap.unsqueeze(2).broadcast_to([P, NT, E])

        @block.sync
        def _(sp):
            sp.dma_start(gw[:, :, :], gate_w.rearrange("(k p) e -> p k e", p=P)).then_inc(loaded, 16)
            sp.dma_start(gb[:, :], rows(gate_b)).then_inc(loaded, 16)

        @block.tensor
        def _(pe):
            pe.wait_ge(loaded, 32)
            for t in range(NT):
                for k in range(2):
                    ins = nc.tensor.matmul(pl[:, t, :], xnT[:, k, t * P:(t + 1) * P], gw[:, k, :], start=(k == 0), stop=(k == 1))
            ins.then_inc(logits, 1)

        @block.scalar
        def _(act):
            act.wait_ge(shifted, 1)
            nc.scalar.activation(pr[:, :, :], pr[:, :, :], ACT.Exp).then_inc(powers, 1)

        @block.vector
        def _(dve):
            v, do = nc.vector, Chain(dve, dv)
            do(v.tensor_scalar(down[:, :], c["ramp"][:, 0:E], -1.0, float(E), ALU.mult, ALU.add))
            dve.wait_ge(loaded, 32)
            dve.wait_ge(logits, 1)
            do(v.tensor_tensor(pr[:, :, :], pl[:, :, :], bcast(gb[:, :], [[0, NT], [1, E]]), ALU.add))
            do(v.tensor_reduce(red[:, :], pr[:, :, :], AX.X, ALU.max))
            v.tensor_tensor(pr[:, :, :], pr[:, :, :], wide(red[:, :]), ALU.subtract).then_inc(shifted, 1)
            dve.wait_ge(powers, 1)
            do(v.tensor_reduce(red[:, :], pr[:, :, :], AX.X, ALU.add))
            do(v.reciprocal(red[:, :], red[:, :]))
            do(v.tensor_tensor(pr[:, :, :], pr[:, :, :], wide(red[:, :]), ALU.mult))
            for k in range(2):
                do(v.tensor_reduce(top[k][:, :], pr[:, :, :], AX.X, ALU.max))
                do(v.tensor_tensor(score[:, :, :], pr[:, :, :], wide(top[k][:, :]), ALU.is_equal))
                do(v.tensor_tensor(score[:, :, :], score[:, :, :], bcast(down[:, :], [[0, NT], [1, E]]), ALU.mult))
                do(v.tensor_reduce(red[:, :], score[:, :, :], AX.X, ALU.max))
                do(v.tensor_tensor(mask[k][:, :, :], score[:, :, :], wide(red[:, :]), ALU.is_equal))
                if k == 0:
                    do(v.scalar_tensor_tensor(out=pr[:, :, :], in0=mask[0][:, :, :], scalar=-2.0, in1=pr[:, :, :],
                                              op0=ALU.mult, op1=ALU.add))


def mixture(nc, c, a, xnT, x_res, side):
    G, N = 3, 3 * P
    with Stage(nc, "mix") as S:
        mask = [S.sb(f"mask{k}", [P, NT, EX0]) for k in range(2)]
        top = [S.sb(f"top{k}", [P, NT]) for k in range(2)]
        route(nc, "route0", c, EX0, a["L0_ffn_gW"], a["L0_ffn_gb"], xnT, mask, top, side(2))
        with Stage(nc, "mixf") as s:
            gate = s.sb("gate", [P, NT, EX0])
            w1, w2, w3 = s.sb("w1", [P, 2, 2 * P]), s.sb("w2", [P, 2, P]), s.sb("w3", [P, D])
            e1w, e2w, e3w = s.sb("e1w", [P, EX0, 2, P]), s.sb("e2w", [P, EX0, 64]), s.sb("e3w", [65, EX0, D])
            b1, b2, b3 = s.sb("b1", [P, 2]), s.sb("b2", [P, 1]), s.sb("b3", [P, D])
            eb1, eb2 = s.sb("eb1", [P, EX0]), s.sb("eb2", [64, EX0])
            s1, s2 = s.sb("s1", [P, 2, N]), s.sb("s2", [P, N])
            h1, h2 = s.sb("h1", [P, EX0, N]), s.sb("h2", [65, EX0, N])
            order1, order2, outs = [0, 1, 2, 3, 4, 5], [6, 7, 0, 1, 2], [[3, 4, 5], [6, 7, 0], [1, 2, 3]]
            every = order1 + order2 + sum(outs, [])
            banks = [s.ps(f"bank{b}", [P, 512]) for b in range(8)]
            loaded, dv, biased = s.sem("loaded"), s.sem("dv"), s.sem("biased")
            drop_ready, power_ready = s.sem("drop_ready"), s.sem("power_ready")
            l1, l2, l3 = s.sem("layer1"), s.sem("layer2"), s.sem("layer3")
            r1, r2 = s.sem("relu1"), s.sem("relu2")
            added = s.sem("added")
            send = side(3)(s)
            block = s.block()
            loads = [
                (w1[:, :, :], a["L0_ffn_sW1"].rearrange("(k p) n -> p k n", p=P)),
                (w2[:, :, :], a["L0_ffn_sW2"].rearrange("(k p) n -> p k n", p=P)),
                (w3[:, :], a["L0_ffn_sW3"]),
                (e1w[:, :, :, :].rearrange("p e k n -> p (e k) n"), a["L0_ffn_eW1"].rearrange("e (k p) n -> p (e k) n", p=P)),
                (e2w[:, :, :], a["L0_ffn_eW2"].rearrange("e p n -> p e n")),
                (e3w[0:64, :, :], a["L0_ffn_eW3"].rearrange("e p n -> p e n")),
                (e3w[64:65, :, :], a["L0_ffn_eb3"].rearrange("(o e) n -> o e n", o=1)),
                (b1[:, :], a["L0_ffn_sb1"].rearrange("(k p) -> p k", p=P)),
                (b2[:, :], a["L0_ffn_sb2"].rearrange("(p o) -> p o", o=1)),
                (eb1[:, :], a["L0_ffn_eb1"].rearrange("e p -> p e")),
                (eb2[:, :], a["L0_ffn_eb2"].rearrange("e p -> p e")),
                (b3[:, :], rows(a["L0_ffn_sb3"])),
            ]
            LOADED = 16 * len(loads)

            @block.sync
            def _(sp):
                with nc.allow_non_contiguous_dma(reason="small biases"):
                    for dest, source in loads:
                        sp.dma_start(dest, source).then_inc(loaded, 16)

            @block.gpsimd
            def _(pool):
                nc.gpsimd.memset(h2[64:65, :, :], 1.0).then_inc(biased, 1)
                pool.wait_ge(biased, 1)
                pool.wait_ge(loaded, LOADED)
                nc.gpsimd.tensor_tensor(x_res[:, :, :], x_res[:, :, :], bcast(b3[:, :], [[0, NT], [1, D]]), ALU.add).then_inc(biased, 1)
                send(pool)

            def wait_free(eng, i, q, first):
                before = [p for p in range(q) if every[p] == every[q]]
                if not before:
                    if first:
                        return
                    i, before = i - 1, [p for p in range(len(every)) if every[p] == every[q]]
                p = before[-1]
                if p < 6:
                    eng.wait_ge(r1, i * 6 + p + 1)
                elif p < 11:
                    eng.wait_ge(r2, i * 5 + p - 5)
                else:
                    t, m = divmod(p - 11, 3)
                    eng.wait_ge(added, i * G * 5 + t * 5 + min(2 * m + 2, 5))

            @block.tensor
            def _(pe):
                pe.wait_ge(loaded, LOADED)
                pe.wait_ge(biased, 1)

                def group(i, first=False):
                    cols = [xnT[:, k, bass.ds(i * N, N)] for k in range(2)]
                    for j, w in enumerate([w1[:, :, 0:P], w1[:, :, P:2 * P]] + [e1w[:, e, :, :] for e in range(EX0)]):
                        wait_free(pe, i, j, first)
                        b = order1[j]
                        for k in range(2):
                            ins = nc.tensor.matmul(banks[b][:, 0:N], w[:, k, :], cols[k], start=(k == 0), stop=(k == 1))
                        ins.then_inc(l1, 1)
                    for j in range(5):
                        wait_free(pe, i, 6 + j, first)
                        b = order2[j]
                        pe.wait_ge(r1, i * 6 + 2 + j)
                        if j == 0:
                            for k in range(2):
                                ins = nc.tensor.matmul(banks[b][:, 0:N], w2[:, k, :], s1[:, k, :], start=(k == 0), stop=(k == 1))
                        else:
                            ins = nc.tensor.matmul(banks[b][0:64, 0:N], e2w[:, j - 1, :], h1[:, j - 1, :], start=True, stop=True)
                        ins.then_inc(l2, 1)
                    pe.wait_ge(r2, i * 5 + 5)
                    for t in range(G):
                        for m in range(3):
                            wait_free(pe, i, 11 + 3 * t + m, first)
                            b = outs[t][m]
                            for o in range(2 * m, min(2 * m + 2, 5)):
                                half = banks[b][:, (o % 2) * D:(o % 2 + 1) * D]
                                if o == 0:
                                    ins = nc.tensor.matmul(half, s2[:, t * P:(t + 1) * P], w3[:, :], start=True, stop=True)
                                else:
                                    ins = nc.tensor.matmul(half, h2[:, o - 1, t * P:(t + 1) * P], e3w[:, o - 1, :], start=True, stop=True)
                            ins.then_inc(l3, 1)

                group(0, first=True)
                with pe.Fori(1, NT // G) as i:
                    group(i)

            @block.scalar
            def _(act):
                act.wait_ge(loaded, LOADED)
                act.wait_ge(drop_ready, 1)
                nc.scalar.activation(top[1][:, :], top[1][:, :], ACT.Exp).then_inc(power_ready, 1)

                def group(i, first=False):
                    for j in range(6):
                        act.wait_ge(l1, i * 6 + j + 1)
                        if not first:
                            act.wait_ge(l2, (i - 1) * 5 + max(j, 1))
                        dest, bias = (s1[:, j, :], b1[:, j:j + 1]) if j < 2 else (h1[:, j - 2, :], eb1[:, j - 2:j - 1])
                        nc.scalar.activation(dest, banks[order1[j]][:, 0:N], ACT.Relu, bias=bias).then_inc(r1, 1)
                    for j in range(5):
                        act.wait_ge(l2, i * 5 + j + 1)
                        if not first:
                            act.wait_ge(l3, i * 9)
                        bank = banks[order2[j]]
                        if j == 0:
                            nc.scalar.activation(s2[:, :], bank[:, 0:N], ACT.Relu, bias=b2[:, 0:1]).then_inc(r2, 1)
                        else:
                            nc.scalar.activation(h2[0:64, j - 1, :], bank[0:64, 0:N], ACT.Relu, bias=eb2[:, j - 1:j]).then_inc(r2, 1)

                group(0, first=True)
                with act.Fori(1, NT // G) as i:
                    group(i)

            @block.vector
            def _(dve):
                v, do = nc.vector, Chain(dve, dv)
                v.tensor_tensor(top[1][:, :], top[1][:, :], top[0][:, :], ALU.subtract).then_inc(drop_ready, 1)
                dve.wait_ge(power_ready, 1)
                do(v.tensor_scalar(top[0][:, :], top[1][:, :], 1.0, None, ALU.add))
                do(v.reciprocal(top[0][:, :], top[0][:, :]))
                do(v.tensor_tensor(top[1][:, :], top[1][:, :], top[0][:, :], ALU.mult))
                for k in range(2):
                    do(v.tensor_tensor(mask[k][:, :, :], mask[k][:, :, :], top[k][:, :].unsqueeze(2).broadcast_to([P, NT, EX0]), ALU.mult))
                do(v.tensor_tensor(gate[:, :, :], mask[0][:, :, :], mask[1][:, :, :], ALU.add))
                dve.wait_ge(biased, 2)
                def group(i):
                    count = Steps(dve, added, i * G * 5)
                    for t in range(G):
                        x = flat(x_res[:, bass.ds(i * G + t, 1), :])
                        for o in range(5):
                            b = outs[t][o // 2]
                            half = banks[b][:, (o % 2) * D:(o % 2 + 1) * D]
                            if o % 2 == 0:
                                dve.wait_ge(l3, i * 9 + 3 * t + o // 2 + 1)
                            count.wait()
                            if o == 0:
                                count(v.tensor_tensor(x, x, half, ALU.add))
                            else:
                                count(v.scalar_tensor_tensor(out=x, in0=half, scalar=gate[:, bass.ds(i * G + t, 1), o - 1],
                                                             in1=x, op0=ALU.mult, op1=ALU.add))

                group(0)
                with dve.Fori(1, NT // G) as i:
                    group(i)


def turn_rows(nc, name, c, src, dstT):
    with Stage(nc, name) as s:
        row = [s.sb(f"row{u}", [P, D]) for u in range(2)]
        pt = [s.ps(f"pt{u}", [P, 2, P]) for u in range(2)]
        taken, turned, copied = s.sem("taken"), s.sem("turned"), s.sem("copied")
        block = s.block()

        def pairs(eng, step):
            for u in range(2):
                step(0, u, True)
            with eng.Fori(1, NT // 2) as i:
                for u in range(2):
                    step(i, u, False)

        @block.vector
        def _(dve):
            def step(i, u, first):
                if not first:
                    dve.wait_ge(turned, i * 2 + u - 1)
                nc.vector.tensor_scalar(row[u][:, :], flat(src[:, bass.ds(i * 2 + u, 1), :]), 1.0, None, ALU.mult).then_inc(taken, 1)
            pairs(dve, step)

        @block.tensor
        def _(pe):
            def step(i, u, first):
                pe.wait_ge(taken, i * 2 + u + 1)
                if not first:
                    pe.wait_ge(copied, i * 2 + u - 1)
                for h in range(2):
                    ins = nc.tensor.transpose(pt[u][:, h, :], row[u][:, h * P:(h + 1) * P], c["ident"][:, :])
                ins.then_inc(turned, 1)
            pairs(pe, step)

        @block.scalar
        def _(act):
            def step(i, u, first):
                act.wait_ge(turned, i * 2 + u + 1)
                nc.scalar.activation(dstT[:, :, bass.ds((i * 2 + u) * P, P)], pt[u][:, :, :], ACT.Copy).then_inc(copied, 1)
            pairs(act, step)


def convolve(nc, c, a, agg, table1, xtab, bins1):
    GROUPS, SLOTS = ET // K, 3
    N = K * P
    ROWS = 6 * NG
    with Stage(nc, "conv") as s:
        two, three = range(2), range(SLOTS)
        recs = s.sb("recs", [P, ET, W1])
        rowidx = s.sb("rowidx", [P, ET], I32)
        wf1, wf1_rest = s.sb("wf1", [NG, D]), s.sb("wf1_rest", [NG, D])
        wparts, wrows = s.sb("wparts", [NG, 3, D], BF16), s.sb("wrows", [ROWS, D], BF16)
        wf2 = s.sb("wf2", [P, 2, D])
        bf1, bf2 = s.sb("bf1", [P, 2]), s.sb("bf2", [P, D])
        idx = [s.sb(f"idx{u}", [P, K], I32) for u in three]
        got = [s.sb(f"got{u}", [P, K, D]) for u in three]
        attr = [s.sb(f"attr{u}", [P, K, 3, 2, NG], BF16) for u in three]
        rest = s.sb("rest", [P, K, NG])
        attrT = [s.sb(f"attrT{u}", [ROWS, N], BF16) for u in three]
        act1 = [s.sb(f"act1{u}", [P, 2, N]) for u in three]
        oh = [s.sb(f"onehot{u}", [P, K, P]) for u in three]
        filt = s.sb("filt", [P, K, D])
        msg = [s.sb(f"msg{u}", [P, K, D]) for u in three]
        pT = s.ps("pT", [ROWS, N], BF16)
        p1 = [s.ps(f"p1{h}", [P, N]) for h in two]
        pf = [s.ps(f"pf{h}", [P, 2, D]) for h in two]
        psum = [s.ps(f"psum{u}", [P, 512]) for u in three]
        loaded, prep, w_cut, w_placed, dv = (s.sem(n) for n in ("loaded", "prep", "w_cut", "w_placed", "dv"))
        idx_ready, h_ready, attr_ready, turned, attrT_ready = (s.sem(n) for n in ("idx_ready", "h_ready", "attr_ready", "turned", "attrT_ready"))
        layer1, act_ready, filtered, oh_ready = (s.sem(n) for n in ("layer1", "act_ready", "filtered", "oh_ready"))
        filt_ready, msg_ready, summed, agg_done = (s.sem(n) for n in ("filt_ready", "msg_ready", "summed", "agg_done"))
        got_s = [s.sem(f"got_s{u}") for u in three]
        block = s.block()
        LOADED = 16 * 5

        def in_steps(eng, step):
            def peeled(t):
                step(t, t // 3, t % 3, {d for d in range(6) if 0 <= t - d < GROUPS})
            for t in range(6):
                peeled(t)
            with eng.Fori(2, GROUPS // 3) as i:
                for u in three:
                    step(i * 3 + u, i, u, {0, 1, 2, 3, 4, 5})
            for t in range(GROUPS, GROUPS + 5):
                peeled(t)

        @block.sync
        def _(sp):
            sp.dma_start(wf1[:, :], a["L1_gnn_Wf1"]).then_inc(loaded, 16)
            sp.dma_start(recs[:, :, :], table1.rearrange("(p t) w -> p t w", p=P)).then_inc(loaded, 16)
            sp.dma_start(wf2[:, :, :], a["L1_gnn_Wf2"].rearrange("(k p) n -> p k n", p=P)).then_inc(loaded, 16)
            with nc.allow_non_contiguous_dma(reason="a small bias"):
                sp.dma_start(bf1[:, :], a["L1_gnn_bf1"].rearrange("(k p) -> p k", p=P)).then_inc(loaded, 16)
            sp.dma_start(bf2[:, :], rows(a["L1_gnn_bf2"])).then_inc(loaded, 16)
            sp.wait_ge(w_cut, 4)
            for place, part in enumerate((0, 0, 1, 1, 2, 0)):
                sp.dma_start(wrows[place * NG:(place + 1) * NG, :], wparts[:, part, :]).then_inc(w_placed, 16)

        @block.gpsimd
        def _(pool):
            nc.gpsimd.memset(agg[:, :, :], 0.0).then_inc(prep, 1)
            pool.wait_ge(prep, 2)

            def gathers(g, i, u):
                wait_positive(pool, msg_ready, (g - 2) * 2)
                nc.gpsimd.tensor_copy(idx[u][:, :], rowidx[:, bass.ds(g * K, K)]).then_inc(idx_ready, 1)
                pool.wait_ge(idx_ready, g + 1)
                keep_apart(pool)
                for k in range(K):
                    nc.gpsimd.indirect_dma_start(
                        out=got[u][:, k, :], out_offset=None, in_=xtab,
                        in_offset=bass.IndirectOffsetOnAxis(ap=idx[u][:, k:k + 1], axis=0)).then_inc(got_s[u], 16)

            for u in three:
                gathers(u, 0, u)
            with pool.Fori(1, GROUPS // 3) as i:
                for u in three:
                    gathers(i * 3 + u, i, u)

        @block.scalar
        def _(act):
            act.wait_ge(loaded, LOADED)

            def step(t, i, u, parts):
                s1, s2 = (u - 1) % 3, (u - 2) % 3
                if 0 in parts:
                    wait_positive(act, turned, t - 2)
                    source = recs[:, bass.ds(t * K, K), 0:NG].unsqueeze(2).broadcast_to([P, K, 3, NG])
                    nc.scalar.activation(attr[u][:, :, :, 0, :], source, ACT.Copy).then_inc(h_ready, 1)
                if 2 in parts:
                    for h in two:
                        act.wait_ge(layer1, (t - 2) * 2 + h + 1)
                        wait_positive(act, filtered, (t - 4) * 2)
                        nc.scalar.activation(act1[s2][:, h, :], p1[h][:, :], ACT.Silu, bias=bf1[:, h:h + 1]).then_inc(act_ready, 1)
                if 1 in parts:
                    act.wait_ge(turned, t)
                    wait_positive(act, layer1, (t - 3) * 2)
                    nc.scalar.activation(attrT[s1][:, :], pT[:, :], ACT.Copy).then_inc(attrT_ready, 1)

            in_steps(act, step)

        @block.tensor
        def _(pe):
            pe.wait_ge(loaded, LOADED)
            pe.wait_ge(w_placed, 16 * 6)

            def step(t, i, u, parts):
                s1, s2, s3, s4 = ((u - d) % 3 for d in range(1, 5))
                if 1 in parts:
                    pe.wait_ge(attr_ready, t)
                    wait_positive(pe, attrT_ready, t - 1)
                    for k in range(K):
                        ins = nc.tensor.transpose(pT[:, k * P:(k + 1) * P], flat(attr[s1][:, k, :, :, :], "p a b n -> p (a b n)"), c["identb"][:, :])
                    ins.then_inc(turned, 1)
                if 2 in parts:
                    pe.wait_ge(attrT_ready, t - 1)
                    for h in two:
                        if not isinstance(t, int) or t > 2:
                            pe.wait_ge(act_ready, (t - 3) * 2 + h + 1)
                        nc.tensor.matmul(p1[h][:, :], wrows[:, h * P:(h + 1) * P], attrT[s2][:, :], start=True, stop=True).then_inc(layer1, 1)
                if 3 in parts:
                    pe.wait_ge(act_ready, (t - 2) * 2)
                    for b in two:
                        if not isinstance(t, int) or t > 3:
                            pe.wait_ge(filt_ready, (t - 4) * 2 + b + 1)
                        for k in two:
                            for h in two:
                                ins = nc.tensor.matmul(pf[b][:, k, :], act1[s3][:, h, (2 * b + k) * P:(2 * b + k + 1) * P], wf2[:, h, :],
                                                       start=(h == 0), stop=(h == 1))
                        ins.then_inc(filtered, 1)
                if 4 in parts:
                    pe.wait_ge(oh_ready, t - 3)
                    wait_positive(pe, agg_done, t - 6)
                    for k in range(K):
                        if k % 2 == 0:
                            pe.wait_ge(msg_ready, (t - 4) * 2 + k // 2 + 1)
                        ins = nc.tensor.matmul(psum[s4][:, 0:D], oh[s4][:, k, :], msg[s4][:, k, :], start=(k == 0), stop=(k == K - 1))
                    ins.then_inc(summed, 1)

            in_steps(pe, step)

        @block.vector
        def _(dve):
            v, cut = nc.vector, Chain(dve, w_cut)
            dve.wait_ge(loaded, LOADED)
            cut(v.tensor_copy(wparts[:, 0, :], wf1[:, :]))
            cut(v.tensor_tensor(wf1_rest[:, :], wf1[:, :], wparts[:, 0, :], ALU.subtract))
            cut(v.tensor_copy(wparts[:, 1, :], wf1_rest[:, :]))
            cut(v.tensor_tensor(wparts[:, 2, :], wf1_rest[:, :], wparts[:, 1, :], ALU.subtract))
            v.tensor_copy(rowidx[:, :], recs[:, :, NG]).then_inc(prep, 1)

            def step(t, i, u, parts):
                s3, s5 = u, (u - 5) % 3
                if 5 in parts:
                    bin5 = dve.value_load(bins1[0:1, bass.ds(t - 5, 1)], min_val=0, max_val=NT - 1)
                if 3 in parts:
                    g = t - 3
                    node = recs[:, bass.ds(g * K, K), NG + 1]
                    wait_positive(dve, summed, t - 5)
                    v.tensor_tensor(oh[s3][:, :, :], bcast(c["ramp"][:, 0:P], [[0, K], [1, P]]),
                                    node.unsqueeze(2).broadcast_to([P, K, P]), ALU.is_equal).then_inc(oh_ready, 1)
                if 0 in parts:
                    count = Steps(dve, dv, t * 2)
                    dve.wait_ge(h_ready, t + 1)
                    wait_positive(dve, attr_ready, t)
                    count(v.tensor_tensor(rest[:, :, :], recs[:, bass.ds(t * K, K), 0:NG], attr[u][:, :, 0, 0, :], ALU.subtract))
                    count.wait()
                    count(v.tensor_copy(attr[u][:, :, 0:2, 1, :], rest[:, :, :].unsqueeze(2).broadcast_to([P, K, 2, NG])))
                    count.wait()
                    v.tensor_tensor(attr[u][:, :, 2, 1, :], rest[:, :, :], attr[u][:, :, 0, 1, :], ALU.subtract).then_inc(attr_ready, 1)
                if 3 in parts:
                    wait_positive(dve, msg_ready, g * 2)
                    for b in two:
                        dve.wait_ge(filtered, g * 2 + b + 1)
                        part = filt[:, 2 * b:2 * b + 2, :]
                        v.tensor_tensor(part, pf[b][:, :, :], bcast(bf2[:, :], [[0, 2], [1, D]]), ALU.add).then_inc(filt_ready, 1)
                    dve.wait_ge(got_s[s3], i * 16 * K)
                    for b in two:
                        dve.wait_ge(filt_ready, g * 2 + b + 1)
                        part = slice(2 * b, 2 * b + 2)
                        v.tensor_tensor(msg[s3][:, part, :], filt[:, part, :], got[s3][:, part, :], ALU.mult).then_inc(msg_ready, 1)
                if 5 in parts:
                    dve.wait_ge(summed, t - 4)
                    wait_positive(dve, agg_done, t - 5)
                    at = flat(agg[:, bass.ds(bin5, 1), :])
                    v.tensor_tensor(at, at, psum[s5][:, 0:D], ALU.add).then_inc(agg_done, 1)

            dve.wait_ge(prep, 2)
            in_steps(dve, step)


def update(nc, c, a, aggT, x_res):
    G, N = 10, PADN // 10
    BN, BC = 10, NODES // 10
    with Stage(nc, "upd") as s:
        w1, w2 = s.sb("w1", [P, 2, D]), s.sb("w2", [P, 2, D])
        b1, b2, gamma, beta = (s.sb(n, [P, 2]) for n in ("b1", "b2", "gamma", "beta"))
        h1 = s.sb("h1", [P, 2, N])
        hT = s.sb("hT", [P, 2, PADN])
        st, mv = s.sb("st", [P, 2, BN, 6]), s.sb("mv", [P, 2, 2])
        scale, shift = s.sb("scale", [P, 2]), s.sb("shift", [P, 2])
        col = [s.sb(f"col{u}", [P, 2, P]) for u in range(2)]
        p1 = [s.ps(f"p1{h}", [P, N]) for h in range(2)]
        p2 = [s.ps(f"p2{h}", [P, N]) for h in range(2)]
        pt = [s.ps(f"pt{u}", [P, D]) for u in range(2)]
        names = ("loaded", "dv", "layer1", "act1", "layer2", "kept", "var_ready", "std_ready", "scale_ready",
                 "taken", "turned", "joined")
        loaded, dv, layer1, act1, layer2, kept, var_ready, std_ready, scale_ready, taken, turned, joined = (s.sem(n) for n in names)
        block = s.block()
        loads = [
            (w1[:, :, :], a["L1_gnn_Wu1"].rearrange("(k p) n -> p k n", p=P)),
            (w2[:, :, :], a["L1_gnn_Wu2"].rearrange("(k p) n -> p k n", p=P)),
            (b1[:, :], a["L1_gnn_bu1"].rearrange("(k p) -> p k", p=P)), (b2[:, :], a["L1_gnn_bu2"].rearrange("(k p) -> p k", p=P)),
            (gamma[:, :], a["L1_gnn_gamma"].rearrange("(k p) -> p k", p=P)), (beta[:, :], a["L1_gnn_beta"].rearrange("(k p) -> p k", p=P)),
        ]

        @block.sync
        def _(sp):
            with nc.allow_non_contiguous_dma(reason="small vectors"):
                for dest, source in loads:
                    sp.dma_start(dest, source).then_inc(loaded, 16)

        @block.tensor
        def _(pe):
            pe.wait_ge(loaded, 16 * len(loads))

            def group(i, first):
                for h in range(2):
                    if not first:
                        pe.wait_ge(act1, (i - 1) * 2 + h + 1)
                    for k in range(2):
                        ins = nc.tensor.matmul(p1[h][:, :], w1[:, k, h * P:(h + 1) * P], aggT[:, k, bass.ds(i * N, N)], start=(k == 0), stop=(k == 1))
                    ins.then_inc(layer1, 1)
                pe.wait_ge(act1, i * 2 + 2)
                for h in range(2):
                    if not first:
                        pe.wait_ge(kept, (i - 1) * 2 + h + 1)
                    for k in range(2):
                        ins = nc.tensor.matmul(p2[h][:, :], w2[:, k, h * P:(h + 1) * P], h1[:, k, :], start=(k == 0), stop=(k == 1))
                    ins.then_inc(layer2, 1)

            group(0, True)
            with pe.Fori(1, G) as i:
                group(i, False)

            def turn(i, u, first):
                pe.wait_ge(taken, (i * 2 + u + 1) * 2)
                if not first:
                    pe.wait_ge(joined, i * 2 + u - 1)
                for h in range(2):
                    ins = nc.tensor.transpose(pt[u][:, h * P:(h + 1) * P], col[u][:, h, :], c["ident"][:, :])
                ins.then_inc(turned, 1)

            for u in range(2):
                turn(0, u, True)
            with pe.Fori(1, NT // 2) as i:
                for u in range(2):
                    turn(i, u, False)

        @block.scalar
        def _(act):
            act.wait_ge(loaded, 16 * len(loads))

            def group(i, first):
                for h in range(2):
                    act.wait_ge(layer1, i * 2 + h + 1)
                    if not first:
                        act.wait_ge(layer2, (i - 1) * 2 + 2)
                    nc.scalar.activation(h1[:, h, :], p1[h][:, :], ACT.Silu, bias=b1[:, h:h + 1]).then_inc(act1, 1)

            group(0, True)
            with act.Fori(1, G) as i:
                group(i, False)
            act.wait_ge(var_ready, 1)
            nc.scalar.activation(scale[:, :], mv[:, :, 1], ACT.Sqrt, bias=c["bn_eps"][:, 0:1]).then_inc(std_ready, 1)
            act.wait_ge(scale_ready, 1)

            def take(i, u, first):
                if not first:
                    act.wait_ge(turned, i * 2 + u - 1)
                for h in range(2):
                    ins = nc.scalar.activation(col[u][:, h, :], hT[:, h, bass.ds((i * 2 + u) * P, P)], ACT.Identity,
                                               bias=shift[:, h:h + 1], scale=scale[:, h:h + 1])
                    ins.then_inc(taken, 1)

            for u in range(2):
                take(0, u, True)
            with act.Fori(1, NT // 2) as i:
                for u in range(2):
                    take(i, u, False)

        @block.vector
        def _(dve):
            v, do = nc.vector, Chain(dve, dv)
            dve.wait_ge(loaded, 16 * len(loads))
            with dve.Fori(0, G) as i:
                for h in range(2):
                    dve.wait_ge(layer2, i * 2 + h + 1)
                    v.tensor_scalar(hT[:, h, bass.ds(i * N, N)], p2[h][:, :], b2[:, h:h + 1], None, ALU.add).then_inc(kept, 1)
            dve.wait_ge(kept, 2 * G)
            for h in range(2):
                for j in range(BN):
                    do(v.bn_stats(st[:, h, j, :], hT[:, h, j * BC:(j + 1) * BC]))
                do(v.bn_aggr(mv[:, h, :], st[:, h, :, :]))
            v.memset(shift[:, :], 0.0).then_inc(var_ready, 1)
            dve.wait_ge(std_ready, 1)
            dve.wait_ge(var_ready, 1)
            do(v.reciprocal(scale[:, :], scale[:, :]))
            do(v.tensor_tensor(scale[:, :], scale[:, :], gamma[:, :], ALU.mult))
            do(v.tensor_tensor(shift[:, :], mv[:, :, 0], scale[:, :], ALU.mult))
            v.tensor_tensor(shift[:, :], beta[:, :], shift[:, :], ALU.subtract).then_inc(scale_ready, 1)
            with dve.Fori(0, NT // 2) as i:
                for u in range(2):
                    dve.wait_ge(turned, i * 2 + u + 1)
                    x = flat(x_res[:, bass.ds(i * 2 + u, 1), :])
                    v.tensor_tensor(x, x, pt[u][:, :], ALU.add).then_inc(joined, 1)


def routed(nc, c, a, xnT, x_res, xtab, slots, results):
    with Stage(nc, "rt") as S:
        mask = [S.sb(f"mask{k}", [P, NT, EX1]) for k in range(2)]
        top = [S.sb(f"top{k}", [P, NT]) for k in range(2)]
        bin_f, pos_f = S.sb("bin_f", [P, 2 * NT]), S.sb("pos_f", [P, 2 * NT])
        addr_i, pos_i = S.sb("addr_i", [P, 2 * NT], I32), S.sb("pos_i", [P, 2 * NT], I32)
        expert = S.sb("expert", [1, 512], I32)
        token = S.sb("token", [P, NT], I32)
        route(nc, "route1", c, EX1, a["L1_ffn_gate_w"], a["L1_ffn_gate_b"], xnT, mask, top)

        with Stage(nc, "pick") as s:
            tmp, red = s.sb("tmp", [P, NT, EX1]), s.sb("red", [P, NT])
            empty = s.sb("empty", [P, MT], I32)
            dv, cleared, filled = s.sem("dv"), s.sem("cleared"), s.sem("filled")
            block = s.block()

            @block.gpsimd
            def _(pool):
                nc.gpsimd.memset(empty[:, :], 0).then_inc(cleared, 1)
                nc.gpsimd.iota(token[:, :], pattern=[[P, NT]], base=0, channel_multiplier=1).then_inc(cleared, 1)

            @block.sync
            def _(sp):
                sp.wait_ge(cleared, 2)
                sp.dma_start(slots.rearrange("(p t) o -> p (t o)", p=P), empty[:, :]).then_inc(filled, 16)
                sp.wait_ge(filled, 16)

            @block.vector
            def _(dve):
                v, do = nc.vector, Chain(dve, dv)
                bins = bin_f[:, :].rearrange("p (k t) -> p k t", k=2)
                for k in range(2):
                    do(v.tensor_tensor(tmp[:, :, :], mask[k][:, :, :], bcast(c["ramp"][:, 0:EX1], [[0, NT], [1, EX1]]), ALU.mult))
                    do(v.tensor_reduce(bins[:, k, :], tmp[:, :, :], AX.X, ALU.add))
                    last = bins[:, k, NT - 1:NT]
                    do(v.scalar_tensor_tensor(out=last, in0=c["beyond"][:, :], scalar=100.0, in1=last, op0=ALU.mult, op1=ALU.add))
                do(v.tensor_tensor(red[:, :], top[0][:, :], top[1][:, :], ALU.add))
                do(v.reciprocal(red[:, :], red[:, :]))
                for k in range(2):
                    do(v.tensor_tensor(top[k][:, :], top[k][:, :], red[:, :], ALU.mult))

        positions(nc, "by_expert", c, P, 2 * NT, EX1, MT, bin_f[:, :], pos_f[:, :], addr_i[:, :], expert)

        with Stage(nc, "send") as s:
            slot = [s.sb(f"slot{u}", [P, 2], I32) for u in range(2)]
            tok = [s.sb(f"tok{u}", [P, 1], I32) for u in range(2)]
            staged = s.sem("staged")
            sent = [[s.sem(f"sent{u}{k}") for k in range(2)] for u in range(2)]
            dv = s.sem("dv")
            block = s.block()

            @block.vector
            def _(dve):
                nc.vector.tensor_copy(pos_i[:, :], pos_f[:, :]).then_inc(dv, 1)

            @block.gpsimd
            def _(pool):
                def tile(t, u, i, n):
                    for k in range(2):
                        wait_positive(pool, sent[u][k], i * 16)
                    view = addr_i[:, :].rearrange("p (k t) -> p t k", k=2)
                    nc.gpsimd.tensor_copy(slot[u][:, :].unsqueeze(1), view[:, bass.ds(t, 1), :]).then_inc(staged, 1)
                    nc.gpsimd.tensor_copy(tok[u][:, :], token[:, bass.ds(t, 1)]).then_inc(staged, 1)
                    pool.wait_ge(staged, t * 2 + 2)
                    keep_apart(pool)
                    for k in range(2):
                        nc.gpsimd.indirect_dma_start(
                            out=slots, out_offset=bass.IndirectOffsetOnAxis(ap=slot[u][0:n, k:k + 1], axis=0),
                            in_=tok[u][0:n, :], in_offset=None).then_inc(sent[u][k], 16)

                for u in range(2):
                    tile(u, u, 0, P)
                with pool.Fori(1, NT // 2 - 1) as i:
                    for u in range(2):
                        tile(i * 2 + u, u, i, P)
                tile(NT - 2, 0, NT // 2 - 1, P)
                tile(NT - 1, 1, NT // 2 - 1, TAIL)
                for u in range(2):
                    for k in range(2):
                        pool.wait_ge(sent[u][k], 16 * (NT // 2))

        with Stage(nc, "moe") as s:
            tokens = s.sb("tokens", [P, MT], I32)
            two = range(2)
            idx = [s.sb(f"idx{u}", [P, 1], I32) for u in two]
            got = [s.sb(f"got{u}", [P, D]) for u in two]
            xT = [s.sb(f"xT{u}", [P, 2, P]) for u in two]
            w1 = [s.sb(f"w1{u}", [P, 2, HID]) for u in two]
            w2 = [s.sb(f"w2{u}", [P, 2, HID]) for u in two]
            w3 = [s.sb(f"w3{u}", [P, HID // P, D]) for u in two]
            gatev, hid = s.sb("gatev", [P, HID]), [s.sb(f"hid{u}", [P, HID]) for u in two]
            y = [s.sb(f"y{u}", [P, D]) for u in two]
            pT = s.ps("pT", [P, 2, P])
            p1 = [s.ps(f"p1{u}", [P, HID]) for u in two]
            p2 = [s.ps(f"p2{u}", [P, HID]) for u in two]
            p3 = [s.ps(f"p3{u}", [P, D]) for u in two]
            w_s = [[s.sem(f"w{n}_loaded{u}") for n in range(3)] for u in two]
            loaded, idx_ready = s.sem("loaded"), s.sem("idx_ready")
            got_s = [s.sem(f"got_s{u}") for u in two]
            turned, xT_ready, up, gate_ready, hid_ready, down = (
                s.sem(n) for n in ("turned", "xT_ready", "up", "gate_ready", "hid_ready", "down"))
            y_ready = [s.sem(f"y_ready{u}") for u in two]
            stored = [s.sem(f"stored{u}") for u in two]
            block = s.block()
            NH = HID // P
            T2 = MT // 2

            @block.sync
            def _(sp):
                sp.dma_start(tokens[:, :], slots.rearrange("(p t) o -> p (t o)", p=P)).then_inc(loaded, 16)
                v1 = a["L1_ffn_w1"].rearrange("e (k p) n -> e p k n", p=P)
                v2 = a["L1_ffn_w2"].rearrange("e (k p) n -> e p k n", p=P)
                v3 = a["L1_ffn_w3"].rearrange("e (k p) n -> e p k n", p=P)

                def load(dest, view, e, sem):
                    sp.dma_start(dest[:, :, :], view[bass.ds(e, 1)].rearrange("o p k n -> (o p) k n")).then_inc(sem, 16)

                def tile(i, u, first):
                    t = i * 2 + u
                    e = sp.value_load(expert[0:1, bass.ds(t, 1)], min_val=0, max_val=EX1 - 1)
                    if first:
                        for n, (w, view) in enumerate(((w1, v1), (w2, v2), (w3, v3))):
                            load(w[u], view, e, w_s[u][n])
                        return
                    last = sp.value_load(expert[0:1, bass.ds(t - 2, 1)], min_val=0, max_val=EX1 - 1)
                    sp.wait_ge(up, t - 1)
                    keep_apart(sp)
                    with sp.If(e != last):
                        load(w1[u], v1, e, w_s[u][0])
                        load(w2[u], v2, e, w_s[u][1])
                    with sp.If(e == last):
                        sp.sem_inc(w_s[u][0], 16)
                        sp.sem_inc(w_s[u][1], 16)
                    sp.wait_ge(down, t - 1)
                    keep_apart(sp)
                    with sp.If(e != last):
                        load(w3[u], v3, e, w_s[u][2])
                    with sp.If(e == last):
                        sp.sem_inc(w_s[u][2], 16)

                for u in two:
                    tile(0, u, True)
                with sp.Fori(1, T2) as i:
                    for u in two:
                        tile(i, u, False)

            @block.gpsimd
            def _(pool):
                pool.wait_ge(loaded, 16)

                def gather(i, u, first):
                    t = i * 2 + u
                    if not first:
                        pool.wait_ge(turned, t - 1)
                    nc.gpsimd.tensor_copy(idx[u][:, :], tokens[:, bass.ds(t, 1)]).then_inc(idx_ready, 1)
                    pool.wait_ge(idx_ready, t + 1)
                    keep_apart(pool)
                    nc.gpsimd.indirect_dma_start(
                        out=got[u][:, :], out_offset=None, in_=xtab,
                        in_offset=bass.IndirectOffsetOnAxis(ap=idx[u][:, 0:1], axis=0)).then_inc(got_s[u], 16)

                for u in two:
                    gather(0, u, True)
                with pool.Fori(1, T2) as i:
                    for u in two:
                        gather(i, u, False)

            def in_steps(eng, step):
                step(0, 0, {0})
                step(0, 1, {0, 1})
                step(1, 0, {0, 1, 2})
                step(1, 1, {0, 1, 2})
                with eng.Fori(2, T2) as i:
                    step(i, 0, {0, 1, 2})
                    step(i, 1, {0, 1, 2})
                step(T2, 0, {1, 2})
                step(T2, 1, {2})

            @block.tensor
            def _(pe):
                def step(i, u, parts):
                    t, w = i * 2 + u, 1 - u
                    if 0 in parts:
                        pe.wait_ge(got_s[u], (i + 1) * 16)
                        if 1 in parts:
                            pe.wait_ge(xT_ready, t)
                        for h in two:
                            ins = nc.tensor.transpose(pT[:, h, :], got[u][:, h * P:(h + 1) * P], c["ident"][:, :])
                        ins.then_inc(turned, 1)
                    if 1 in parts:
                        pe.wait_ge(xT_ready, t)
                        done = (i + 1) * 16 if u == 1 else i * 16
                        for n, (wt, ps) in enumerate(((w1, p1), (w2, p2))):
                            pe.wait_ge(w_s[w][n], done)
                            if 2 in parts and not (isinstance(t, int) and t < 3):
                                pe.wait_ge(hid_ready, t - 2)
                            for j in range(NH):
                                for k in two:
                                    ins = nc.tensor.matmul(ps[w][:, j * P:(j + 1) * P], wt[w][:, k, j * P:(j + 1) * P], xT[w][:, k, :],
                                                           start=(k == 0), stop=(k == 1))
                        ins.then_inc(up, 1)
                    if 2 in parts:
                        pe.wait_ge(hid_ready, t - 1)
                        pe.wait_ge(w_s[u][2], i * 16)
                        wait_positive(pe, y_ready[u], i - 1)
                        for j in range(NH):
                            ins = nc.tensor.matmul(p3[u][:, :], hid[u][:, j * P:(j + 1) * P], w3[u][:, j, :], start=(j == 0), stop=(j == NH - 1))
                        ins.then_inc(down, 1)

                in_steps(pe, step)

            @block.scalar
            def _(act):
                yv = results.rearrange("(t p) d -> t p d", p=P)

                def step(i, u, parts):
                    t, w = i * 2 + u, 1 - u
                    if 0 in parts:
                        act.wait_ge(turned, t + 1)
                        if 2 in parts:
                            act.wait_ge(up, t - 1)
                        nc.scalar.activation(xT[u][:, :, :], pT[:, :, :], ACT.Copy).then_inc(xT_ready, 1)
                    if 1 in parts:
                        act.wait_ge(up, t)
                        if 2 in parts:
                            act.wait_ge(hid_ready, t - 1)
                        nc.scalar.activation(gatev[:, :], p1[w][:, :], ACT.Silu).then_inc(gate_ready, 1)
                    if 2 in parts:
                        act.wait_ge(down, t - 1)
                        wait_positive(act, stored[u], (i - 1) * 16)
                        nc.scalar.activation(y[u][:, :], p3[u][:, :], ACT.Copy).then_inc(y_ready[u], 1)
                        act.wait_ge(y_ready[u], i)
                        act.dma_start(yv[bass.ds(t - 2, 1)].rearrange("o p d -> (o p) d"), y[u][:, :]).then_inc(stored[u], 16)

                in_steps(act, step)
                for u in two:
                    act.wait_ge(stored[u], 16 * T2)

            @block.vector
            def _(dve):
                def step(i, u, parts):
                    t, w = i * 2 + u, 1 - u
                    if 1 in parts:
                        dve.wait_ge(gate_ready, t)
                        if 2 in parts and not (isinstance(t, int) and t < 3):
                            dve.wait_ge(down, t - 2)
                        nc.vector.tensor_tensor(hid[w][:, :], gatev[:, :], p2[w][:, :], ALU.mult).then_inc(hid_ready, 1)

                in_steps(dve, step)

        with Stage(nc, "comb") as s:
            two = range(2)
            idx = [s.sb(f"idx{u}", [P, 2], I32) for u in two]
            got = [[s.sb(f"got{u}{k}", [P, D]) for k in two] for u in two]
            got_s = [[s.sem(f"got_s{u}{k}") for k in two] for u in two]
            idx_ready, added = s.sem("idx_ready"), s.sem("added")
            block = s.block()

            @block.gpsimd
            def _(pool):
                def tile(t, u, i, n, first=False):
                    if not first:
                        pool.wait_ge(added, (t - 1) * 2)
                    view = pos_i[:, :].rearrange("p (k t) -> p t k", k=2)
                    nc.gpsimd.tensor_copy(idx[u][:, :].unsqueeze(1), view[:, bass.ds(t, 1), :]).then_inc(idx_ready, 1)
                    pool.wait_ge(idx_ready, t + 1)
                    keep_apart(pool)
                    for k in two:
                        nc.gpsimd.indirect_dma_start(
                            out=got[u][k][0:n, :], out_offset=None, in_=results,
                            in_offset=bass.IndirectOffsetOnAxis(ap=idx[u][0:n, k:k + 1], axis=0)).then_inc(got_s[u][k], 16)

                for u in two:
                    tile(u, u, 0, P, first=True)
                with pool.Fori(1, NT // 2 - 1) as i:
                    for u in two:
                        tile(i * 2 + u, u, i, P)
                tile(NT - 2, 0, NT // 2 - 1, P)
                tile(NT - 1, 1, NT // 2 - 1, TAIL)

            @block.vector
            def _(dve):
                def tile(t, u, i, n):
                    for k in two:
                        dve.wait_ge(got_s[u][k], (i + 1) * 16)
                        wait_positive(dve, added, t * 2 + k)
                        x = flat(x_res[0:n, bass.ds(t, 1), :])
                        nc.vector.scalar_tensor_tensor(out=x, in0=got[u][k][0:n, :], scalar=top[k][0:n, bass.ds(t, 1)], in1=x,
                                                       op0=ALU.mult, op1=ALU.add).then_inc(added, 1)

                for u in two:
                    tile(u, u, 0, P)
                with dve.Fori(1, NT // 2 - 1) as i:
                    for u in two:
                        tile(i * 2 + u, u, i, P)
                tile(NT - 2, 0, NT // 2 - 1, P)
                tile(NT - 1, 1, NT // 2 - 1, TAIL)


def store(nc, x_res, out):
    with Stage(nc, "store") as s:
        stored = s.sem("stored")
        block = s.block()

        @block.sync
        def _(sp):
            sp.dma_start(out[0:(NT - 1) * P, :].rearrange("(t p) d -> p t d", p=P), x_res[:, 0:NT - 1, :]).then_inc(stored, 16)
            sp.dma_start(out[(NT - 1) * P:NODES, :], x_res[0:TAIL, NT - 1, :]).then_inc(stored, 16)
            sp.wait_ge(stored, 32)


def graph_layers(nc, a, out):
    feat = nc.dram_tensor("feat", (RELS * PADN, FW), F32).ap()
    table0 = nc.dram_tensor("table0", (P * ET, W0), F32).ap()
    table1 = nc.dram_tensor("table1", (P * ET, W1), F32).ap()
    xtab = nc.dram_tensor("xtab", (PADN, D), F32).ap()
    xtab2 = nc.dram_tensor("xtab2", (PADN, D), F32).ap()
    slots = nc.dram_tensor("slots", (P * MT, 1), I32).ap()
    results = nc.dram_tensor("results", (P * MT, D), F32).ap()
    with Stage(nc, "all") as S:
        x_res = S.sb("x_res", [P, NT, D])
        c = make_consts(S)
        constants(nc, c, x_res)
        bins0, bins1 = S.sb("bins0", [1, 512], I32), S.sb("bins1", [1, 512], I32)
        with Stage(nc, "recs1") as R:
            rec1, addr1 = R.sb("rec1", [P, EJ, W1]), R.sb("addr1", [P, EJ], I32)

            def side1(k):
                return lambda s: Sender(nc, s, table1, rec1, addr1, W1, sum(COLS1[:k]), COLS1[k])

            with Stage(nc, "l0") as L:
                er = L.sb("er", [P, NT, RELS * HEADS])
                with Stage(nc, "l0a") as M:
                    rec0, addr0 = M.sb("rec0", [P, EJ, W0]), M.sb("addr0", [P, EJ], I32)
                    with Stage(nc, "l0b") as N:
                        pos_f = N.sb("pos_f", [P, EJ])
                        edge_records(nc, c, a, x_res, rec0, rec1, pos_f, addr0, addr1, bins0, bins1, table0, table1)
                    with Stage(nc, "l0c") as N:
                        xnT = N.sb("xnT", [P, 2, PADN])
                        layer_norm(nc, "ln0", c, x_res, xnT, side=lambda s: Sender(nc, s, table0, rec0, addr0, W0, COLS0[0], COLS0[1]))
                        project(nc, a, xnT, er, feat, rec0, addr0, table0)
                acc = L.sb("acc", [P, NT, HEADS, HD + 1])
                attend(nc, c, er, acc, rec1, addr1, table0, table1, feat, bins0)
                join_attention(nc, a, acc, x_res, side1(1))
            with Stage(nc, "l1") as L:
                xnT = L.sb("xnT", [P, 2, PADN])
                layer_norm(nc, "ln1", c, x_res, xnT, side=side1(2))
                mixture(nc, c, a, xnT, x_res, lambda k: side1(k + 1))
            with Stage(nc, "l2a") as L:
                xnT = L.sb("xnT", [P, 2, PADN])
                layer_norm(nc, "ln2", c, x_res, xnT, xtab, add=True, side=side1(5))
        with Stage(nc, "l2b") as L:
            agg = L.sb("agg", [P, NT, D])
            convolve(nc, c, a, agg, table1, xtab, bins1)
            aggT = L.sb("aggT", [P, 2, PADN])
            turn_rows(nc, "turn", c, agg, aggT)
            update(nc, c, a, aggT, x_res)
        with Stage(nc, "l3") as L:
            xnT = L.sb("xnT", [P, 2, PADN])
            layer_norm(nc, "ln3", c, x_res, xnT, xtab2)
            routed(nc, c, a, xnT, x_res, xtab2, slots, results)
        store(nc, x_res, out)


def kernel(**inputs):
    import numpy as np
    import concourse.bacc as bacc
    from concourse.bass_utils import run_bass_kernel_spmd

    nc = bacc.Bacc("TRN2", target_bir_lowering=False, num_devices=1)
    arrays, a = {}, {}
    for name in inputs:
        array = np.ascontiguousarray(inputs[name])
        arrays[f"in_{name}"] = array
        a[name] = nc.dram_tensor(f"in_{name}", array.shape, mybir.dt.from_np(array.dtype), kind="ExternalInput").ap()
    out = nc.dram_tensor("out", (NODES, D), F32, kind="ExternalOutput").ap()
    graph_layers(nc, a, out)
    result = run_bass_kernel_spmd(nc, [arrays], core_ids=[0])
    return result.results[0]["out"]
```
